# Optimizing a Trainium2 kernel written in Bass

```python
import numpy as np
import jax
import jax.numpy as jnp

def _softmax(x, axis=-1):
    return jax.nn.softmax(x, axis=axis)

def _gelu(x):
    return jax.nn.gelu(x, approximate=True)

def _silu(x):
    return jax.nn.silu(x)

def _sigmoid(x):
    return jax.nn.sigmoid(x)

def _layernorm(x, axis=-1, eps=1e-05):
    m = jnp.mean(x, axis=axis, keepdims=True)
    v = jnp.var(x, axis=axis, keepdims=True)
    return (x - m) / jnp.sqrt(v + eps)

def _scatter_add(tgt, idx, src, axis=0):
    return tgt.at[idx].add(src)

def _segment_sum(src, seg, n):
    return jax.ops.segment_sum(src, seg, n)
kernel_name = 'mk_macaron_d1_jaxref_r8_598728'

def setup_inputs(seed: int=0):
    np.random.seed(seed)
    _w = jnp.asarray

    def _L0_attn_setup():
        import jax, jax.numpy as jnp
        import numpy as np
        HIDDEN = 512
        N_HEADS = 32
        N_KV_HEADS = 8
        HEAD_DIM = HIDDEN // N_HEADS
        N_REP = N_HEADS // N_KV_HEADS
        KV_DIM = N_KV_HEADS * HEAD_DIM

        def _kaiming_uniform(key, out_f, in_f):
            bound = 1.0 / np.sqrt(in_f)
            return jax.random.uniform(key, (out_f, in_f), jnp.float32, -bound, bound)

        def bitnet_linear(x, weight, scale_param):
            s = jnp.maximum(jnp.mean(jnp.abs(weight), axis=1), 1e-08)
            binary_w = jnp.sign(weight / s[:, None])
            y = jnp.einsum('bsi,oi->bso', x, binary_w)
            y = y * (s * scale_param)[None, None, :]
            return jnp.nan_to_num(y, nan=0.0, posinf=1000000.0, neginf=-1000000.0)
        key = jax.random.key(seed)
        ks = jax.random.split(key, 5)
        return {'hidden_states': jax.random.normal(ks[0], (1, 256, HIDDEN), jnp.float32), 'q_weight': _kaiming_uniform(ks[1], HIDDEN, HIDDEN), 'q_scale': jnp.ones((HIDDEN,), jnp.float32), 'k_weight': _kaiming_uniform(ks[2], KV_DIM, HIDDEN), 'k_scale': jnp.ones((KV_DIM,), jnp.float32), 'v_weight': _kaiming_uniform(ks[3], KV_DIM, HIDDEN), 'v_scale': jnp.ones((KV_DIM,), jnp.float32), 'o_weight': _kaiming_uniform(ks[4], HIDDEN, HIDDEN), 'o_scale': jnp.ones((HIDDEN,), jnp.float32)}
    _L0_attn_in = _L0_attn_setup()

    def _L0_ffn_setup():
        import jax, jax.numpy as jnp
        import numpy as np
        B, S, D, O, E, R = (2, 512, 512, 512, 8, 16)
        TOP_K = 2
        SCALING = 32.0 / 16.0
        key = jax.random.key(seed)
        k = jax.random.split(key, 6)
        x = jax.random.normal(k[0], (B, S, D), dtype=jnp.float32)
        W_base = jax.random.normal(k[1], (O, D), dtype=jnp.float32) * 0.02
        b_base = jax.random.normal(k[2], (O,), dtype=jnp.float32) * 0.02
        W_router = jax.random.normal(k[3], (E, D), dtype=jnp.float32) * 0.01
        lora_A = jax.random.normal(k[4], (E, R, D), dtype=jnp.float32) * (1.0 / np.sqrt(D))
        lora_B = jax.random.normal(k[5], (E, O, R), dtype=jnp.float32) * 0.02
        return {'x': x, 'W_base': W_base, 'b_base': b_base, 'W_router': W_router, 'lora_A': lora_A, 'lora_B': lora_B}
    _L0_ffn_in = _L0_ffn_setup()
    _d = {'L0_attn_hidden_states': _L0_attn_in['hidden_states'], 'L0_attn_q_weight': _L0_attn_in['q_weight'], 'L0_attn_q_scale': _L0_attn_in['q_scale'], 'L0_attn_k_weight': _L0_attn_in['k_weight'], 'L0_attn_k_scale': _L0_attn_in['k_scale'], 'L0_attn_v_weight': _L0_attn_in['v_weight'], 'L0_attn_v_scale': _L0_attn_in['v_scale'], 'L0_attn_o_weight': _L0_attn_in['o_weight'], 'L0_attn_o_scale': _L0_attn_in['o_scale'], 'L0_ffn_W_base': _L0_ffn_in['W_base'], 'L0_ffn_b_base': _L0_ffn_in['b_base'], 'L0_ffn_W_router': _L0_ffn_in['W_router'], 'L0_ffn_lora_A': _L0_ffn_in['lora_A'], 'L0_ffn_lora_B': _L0_ffn_in['lora_B']}
    _x0 = _d['L0_attn_hidden_states']
    _d['L0_attn_hidden_states'] = jax.random.normal(jax.random.fold_in(jax.random.key(seed), 1), (2, 1024, 512), dtype=_x0.dtype)
    del _x0
    return _d

def reference(L0_attn_hidden_states, L0_attn_q_weight, L0_attn_q_scale, L0_attn_k_weight, L0_attn_k_scale, L0_attn_v_weight, L0_attn_v_scale, L0_attn_o_weight, L0_attn_o_scale, L0_ffn_W_base, L0_ffn_b_base, L0_ffn_W_router, L0_ffn_lora_A, L0_ffn_lora_B):

    def _L0_attn_ref(hidden_states, q_weight, q_scale, k_weight, k_scale, v_weight, v_scale, o_weight, o_scale):
        import jax, jax.numpy as jnp
        import numpy as np
        HIDDEN = 512
        N_HEADS = 32
        N_KV_HEADS = 8
        HEAD_DIM = HIDDEN // N_HEADS
        N_REP = N_HEADS // N_KV_HEADS
        KV_DIM = N_KV_HEADS * HEAD_DIM

        def _kaiming_uniform(key, out_f, in_f):
            bound = 1.0 / np.sqrt(in_f)
            return jax.random.uniform(key, (out_f, in_f), jnp.float32, -bound, bound)

        def bitnet_linear(x, weight, scale_param):
            s = jnp.maximum(jnp.mean(jnp.abs(weight), axis=1), 1e-08)
            binary_w = jnp.sign(weight / s[:, None])
            y = jnp.einsum('bsi,oi->bso', x, binary_w)
            y = y * (s * scale_param)[None, None, :]
            return jnp.nan_to_num(y, nan=0.0, posinf=1000000.0, neginf=-1000000.0)
        b, s, _ = hidden_states.shape
        q = bitnet_linear(hidden_states, q_weight, q_scale)
        k = bitnet_linear(hidden_states, k_weight, k_scale)
        v = bitnet_linear(hidden_states, v_weight, v_scale)
        q = q.reshape(b, s, N_HEADS, HEAD_DIM).transpose(0, 2, 1, 3)
        k = k.reshape(b, s, N_KV_HEADS, HEAD_DIM).transpose(0, 2, 1, 3)
        v = v.reshape(b, s, N_KV_HEADS, HEAD_DIM).transpose(0, 2, 1, 3)
        k = jnp.repeat(k, N_REP, axis=1)
        v = jnp.repeat(v, N_REP, axis=1)
        scores = jnp.einsum('bhqd,bhkd->bhqk', q, k) / np.sqrt(HEAD_DIM)
        attn = jax.nn.softmax(scores, axis=-1)
        out = jnp.einsum('bhqk,bhkd->bhqd', attn, v)
        out = out.transpose(0, 2, 1, 3).reshape(b, s, HIDDEN)
        return bitnet_linear(out, o_weight, o_scale)

    def _L0_ffn_ref(x, W_base, b_base, W_router, lora_A, lora_B):
        import jax, jax.numpy as jnp
        import numpy as np
        B, S, D, O, E, R = (2, 512, 512, 512, 8, 16)
        TOP_K = 2
        SCALING = 32.0 / 16.0
        d = x.shape[-1]
        n_experts = W_router.shape[0]
        xf = x.reshape(-1, d)
        logits = xf @ W_router.T
        probs = jax.nn.softmax(logits, axis=-1)
        topk_p, topk_i = jax.lax.top_k(probs, TOP_K)
        topk_p = topk_p / jnp.sum(topk_p, axis=-1, keepdims=True)
        w = jnp.sum(jax.nn.one_hot(topk_i, n_experts, dtype=xf.dtype) * topk_p[..., None], axis=1)
        h = jnp.einsum('td,erd->ter', xf, lora_A)
        lora_out = jnp.einsum('ter,eor,te->to', h, lora_B, w) * SCALING
        base = x @ W_base.T + b_base
        return base + lora_out.reshape(x.shape[:-1] + (W_base.shape[0],))
    x = L0_attn_hidden_states
    x = x + 0.5 * _L0_ffn_ref(_layernorm(x, axis=-1), L0_ffn_W_base, L0_ffn_b_base, L0_ffn_W_router, L0_ffn_lora_A, L0_ffn_lora_B)
    x = x + _L0_attn_ref(_layernorm(x, axis=-1), L0_attn_q_weight, L0_attn_q_scale, L0_attn_k_weight, L0_attn_k_scale, L0_attn_v_weight, L0_attn_v_scale, L0_attn_o_weight, L0_attn_o_scale)
    x = x + 0.5 * _L0_ffn_ref(_layernorm(x, axis=-1), L0_ffn_W_base, L0_ffn_b_base, L0_ffn_W_router, L0_ffn_lora_A, L0_ffn_lora_B)
    return x

_drawn_inputs = setup_inputs


def setup_inputs(seed=0):
    import zlib

    import numpy as np

    out = dict(_drawn_inputs(seed))
    spreads = {'L0_attn_q_scale': (1.0, 0.6),
     'L0_attn_k_scale': (1.0, 0.6),
     'L0_attn_v_scale': (1.0, 0.6),
     'L0_attn_o_scale': (1.0, 0.6)}
    factors = {'L0_attn_q_weight': 8.0,
     'L0_attn_k_weight': 8.0,
     'L0_attn_v_weight': 5.463,
     'L0_attn_o_weight': 5.745,
     'L0_ffn_b_base': 3.065}
    for name, (base, spread) in spreads.items():
        noise = np.random.default_rng([zlib.crc32(name.encode()), seed]).standard_normal(out[name].shape)
        drawn = base * np.exp(spread * noise) if base else spread * noise
        out[name] = jnp.asarray(drawn.astype(out[name].dtype))
    for name, factor in factors.items():
        out[name] = (out[name] * factor).astype(out[name].dtype)
    return out
```

```python
from contextlib import ExitStack

import concourse.bass as bass
from concourse import mybir

F32 = mybir.dt.float32
F32R = mybir.dt.float32r
BF16 = mybir.dt.bfloat16
I32 = mybir.dt.int32
U32 = mybir.dt.uint32
ALU = mybir.AluOpType
ACT = mybir.ActivationFunctionType
AX = mybir.AxisListType.X

P = 128
B, S, D = 2, 1024, 512
T = B * S
H, KV, HD = 32, 8, 16
REP = H // KV
E, R = 8, 16
DC = D // P
CH = 256
CT = CH // P
NCH = T // CH
BLK = 512
QT = BLK // P
KT = S // P
NU = (T // BLK) * KV
UB = 4
PARTS = 3
PAIRS = 6
SR = PAIRS * HD
Q_PARTS = (0, 0, 0, 1, 1, 2)
K_PARTS = (0, 1, 2, 0, 1, 0)
EPS = 1e-5
BIG = 1e6
INF_BITS = 0x7F800000
KQ = CH + DC * CH
ZW = 3 * 512

FRONT = ["LN1", "T1a", "T1b", "RT", "HT", "WR", "FFa", "FFb", "LN2", "T2a", "T2b", "VK", "Q0", "Q1", "VT", "SPL"]
BACK = ["T0a", "T0b", "Oa", "Ob", "ADD", "LN3", "T1a", "T1b", "RT", "HT", "WR", "FFa", "FFb"]
F_USES = [s for s in FRONT if s not in ("LN1", "LN2", "SPL")]
B_USES = [s for s in BACK if s not in ("ADD", "LN3")]
NF, NB = len(F_USES), len(B_USES)
FRONT_PAIRS = NCH // 2
LOOP_BACKS = NCH - 2
WAIT_PADS = 256
R_STEPS = 15


class Chunk:

    def __init__(self, kind, slot, n, tail=False):
        self.kind, self.slot, self.n, self.tail = kind, slot, n, tail
        self.front = kind == "front"
        self.order = FRONT if self.front else BACK
        self.uses = F_USES if self.front else B_USES
        self.ffn = n if self.front else FRONT_PAIRS + n
        self.t0 = n * 4 if self.front else 4 * FRONT_PAIRS + n * 4
        self.guard0 = n * 9 if self.front else 9 * FRONT_PAIRS + n * 6
        self.clamp0 = n * 6 if self.front else 6 * FRONT_PAIRS + n * 4
        self.load = (n + 1) * 16 if self.front else 16 * FRONT_PAIRS + (n + 1) * 48
        self.mb0 = n * NF if self.front else NF * FRONT_PAIRS + n * NB

    def ln(self, which):
        return self.n * 2 + which if self.front else 2 * FRONT_PAIRS + self.n

    def written(self, stage):
        return self.mb0 + (self.uses.index(stage) + 1)

    def bank(self, stage):
        s = self.uses.index(stage)
        if self.front:
            return self.slot, self.n * NF + s
        if not self.tail:
            return s % 2, self.n * (6 - s % 2) + (NF * FRONT_PAIRS + s // 2)
        return self.slot, NF * FRONT_PAIRS + (6 - self.slot) * LOOP_BACKS + s

    def tn(self, stage):
        return ["T1a", "T1b", "T2a", "T2b"].index(stage) if self.front else ["T0a", "T0b", "T1a", "T1b"].index(stage)


def positive(value):
    return not isinstance(value, int) or value > 0


def macaron(nc, x, wbT, b, wrT, aT, bT, qN, kN, vN, qT, kT, vT, oT, qs, ks, vs, osc, out):
    ctx = ExitStack()
    with ctx:
        def sb(name, shape, dt):
            return ctx.enter_context(nc.sbuf_tensor(name, shape, dt))

        def sem(name):
            return ctx.enter_context(nc.semaphore(name))

        x1_dram = nc.dram_tensor("x1_dram", [T, D], F32, kind="Internal").ap()
        q_dram = nc.dram_tensor("q_dram", [PARTS, D, T], BF16, kind="Internal").ap()
        k_dram = nc.dram_tensor("k_dram", [PARTS, P, T], BF16, kind="Internal").ap()
        att_dram = nc.dram_tensor("att_dram", [T // P, KV, P, REP * HD], F32, kind="Internal").ap()

        ident = sb("ident", [P, P], F32)
        identb = sb("identb", [P, P], BF16)
        ones = sb("ones", [P, P], F32)
        expert_of = sb("expert_of", [P, P], F32)
        expert_i = sb("expert_i", [P, P], I32)
        mhalf = sb("mhalf", [P, CT], F32)
        wb_h, wb_l = sb("wb_h", [P, DC, D], F32R), sb("wb_l", [P, DC, D], F32R)
        wr_hl = sb("wr_hl", [P, DC, 2 * E], F32R)
        a_h, a_l = sb("a_h", [P, DC, P], F32R), sb("a_l", [P, DC, P], F32R)
        b_h, b_l = sb("b_h", [P, D], F32R), sb("b_l", [P, D], F32R)
        sq, sk = sb("sq", [P, DC, D], F32R), sb("sk", [P, DC, P], F32R)
        sv, so = sb("sv", [P, DC, P], F32R), sb("so", [P, DC, D], F32R)
        bias_half = sb("bias_half", [P, D], F32)
        o_scale = sb("o_scale", [P, D], F32)
        osc_row = sb("osc_row", [P, D], F32)
        raw_scale = sb("raw_scale", [P, 2 + DC], F32)
        col_scale = sb("col_scale", [P, 2 + DC], F32)
        wr_raw = sb("wr_raw", [P, DC, E], F32)

        probs = sb("probs", [P, 2, REP, BLK], F32)
        qst = sb("qst", [P, UB, REP, BLK], BF16)
        kst = sb("kst", [P, UB, S], BF16)
        v_all = sb("v_all", [P, T // P, KV * HD], F32)
        v_ring = sb("v_ring", [P, 2, KT, 2 * HD], F32)
        neg_max_parts = sb("neg_max_parts", [P, 2, REP * QT, 2], F32)
        neg_max = sb("neg_max", [P, 2, REP * QT], F32)
        neg_max_rest = sb("neg_max_rest", [P, 2, REP * QT], F32)
        shift = sb("shift", [P, 2, P], BF16)
        wait_pad = sb("wait_pad", [1, WAIT_PADS], BF16)
        shift_rows = sb("shift_rows", [P, 2, P], BF16)
        o_sb = sb("o_sb", [P, 2, BLK], F32)
        recip = sb("recip", [P, 2, QT, REP], F32)
        att = sb("att", [P, 2, QT, REP * HD], F32)

        xc = [sb(f"xc{s}", [P, CT, D], F32) for s in range(2)]
        xn = [sb(f"xn{s}", [P, CT, D], F32) for s in range(2)]
        xt_h = [sb(f"xt_h{s}", [P, DC, CH], F32R) for s in range(2)]
        xt_l = [sb(f"xt_l{s}", [P, DC, CH], F32R) for s in range(2)]
        hT = [sb(f"hT{s}", [P, CH], F32) for s in range(2)]
        hT_h = [sb(f"hT_h{s}", [P, CH], F32R) for s in range(2)]
        hT_l = [sb(f"hT_l{s}", [P, CH], F32R) for s in range(2)]
        w_rep = [sb(f"w_rep{s}", [P, CT, P], F32) for s in range(2)]
        w_tmp = [sb(f"w_tmp{s}", [P, 2 * CT, P], F32) for s in range(2)]
        zm = [sb(f"zm{s}", [P, 2 * ZW], F32) for s in range(2)]
        zd = [sb(f"zd{s}", [P, ZW], F32) for s in range(2)]
        stats = [sb(f"stats{s}", [P, CT, 6], F32) for s in range(2)]
        meanvar = [sb(f"meanvar{s}", [P, CT, 2], F32) for s in range(2)]
        var_eps = [sb(f"var_eps{s}", [P, CT], F32) for s in range(2)]
        rstd = [sb(f"rstd{s}", [P, CT], F32) for s in range(2)]
        logit2 = [sb(f"logit2{s}", [P, CT, 2 * E], F32) for s in range(2)]
        logit = [sb(f"logit{s}", [P, CT, E], F32) for s in range(2)]
        top = [sb(f"top{s}", [P, CT, 8], F32) for s in range(2)]
        top_i = [sb(f"top_i{s}", [P, CT, 8], U32) for s in range(2)]
        top_e = [sb(f"top_e{s}", [P, CT, 2], F32) for s in range(2)]
        gap = [sb(f"gap{s}", [P, CT], F32) for s in range(2)]
        e2 = [sb(f"e2{s}", [P, CT], F32) for s in range(2)]
        den = [sb(f"den{s}", [P, CT], F32) for s in range(2)]
        rden = [sb(f"rden{s}", [P, CT], F32) for s in range(2)]
        w12 = [sb(f"w12{s}", [P, CT, 2], F32) for s in range(2)]

        z = [t[:, 0:ZW] for t in zm]
        zneg = [t[:, ZW:2 * ZW] for t in zm]
        parts = [t[:, 0:PARTS * KQ // 2].bitcast(BF16).rearrange("p (c n) -> p c n", c=PARTS) for t in zm]

        raw_wb, raw_q = probs[:, 0, :, :], probs[:, 1, :, :]
        raw_qn = zm[0][:, 0:DC * D].rearrange("p (c n) -> p c n", c=DC)
        raw_o = zm[1][:, 0:DC * D].rearrange("p (c n) -> p c n", c=DC)
        stage = [qst[:, r, :, :].rearrange("p a b -> p (a b)").bitcast(F32) for r in range(UB)]
        raw_k, raw_v = [stage[0][:, i * D:(i + 1) * D].rearrange("p (c n) -> p c n", c=DC) for i in range(2)]
        raw_a, raw_b = stage[1][:, 0:D].rearrange("p (c n) -> p c n", c=DC), stage[1][:, D:2 * D]
        raw_vn, raw_kn = stage[2][:, 0:D], stage[2][:, D:2 * D]

        def bank(name):
            return ctx.enter_context(nc.psum_tensor(name, [P, 512], F32))

        ps_max = [bank(f"ps_max{i}") for i in range(2)]
        ps_score = [bank(f"ps_score{i}") for i in range(2)]
        ps_out = [bank(f"ps_out{i}") for i in range(2)]
        ps_fill = [bank(f"ps_fill{i}") for i in range(2)]

        raw_in = sem("raw_in")
        const_ready = sem("const_ready")
        signs_ready = sem("signs_ready")
        abs_ready = sem("abs_ready")
        osum_ready = sem("osum_ready")
        dve_prep = sem("dve_prep")
        qk_loaded = [sem(f"qk_loaded{r}") for r in range(UB)]
        rows_loaded = [sem(f"rows_loaded{r}") for r in range(UB)]
        max_scores = sem("max_scores")
        max_read = sem("max_read")
        neg_max_ready = sem("neg_max_ready")
        shift_parts = sem("shift_parts")
        scores_ready = sem("scores_ready")
        probs_ready = sem("probs_ready")
        probs_used = sem("probs_used")
        v_ready = sem("v_ready")
        o_copied = sem("o_copied")
        o_turned = sem("o_turned")
        recip_ready = sem("recip_ready")
        att_ready = sem("att_ready")
        att_stored = [sem(f"att_stored{i}") for i in range(2)]
        filler_ready = [sem(f"filler_ready{s}") for s in range(2)]
        filler_read = [sem(f"filler_read{i}") for i in range(2)]
        chunk_loaded = [sem(f"chunk_loaded{s}") for s in range(2)]
        stats_ready = [sem(f"stats_ready{s}") for s in range(2)]
        rstd_ready = [sem(f"rstd_ready{s}") for s in range(2)]
        xn_ready = [sem(f"xn_ready{s}") for s in range(2)]
        bias_added = [sem(f"bias_added{s}") for s in range(2)]
        xt_h_ready = [sem(f"xt_h_ready{s}") for s in range(2)]
        router_step = [sem(f"router_step{s}") for s in range(2)]
        e2_ready = [sem(f"e2_ready{s}") for s in range(2)]
        w_rep_ready = [sem(f"w_rep_ready{s}") for s in range(2)]
        hT_h_ready = [sem(f"hT_h_ready{s}") for s in range(2)]
        hT_l_ready = [sem(f"hT_l_ready{s}") for s in range(2)]
        clamped = [sem(f"clamped{s}") for s in range(2)]
        guard_step = [sem(f"guard_step{s}") for s in range(2)]
        part_cast = [sem(f"part_cast{s}") for s in range(2)]
        part_rest = [sem(f"part_rest{s}") for s in range(2)]
        parts_stored = [sem(f"parts_stored{s}") for s in range(2)]
        xc_stored = [sem(f"xc_stored{s}") for s in range(2)]
        residual = [sem(f"residual{s}") for s in range(2)]

        pad_columns = iter(range(1, WAIT_PADS))

        def pad():
            c = next(pad_columns)
            return wait_pad[0:1, c:c + 1]

        def dve_wait(dve, semaphore, value):
            if isinstance(value, int):
                dve.wait_ge(semaphore, value)
            else:
                dve.wait_ge(semaphore, value)
                dve.tensor_copy(pad(), wait_pad[0:1, 0:1])

        def gp_wait(gp, semaphore, value):
            if isinstance(value, int):
                gp.wait_ge(semaphore, value)
            else:
                gp.wait_ge(semaphore, value)
                gp.tensor_tensor(pad(), wait_pad[0:1, 0:1], wait_pad[0:1, 0:1], ALU.add)

        def max_use(i, uu, pos):
            return i * (33 * UB) + (65 + 33 * uu + pos)

        SHIFT_POS = 4

        def max_tiles(kt):
            return [(t + (t >= SHIFT_POS), t) for t in range(4 * kt, 4 * kt + 4)]

        def shift_use(i, uu, last):
            return max_use(i, uu, 0 if last and uu >= 2 else SHIFT_POS)

        def start_uses(slot):
            if slot < 11:
                return [(t, 0, t) for t in range(3 * slot, min(3 * slot + 3, 32))]
            if slot == 12:
                return [(max_use(0, -1, t), 1, t) for t in range(SHIFT_POS)]
            if slot == 14:
                return [(max_use(0, -1, SHIFT_POS), 0, None)]
            if 15 <= slot < 29:
                return [(max_use(0, -1, t + 1), 1, t) for t in range(2 * slot - 26, 2 * slot - 24)]
            return []

        def both(order, chunks):
            return [(c, pos) for pos in order for c in chunks]

        def front_body(chunks):
            return both(FRONT, chunks)

        def pair_plan(chunks):
            return dict(enumerate(front_body(chunks)))

        def back_plan(chunk):
            return {6 + 2 * n: (chunk, pos) for n, pos in enumerate(BACK)}

        block = ctx.enter_context(nc.Block())

        @block.sync
        def _(sp):
            for dst, src in (
                (raw_wb, wbT.rearrange("(c p) n -> p c n", p=P)), (raw_a, aT.rearrange("(c p) n -> p c n", p=P)),
                (raw_b, bT), (wr_raw[:, :, :], wrT.rearrange("(c p) n -> p c n", p=P)),
                (bias_half[:, :], b.partition_broadcast(P)), (osc_row[:, :], osc.partition_broadcast(P)),
                (raw_scale[:, 0:1], vs), (raw_scale[:, 1:2], ks), (raw_scale[:, 2:2 + DC], qs),
                (raw_k, kT.rearrange("(c p) n -> p c n", p=P)), (raw_v, vT.rearrange("(c p) n -> p c n", p=P)),
                (raw_kn, kN), (raw_vn, vN), (raw_q, qT.rearrange("(c p) n -> p c n", p=P)),
                (raw_qn, qN.rearrange("(c p) n -> p c n", p=P)), (raw_o, oT.rearrange("(c p) n -> p c n", p=P)),
            ):
                sp.dma_start(dst, src).then_inc(raw_in, 16)

            def chunk_rows(dram, c):
                return dram[bass.ds(c * CH, CH), :].rearrange("(t p) d -> p t d", p=P)

            def load_front(ch):
                s, n = ch.slot, ch.n
                if positive(n):
                    sp.wait_ge(xc_stored[s], n * 16)
                    sp.wait_ge(xn_ready[s], n * (2 * 2))
                sp.dma_start(xc[s][:, :, :], chunk_rows(x, n * 2 + s)).then_inc(chunk_loaded[s], 16)

            def fill(item):
                ch, pos = item
                s, n = ch.slot, ch.n
                if ch.front and pos == "FFb":
                    sp.wait_ge(filler_read[ch.bank("FFb")[0]], ch.bank("FFb")[1] + 1)
                    sp.dma_start(chunk_rows(x1_dram, n * 2 + s), xc[s][:, :, :]).then_inc(xc_stored[s], 16)
                if ch.front and pos == "SPL":
                    c = n * 2 + s
                    sp.wait_ge(part_rest[s], n * 2 + 2)
                    for part in range(PARTS):
                        sp.dma_start(k_dram[part, :, bass.ds(c * CH, CH)],
                                     parts[s][:, part, 0:CH]).then_inc(parts_stored[s], 16)
                        sp.dma_start(q_dram[part, :, bass.ds(c * CH, CH)].rearrange("(m p) t -> p m t", p=P),
                                     parts[s][:, part, CH:KQ].rearrange("p (m t) -> p m t", t=CH)
                                     ).then_inc(parts_stored[s], 16)
                if not ch.front and pos == "FFb":
                    a = n if not ch.tail else NCH - 2 + s
                    for st in ("FFa", "FFb"):
                        sp.wait_ge(filler_read[ch.bank(st)[0]], ch.bank(st)[1] + 1)
                    sp.dma_start(chunk_rows(out, a), xc[s][:, :, :]).then_inc(xc_stored[s], 16)

            def load_back(ch):
                s, n = ch.slot, ch.n
                a = n if not ch.tail else NCH - 2 + s
                sp.wait_ge(xc_stored[s], n * 16 + 16 * FRONT_PAIRS)
                for i in range(2):
                    sp.wait_ge(att_stored[i], (a // 2) * 64 + 64)
                sp.dma_start(xc[s][:, :, :], chunk_rows(x1_dram, a)).then_inc(chunk_loaded[s], 16)
                for t in range(CT):
                    sp.dma_start(xn[s][:, t, :].rearrange("p (k d) -> p k d", k=KV),
                                 att_dram[bass.ds(a * 2 + t, 1), :, :, :].rearrange("o k p d -> p (o k) d")
                                 ).then_inc(chunk_loaded[s], 16)

            def load_qk(i, uu):
                r = uu % UB
                if not isinstance(i, int) or UB * i + uu >= UB:
                    sp.wait_ge(scores_ready, i * (32 * UB) + 32 * (uu - 3))
                j = i + uu // UB
                t0, o0, k0 = (j // 2) * BLK, (j % 2) * (UB * REP * HD) + r * REP * HD, (j // 4) * S
                for slot in range(PAIRS):
                    rows = slice(slot * HD, (slot + 1) * HD)
                    sp.dma_start(qst[rows, r, :, :],
                                 q_dram[Q_PARTS[slot], bass.ds(o0, REP * HD), bass.ds(t0, BLK)]
                                 .rearrange("(j d) t -> d j t", j=REP)).then_inc(qk_loaded[r], 16)
                    sp.dma_start(kst[rows, r, :],
                                 k_dram[K_PARTS[slot], bass.ds((j % 2) * (UB * HD) + r * HD, HD), bass.ds(k0, S)]
                                 ).then_inc(qk_loaded[r], 16)

            def load_rows(i, uu, use):
                r = uu % UB
                sp.wait_ge(max_read, use + 1)
                for part in range(PARTS):
                    sp.dma_start(qst[SR + part:SR + part + 1, r, :, :].rearrange("c j (q p) -> c (j q) p", p=P),
                                 shift_rows[REP * QT * part:REP * QT * (part + 1), uu % 2, :]
                                 ).then_inc(rows_loaded[r], 16)

            def store_att(i, uu):
                j = i + uu // UB
                sp.wait_ge(att_ready, i * UB + (uu + 1))
                sp.dma_start(att_dram[bass.ds((j // 2) * QT, QT), bass.ds((j % 2) * UB + uu % UB, 1), :, :]
                             .rearrange("q o p d -> p q (o d)"), att[:, uu % 2, :, :]).then_inc(att_stored[uu % 2], 16)

            def body(i, plan, load_next, first=False, last=False):
                for slot in range(8 * UB):
                    uu, kt = slot // 8, slot % 8
                    if kt == 0 and not (last and uu >= 1):
                        load_qk(i, uu + 3)
                    if kt == 2 and not (last and uu == 3):
                        load_rows(i, uu + 1, shift_use(i, uu, last))
                    if kt == 4 and not (first and uu == 0):
                        store_att(i, uu - 1)
                    if slot == 5 and load_next is not None:
                        load_back(load_next)
                    if slot - 1 in plan:
                        fill(plan[slot - 1])
                if 8 * UB - 1 in plan:
                    fill(plan[8 * UB - 1])

            def fronts(n):
                chunks = [Chunk("front", s, n) for s in range(2)]
                return chunks

            sp.wait_ge(dve_prep, 12)
            sp.wait_ge(signs_ready, 8)
            for n in range(2):
                for ch in fronts(n):
                    load_front(ch)
                for item in front_body(fronts(n)):
                    fill(item)
            start = fronts(2)
            for ch in start:
                load_front(ch)
            for s in range(2):
                sp.wait_ge(parts_stored[s], 16 * 2 * PARTS * 2)
            for v in range(3):
                load_qk(0, v)
            for slot, item in enumerate(front_body(start)):
                fill(item)
                if slot == 16:
                    load_rows(0, 0, max_use(0, -1, SHIFT_POS))
            chunks = fronts(3)
            for ch in chunks:
                load_front(ch)
            body(0, pair_plan(chunks), None, first=True)
            for s in range(2):
                sp.wait_ge(parts_stored[s], 16 * 2 * PARTS * 4)
                sp.wait_ge(xc_stored[s], 16 * FRONT_PAIRS)
                sp.wait_ge(xn_ready[s], 4 * FRONT_PAIRS)
                sp.wait_ge(filler_ready[s], Chunk("front", s, FRONT_PAIRS - 1).written("T2b"))
            body(1, {}, None)
            with sp.Fori(2, 7) as i:
                ch = Chunk("back", 0, i - 2)
                body(i, back_plan(ch), ch)
            ch = Chunk("back", 0, 5)
            body(7, back_plan(ch), ch, last=True)
            store_att(8, -1)
            tail = [Chunk("back", 0, 6, tail=True), Chunk("back", 1, 0, tail=True)]
            for ch in tail:
                load_back(ch)
            for item in both(BACK, tail):
                fill(item)
            sp.wait_ge(xc_stored[0], 16 * (FRONT_PAIRS + 7))
            sp.wait_ge(xc_stored[1], 16 * (FRONT_PAIRS + 1))
            for s in range(2):
                sp.wait_ge(att_stored[s], 16 * NU // 2)

        @block.gpsimd
        def _(gp):
            for n, (dst, value) in enumerate(((ident[:, :], 0.0), (ones[:, :], 1.0), (mhalf[:, :], -0.5),
                                              (v_ring[:, :, :, HD:2 * HD], 1.0), (kst[SR:P, :, :], 1.0),
                                              (shift[:, :, :], 0.0), (wait_pad[:, :], 0.0))):
                if n:
                    gp.wait_ge(const_ready, n)
                gp.memset(dst, value).then_inc(const_ready, 1)
            gp.wait_ge(const_ready, 7)
            gp.iota(expert_i[:, :], pattern=[[1, E], [0, R]], base=0, channel_multiplier=0).then_inc(const_ready, 1)
            gp.wait_ge(const_ready, 8)
            gp.affine_select(out=ident[:, :], in_=ident[:, :], compare_op=ALU.not_equal, fill=1.0, base=0,
                             pattern=[[-1, P]], channel_multiplier=1).then_inc(const_ready, 1)
            gp.tensor_copy(expert_of[:, :], expert_i[:, :]).then_inc(const_ready, 1)
            gp.wait_ge(const_ready, 10)
            gp.tensor_copy(identb[:, :], ident[:, :]).then_inc(const_ready, 1)

            def norm(ch, which):
                s, L = ch.slot, ch.ln(which)
                gp_wait(gp, stats_ready[s], L * 4 + 4)
                gp.tensor_scalar(var_eps[s][:, :], meanvar[s][:, :, 1], EPS, None, ALU.add).then_inc(rstd_ready[s], 1)
                gp.wait_ge(rstd_ready[s], L * 2 + 1)
                gp.tensor_tensor(rstd[s][:, :], var_eps[s][:, :], mhalf[:, :], ALU.pow).then_inc(rstd_ready[s], 1)

            def add_bias(ch, which):
                s = ch.slot
                gp.wait_ge(xn_ready[s], ch.ln(which) * 2 + 2)
                for t in range(CT):
                    gp.tensor_tensor(xc[s][:, t, :], xc[s][:, t, :], bias_half[:, :], ALU.add).then_inc(bias_added[s], 1)

            def clamp(ch, stg, piece):
                s = ch.slot
                cols = slice(512 * piece, 512 * piece + 512)
                bnk, reads = ch.bank(stg)
                gp_wait(gp, filler_read[bnk], reads + 1)
                gp.tensor_scalar(zd[s][:, cols], z[s][:, cols], 0.0, BIG, ALU.max, ALU.min).then_inc(clamped[s], 1)
                gp.tensor_scalar(zneg[s][:, cols], z[s][:, cols], 0.0, -BIG, ALU.min, ALU.max).then_inc(clamped[s], 1)

            def fill(item):
                ch, pos = item
                s, n = ch.slot, ch.n
                if pos == "LN1":
                    norm(ch, 0)
                    add_bias(ch, 0)
                if pos == "LN2":
                    norm(ch, 1)
                if pos == "LN3":
                    norm(ch, 0)
                    add_bias(ch, 0)
                if pos in ("VK", "Q0", "Q1"):
                    clamp(ch, pos, ("VK", "Q0", "Q1").index(pos))
                if pos in ("Oa", "Ob"):
                    clamp(ch, pos, ("Oa", "Ob").index(pos))
                if pos == "SPL":
                    kq = zd[s][:, CH:CH + KQ]
                    gp.wait_ge(part_cast[s], n * 2 + 1)
                    gp.tensor_tensor(kq, kq, parts[s][:, 0, :], ALU.subtract).then_inc(part_rest[s], 1)
                    gp.wait_ge(part_cast[s], n * 2 + 2)
                    gp.wait_ge(part_rest[s], n * 2 + 1)
                    gp.tensor_tensor(parts[s][:, 2, :], kq, parts[s][:, 1, :], ALU.subtract).then_inc(part_rest[s], 1)
                if pos == "ADD":
                    gp.wait_ge(guard_step[s], ch.guard0 + 6)
                    for t in range(CT):
                        gp.tensor_tensor(xc[s][:, t, :], xc[s][:, t, :], zd[s][:, 512 * t:512 * t + 512],
                                         ALU.add).then_inc(residual[s], 1)

            def split_shift(i, uu):
                k = uu % 2
                n = REP * QT
                v4 = i * (4 * UB) + 4 * uu
                gp_wait(gp, neg_max_ready, i * UB + (uu + 1))
                gp.tensor_copy(shift[:, k, 0:n], neg_max[:, k, :]).then_inc(shift_parts, 1)
                gp.wait_ge(shift_parts, v4 + 1)
                gp.tensor_tensor(neg_max_rest[:, k, :], neg_max[:, k, :], shift[:, k, 0:n],
                                 ALU.subtract).then_inc(shift_parts, 1)
                gp_wait(gp, shift_parts, v4 + 2)
                gp.tensor_copy(shift[:, k, n:2 * n], neg_max_rest[:, k, :]).then_inc(shift_parts, 1)
                gp.wait_ge(shift_parts, v4 + 3)
                gp.tensor_tensor(shift[:, k, 2 * n:3 * n], neg_max_rest[:, k, :], shift[:, k, n:2 * n],
                                 ALU.subtract).then_inc(shift_parts, 1)

            def load_v(i, uu):
                j = i + uu // UB
                if not isinstance(i, int) or UB * i + uu >= 2:
                    gp.wait_ge(probs_used, i * (8 * UB) + 8 * (uu - 1))
                gp.tensor_copy(v_ring[:, uu % 2, :, 0:HD],
                               v_all[:, bass.ds((j // 4) * KT, KT), bass.ds((j % 2) * (UB * HD) + (uu % UB) * HD, HD)]
                               ).then_inc(v_ready, 1)

            def body(i, plan, last=False):
                for slot in range(8 * UB):
                    uu, kt = slot // 8, slot % 8
                    if kt == 2 and not (last and uu == 3):
                        load_v(i, uu + 1)
                    if slot - 1 in plan:
                        fill(plan[slot - 1])
                    if kt == 7 and not (last and uu >= 2):
                        split_shift(i, uu + 2)
                if 8 * UB - 1 in plan:
                    fill(plan[8 * UB - 1])

            gp.wait_ge(dve_prep, 12)
            for n in range(2):
                for item in front_body([Chunk("front", s, n) for s in range(2)]):
                    fill(item)
            for s in range(2):
                gp.wait_ge(filler_read[s], 2 * NF)
            load_v(0, 0)
            for slot, item in enumerate(front_body([Chunk("front", s, 2) for s in range(2)])):
                fill(item)
                if slot == 11:
                    split_shift(0, 0)
            split_shift(0, 1)
            body(0, pair_plan([Chunk("front", s, 3) for s in range(2)]))
            for s in range(2):
                gp.wait_ge(filler_read[s], 4 * NF)
            body(1, {})
            with gp.Fori(2, 7) as i:
                body(i, back_plan(Chunk("back", 0, i - 2)))
            body(7, back_plan(Chunk("back", 0, 5)), last=True)
            for item in both(BACK, [Chunk("back", 0, 6, tail=True), Chunk("back", 1, 0, tail=True)]):
                fill(item)

        @block.scalar
        def _(act):
            act.wait_ge(raw_in, 16 * 16)
            for dst, src in ((wb_h, raw_wb), (a_h, raw_a), (b_h, raw_b)):
                act.activation(dst[:], src, ACT.Copy).then_inc(signs_ready, 1)
            act.activation(wr_hl[:, :, 0:E], wr_raw[:, :, :], ACT.Copy).then_inc(signs_ready, 1)
            for dst, src in ((sk, raw_k), (sv, raw_v), (sq, raw_q), (so, raw_o)):
                act.activation(dst[:, :, :], src, ACT.Sign).then_inc(signs_ready, 1)

            def fill(item):
                ch, pos = item
                s, n = ch.slot, ch.n
                if pos in ch.uses:
                    bnk, reads = ch.bank(pos)
                    ps = ps_fill[bnk]
                if pos in ("T0a", "T0b", "T1a", "T1b", "T2a", "T2b"):
                    t = 0 if pos.endswith("a") else 1
                    act.wait_ge(filler_ready[s], ch.written(pos))
                    act.activation(xt_h[s][:, :, t * P:(t + 1) * P], ps[:, :].rearrange("p (c n) -> p c n", c=DC),
                                   ACT.Copy).then_inc(xt_h_ready[s], 1)
                if pos == "RT":
                    act.wait_ge(router_step[s], ch.ffn * R_STEPS + 7)
                    act.activation(e2[s][:, :], gap[s][:, :], ACT.Exp).then_inc(e2_ready[s], 1)
                if pos == "HT":
                    act.wait_ge(filler_ready[s], ch.written(pos))
                    act.activation(hT[s][:, :], ps[:, 0:CH], ACT.Copy).then_inc(filler_read[bnk], 1)
                if pos == "WR":
                    act.wait_ge(filler_read[bnk], reads + 1)
                    act.activation(hT_h[s][:, :], hT[s][:, :], ACT.Copy).then_inc(hT_h_ready[s], 1)
                if pos == "VK":
                    act.wait_ge(filler_ready[s], ch.written(pos))
                    if positive(n):
                        act.wait_ge(parts_stored[s], n * (16 * 2 * PARTS))
                    act.activation(z[s][:, 0:CH], ps[:, 0:CH], ACT.Copy, scale=col_scale[:, 0:1])
                    act.activation(z[s][:, CH:2 * CH], ps[:, CH:2 * CH], ACT.Copy,
                                   scale=col_scale[:, 1:2]).then_inc(filler_read[bnk], 1)
                if pos in ("Q0", "Q1"):
                    m0 = 0 if pos == "Q0" else 2
                    act.wait_ge(filler_ready[s], ch.written(pos))
                    for m in range(2):
                        a0 = 512 + (m0 + m) * CH
                        last = act.activation(z[s][:, a0:a0 + CH], ps[:, m * CH:(m + 1) * CH], ACT.Copy,
                                              scale=col_scale[:, 2 + m0 + m:3 + m0 + m])
                    last.then_inc(filler_read[bnk], 1)
                if pos == "VT":
                    act.wait_ge(filler_ready[s], ch.written(pos))
                    act.activation(v_all[:, bass.ds((n * 2 + s) * CT, CT), :],
                                   ps[:, 0:CH].rearrange("p (t n) -> p t n", t=CT), ACT.Copy
                                   ).then_inc(filler_read[bnk], 1)
                if pos == "SPL":
                    kq = zd[s][:, CH:CH + KQ]
                    act.wait_ge(guard_step[s], ch.guard0 + 9)
                    act.activation(parts[s][:, 0, :], kq, ACT.Copy).then_inc(part_cast[s], 1)
                    act.wait_ge(part_rest[s], n * 2 + 1)
                    act.activation(parts[s][:, 1, :], kq, ACT.Copy).then_inc(part_cast[s], 1)

            def exp_tile(i, uu, kt, j):
                act.wait_ge(scores_ready, i * (32 * UB) + (32 * uu + 4 * kt + j + 1))
                if j == 0 and (not isinstance(i, int) or 8 * (UB * i + uu) + kt >= 2):
                    act.wait_ge(probs_used, i * (8 * UB) + (8 * uu + kt - 1))
                act.activation(probs[:, kt % 2, j, :], ps_score[j % 2][:, :], ACT.Exp,
                               scale=1.0 / HD ** 0.5).then_inc(probs_ready, 1)

            def copy_out(i, uu):
                act.wait_ge(probs_used, i * (8 * UB) + 8 * (uu + 1))
                if not isinstance(i, int) or UB * i + uu >= 2:
                    act.wait_ge(o_turned, i * UB + (uu - 1))
                act.activation(o_sb[:, uu % 2, :], ps_out[uu % 2][:, :], ACT.Copy).then_inc(o_copied, 1)

            def body(i, plan, first=False):
                for slot in range(8 * UB):
                    uu, kt = slot // 8, slot % 8
                    exp_tile(i, uu, kt, 0)
                    exp_tile(i, uu, kt, 1)
                    if kt == 1 and not (first and uu == 0):
                        copy_out(i, uu - 1)
                    if slot - 1 in plan:
                        fill(plan[slot - 1])
                    exp_tile(i, uu, kt, 2)
                    exp_tile(i, uu, kt, 3)
                if 8 * UB - 1 in plan:
                    fill(plan[8 * UB - 1])

            for n in range(2):
                for item in front_body([Chunk("front", s, n) for s in range(2)]):
                    fill(item)
            for item in front_body([Chunk("front", s, 2) for s in range(2)]):
                fill(item)
            body(0, pair_plan([Chunk("front", s, 3) for s in range(2)]), first=True)
            body(1, {})
            with act.Fori(2, 7) as i:
                body(i, back_plan(Chunk("back", 0, i - 2)))
            body(7, back_plan(Chunk("back", 0, 5)))
            copy_out(8, -1)
            for item in both(BACK, [Chunk("back", 0, 6, tail=True), Chunk("back", 1, 0, tail=True)]):
                fill(item)

        @block.vector
        def _(dve):
            dve.wait_ge(raw_in, 16 * 16)
            dve.wait_ge(const_ready, 11)
            dve.wait_ge(signs_ready, 8)
            dve.tensor_tensor(wb_l[:, :, :], raw_wb, wb_h[:, :, :].bitcast(F32), ALU.subtract).then_inc(dve_prep, 1)
            dve.tensor_tensor(a_l[:, :, :], raw_a, a_h[:, :, :].bitcast(F32), ALU.subtract).then_inc(dve_prep, 1)
            dve.tensor_tensor(b_l[:, :], raw_b, b_h[:, :].bitcast(F32), ALU.subtract).then_inc(dve_prep, 1)
            dve.tensor_tensor(wr_hl[:, :, E:2 * E], wr_raw[:, :, :], wr_hl[:, :, 0:E].bitcast(F32),
                              ALU.subtract).then_inc(dve_prep, 1)
            dve.scalar_tensor_tensor(out=raw_o, in0=raw_o, scalar=-1.0, in1=raw_o, op0=ALU.mult, op1=ALU.max).then_inc(abs_ready, 1)
            dve.tensor_reduce(col_scale[:, 0:1], raw_vn, AX, ALU.add, apply_absolute_value=True).then_inc(dve_prep, 1)
            dve.tensor_reduce(col_scale[:, 1:2], raw_kn, AX, ALU.add, apply_absolute_value=True).then_inc(dve_prep, 1)
            dve.tensor_reduce(col_scale[:, 2:2 + DC], raw_qn, AX, ALU.add,
                              apply_absolute_value=True).then_inc(dve_prep, 1)
            dve.tensor_scalar(bias_half[:, :], bias_half[:, :], 0.5, None, ALU.mult).then_inc(dve_prep, 1)
            dve.wait_ge(dve_prep, 8)
            dve.tensor_scalar(col_scale[:, :], col_scale[:, :], 1.0 / D, 1e-8, ALU.mult, ALU.max).then_inc(dve_prep, 1)
            dve.wait_ge(dve_prep, 9)
            dve.tensor_tensor(col_scale[:, :], col_scale[:, :], raw_scale[:, :], ALU.mult).then_inc(dve_prep, 1)
            dve.wait_ge(osum_ready, 1)
            dve.tensor_scalar(o_scale[:, :], ps_out[0][:, :], 1.0 / D, 1e-8, ALU.mult, ALU.max).then_inc(dve_prep, 1)
            dve.wait_ge(dve_prep, 11)
            dve.tensor_tensor(o_scale[:, :], o_scale[:, :], osc_row[:, :], ALU.mult).then_inc(dve_prep, 1)

            def norm(ch, which):
                s, L = ch.slot, ch.ln(which)
                for t in range(CT):
                    dve.bn_stats(stats[s][:, t, :], xc[s][:, t, :]).then_inc(stats_ready[s], 1)
                dve_wait(dve, stats_ready[s], L * 4 + 2)
                for t in range(CT):
                    dve.bn_aggr(meanvar[s][:, t, :], stats[s][:, t, :]).then_inc(stats_ready[s], 1)
                dve.wait_ge(stats_ready[s], L * 4 + 4)
                dve.wait_ge(rstd_ready[s], L * 2 + 2)
                for t in range(CT):
                    dve.tensor_scalar(xn[s][:, t, :], xc[s][:, t, :], meanvar[s][:, t, 0:1], rstd[s][:, t:t + 1],
                                      ALU.subtract, ALU.mult).then_inc(xn_ready[s], 1)

            def router(ch):
                s = ch.slot
                bnk, reads = ch.bank("RT")
                base = ch.ffn * R_STEPS
                st = router_step[s]
                dve.wait_ge(filler_ready[s], ch.written("RT"))
                dve.tensor_copy(logit2[s][:, :, :], ps_fill[bnk][:, 0:CT * 2 * E].rearrange("p (t e) -> p t e", t=CT)
                                ).then_inc(filler_read[bnk], 1)
                dve.wait_ge(filler_read[bnk], reads + 1)
                dve.tensor_tensor(logit[s][:, :, :], logit2[s][:, :, 0:E], logit2[s][:, :, E:2 * E],
                                  ALU.add).then_inc(st, 1)
                dve_wait(dve, st, base + 1)
                for t in range(CT):
                    dve.max(top[s][:, t, :], logit[s][:, t, :]).then_inc(st, 1)
                dve_wait(dve, st, base + 3)
                for t in range(CT):
                    dve.max_index(top_i[s][:, t, :], top[s][:, t, :], logit[s][:, t, :]).then_inc(st, 1)
                dve.wait_ge(st, base + 5)
                dve.tensor_copy(top_e[s][:, :, :], top_i[s][:, :, 0:2]).then_inc(st, 1)
                dve.tensor_tensor(gap[s][:, :], top[s][:, :, 1], top[s][:, :, 0], ALU.subtract).then_inc(st, 1)
                dve.wait_ge(e2_ready[s], ch.ffn + 1)
                dve.tensor_scalar(den[s][:, :], e2[s][:, :], 1.0, None, ALU.add).then_inc(st, 1)
                dve.wait_ge(st, base + 8)
                dve.reciprocal(rden[s][:, :], den[s][:, :]).then_inc(st, 1)
                dve.wait_ge(st, base + 9)
                dve.tensor_scalar(w12[s][:, :, 0], rden[s][:, :], 2.0, None, ALU.mult).then_inc(st, 1)
                dve.wait_ge(st, base + 10)
                dve.tensor_tensor(w12[s][:, :, 1], w12[s][:, :, 0], e2[s][:, :], ALU.mult).then_inc(st, 1)
                dve.wait_ge(st, base + 11)
                for t in range(CT):
                    for k in range(2):
                        dve.tensor_scalar(w_tmp[s][:, 2 * t + k, :], expert_of[:, :], top_e[s][:, t, k:k + 1],
                                          w12[s][:, t, k:k + 1], ALU.is_equal, ALU.mult).then_inc(st, 1)
                dve.wait_ge(st, base + 15)
                tmp = w_tmp[s][:, :, :].rearrange("p (t k) n -> p t k n", k=2)
                dve.tensor_tensor(w_rep[s][:, :, :], tmp[:, :, 0, :], tmp[:, :, 1, :],
                                  ALU.add).then_inc(w_rep_ready[s], 1)

            def guard(ch, piece):
                s = ch.slot
                cols = slice(512 * piece, 512 * piece + 512)
                g = ch.guard0 + 3 * piece
                dve.wait_ge(clamped[s], ch.clamp0 + 2 * (piece + 1))
                dve.tensor_tensor(zd[s][:, cols], zd[s][:, cols], zneg[s][:, cols], ALU.add).then_inc(guard_step[s], 1)
                dve.wait_ge(guard_step[s], g + 1)
                mask = zneg[s][:, cols].bitcast(I32)
                dve.tensor_scalar(mask, z[s][:, cols].bitcast(I32), INF_BITS, INF_BITS, ALU.bitwise_and,
                                  ALU.bitwise_xor).then_inc(guard_step[s], 1)
                dve_wait(dve, guard_step[s], g + 2)
                dve.copy_predicated(zd[s][:, cols], mask, z[s][:, cols]).then_inc(guard_step[s], 1)

            def fill(item):
                ch, pos = item
                s, n = ch.slot, ch.n
                if pos in ch.uses:
                    bnk, reads = ch.bank(pos)
                    ps = ps_fill[bnk]
                if pos == "LN1":
                    dve.wait_ge(chunk_loaded[s], ch.load)
                    norm(ch, 0)
                if pos == "LN2":
                    dve.wait_ge(filler_read[ch.bank("FFb")[0]], ch.bank("FFb")[1] + 1)
                    norm(ch, 1)
                if pos == "LN3":
                    dve.wait_ge(residual[s], n * 2 + 2)
                    norm(ch, 0)
                if pos in ("T0a", "T0b", "T1a", "T1b", "T2a", "T2b"):
                    t = 0 if pos.endswith("a") else 1
                    dve.wait_ge(xt_h_ready[s], ch.t0 + ch.tn(pos) + 1)
                    dve.tensor_tensor(xt_l[s][:, :, t * P:(t + 1) * P], ps[:, :].rearrange("p (c n) -> p c n", c=DC),
                                      xt_h[s][:, :, t * P:(t + 1) * P].bitcast(F32),
                                      ALU.subtract).then_inc(filler_read[bnk], 1)
                if pos == "RT":
                    router(ch)
                if pos == "WR":
                    dve.wait_ge(filler_ready[s], ch.written(pos))
                    dve.wait_ge(filler_read[ch.bank("HT")[0]], ch.bank("HT")[1] + 1)
                    dve.tensor_tensor(hT[s][:, :], ps[:, 0:CH], hT[s][:, :], ALU.mult).then_inc(filler_read[bnk], 1)
                    dve.wait_ge(hT_h_ready[s], ch.ffn + 1)
                    dve.tensor_tensor(hT_l[s][:, :], hT[s][:, :], hT_h[s][:, :].bitcast(F32),
                                      ALU.subtract).then_inc(hT_l_ready[s], 1)
                if pos in ("FFa", "FFb"):
                    t = 0 if pos == "FFa" else 1
                    dve.wait_ge(filler_ready[s], ch.written(pos))
                    dve.wait_ge(bias_added[s], ch.ffn * 2 + (t + 1))
                    dve.scalar_tensor_tensor(out=xc[s][:, t, :], in0=ps[:, :], scalar=0.5, in1=xc[s][:, t, :],
                                             op0=ALU.mult, op1=ALU.add).then_inc(filler_read[bnk], 1)
                if pos == "Q1":
                    guard(ch, 0)
                if pos == "VT":
                    guard(ch, 1)
                if pos == "SPL":
                    guard(ch, 2)
                if pos in ("Oa", "Ob"):
                    t = 0 if pos == "Oa" else 1
                    dve.wait_ge(filler_ready[s], ch.written(pos))
                    dve.tensor_tensor(z[s][:, 512 * t:512 * t + 512], ps[:, :], o_scale[:, :],
                                      ALU.mult).then_inc(filler_read[bnk], 1)
                if pos == "ADD":
                    guard(ch, 0)
                    guard(ch, 1)

            def reduce_tile(i, uu, pos, t):
                use = max_use(i, uu, pos)
                b = (1 + uu + pos) % 2
                dve.wait_ge(max_scores, use + 1)
                if t == 0 and (not isinstance(i, int) or UB * i + uu >= 0):
                    dve.wait_ge(neg_max_ready, i * UB + (uu + 1))
                dve.tensor_reduce(neg_max_parts[:, uu % 2, t // 2, t % 2:t % 2 + 1], ps_max[b][:, :], AX, ALU.max,
                                  negate=True).then_inc(max_read, 1)

            def combine(i, uu, use):
                dve.wait_ge(max_read, use + 1)
                if not isinstance(i, int) or UB * i + uu >= 2:
                    dve.wait_ge(shift_parts, i * (4 * UB) + 4 * (uu - 1))
                dve.tensor_tensor(neg_max[:, uu % 2, :], neg_max_parts[:, uu % 2, :, 0], neg_max_parts[:, uu % 2, :, 1],
                                  ALU.min).then_inc(neg_max_ready, 1)

            def copy_rows(i, uu, use, b):
                dve.wait_ge(max_scores, use + 1)
                if not isinstance(i, int) or UB * i + uu >= 2:
                    dve.wait_ge(rows_loaded[(uu - 2) % UB], i * 48 + 48 * ((uu - 2) // UB + 1))
                n = PARTS * REP * QT
                dve.tensor_copy(shift_rows[0:n, uu % 2, :], ps_max[b][0:n, 0:P // 2].bitcast(BF16)
                                ).then_inc(max_read, 1)

            def normalise(i, uu):
                k = uu % 2
                o = ps_out[k][:, :].rearrange("p (q j n) -> p q j n", q=QT, j=REP)
                dve.wait_ge(o_turned, i * UB + (uu + 1))
                dve.reciprocal(recip[:, k, :, :], o[:, :, :, HD]).then_inc(recip_ready, 1)
                dve.wait_ge(recip_ready, i * UB + (uu + 1))
                if not isinstance(i, int) or UB * i + uu >= 2:
                    dve.wait_ge(att_stored[k], i * 32 + 16 * (uu // 2))
                dve.tensor_tensor(att[:, k, :, :].rearrange("p q (j d) -> p q j d", j=REP), o[:, :, :, 0:HD],
                                  recip[:, k, :, :].unsqueeze(3).broadcast_to([P, QT, REP, HD]),
                                  ALU.mult).then_inc(att_ready, 1)

            def body(i, plan, first=False, last=False):
                for slot in range(8 * UB):
                    uu, kt = slot // 8, slot % 8
                    has_max = not (last and uu >= 2)
                    tiles = max_tiles(kt) if has_max else []
                    if kt == 1 and not (last and uu == 3):
                        copy_rows(i, uu + 1, shift_use(i, uu, last), (1 + uu + (SHIFT_POS if has_max else 0)) % 2)
                    for pos, t in tiles[:2]:
                        reduce_tile(i, uu, pos, t)
                    if kt == 3 and not (first and uu == 0):
                        normalise(i, uu - 1)
                    if slot - 1 in plan:
                        fill(plan[slot - 1])
                    for pos, t in tiles[2:]:
                        reduce_tile(i, uu, pos, t)
                    if kt == 7 and has_max:
                        combine(i, uu + 2, max_use(i, uu, 32))
                if 8 * UB - 1 in plan:
                    fill(plan[8 * UB - 1])

            for n in range(2):
                for item in front_body([Chunk("front", s, n) for s in range(2)]):
                    fill(item)
            for slot, item in enumerate(front_body([Chunk("front", s, 2) for s in range(2)])):
                for use, v, t in start_uses(slot):
                    if t is None:
                        copy_rows(0, 0, use, use % 2)
                    else:
                        dve.wait_ge(max_scores, use + 1)
                        dve.tensor_reduce(neg_max_parts[:, v, t // 2, t % 2:t % 2 + 1], ps_max[use % 2][:, :], AX,
                                          ALU.max, negate=True).then_inc(max_read, 1)
                fill(item)
                if slot == 11:
                    combine(0, 0, 31)
            combine(0, 1, 64)
            body(0, pair_plan([Chunk("front", s, 3) for s in range(2)]), first=True)
            body(1, {})
            with dve.Fori(2, 7) as i:
                body(i, back_plan(Chunk("back", 0, i - 2)))
            body(7, back_plan(Chunk("back", 0, 5)), last=True)
            normalise(8, -1)
            for item in both(BACK, [Chunk("back", 0, 6, tail=True), Chunk("back", 1, 0, tail=True)]):
                fill(item)

        @block.tensor
        def _(pe):
            pe.wait_ge(abs_ready, 1)
            pe.wait_ge(const_ready, 11)
            for c in range(DC):
                last = pe.matmul(ps_out[0][:, :], ones[:, :], raw_o[:, c, :], start=(c == 0), stop=(c == DC - 1))
            last.then_inc(osum_ready, 1)
            pe.wait_ge(dve_prep, 12)

            def fill(item):
                ch, pos = item
                s = ch.slot
                if pos not in ch.uses:
                    return
                bnk, reads = ch.bank(pos)
                ps = ps_fill[bnk]
                if positive(reads):
                    pe.wait_ge(filler_read[bnk], reads)
                t = 1 if pos.endswith("b") else 0
                tok = slice(t * P, (t + 1) * P)
                if pos in ("T0a", "T0b", "T1a", "T1b", "T2a", "T2b"):
                    if pos.startswith("T0"):
                        pe.wait_ge(chunk_loaded[s], ch.load)
                    else:
                        which = 1 if pos.startswith("T2") else 0
                        pe.wait_ge(xn_ready[s], ch.ln(which) * 2 + (t + 1))
                    for c in range(DC):
                        last = pe.transpose(ps[:, c * P:(c + 1) * P], xn[s][:, t, c * P:(c + 1) * P], ident[:, :])
                if pos == "RT":
                    if ch.bank("T1b")[0] != bnk:
                        pe.wait_ge(filler_read[ch.bank("T1b")[0]], ch.bank("T1b")[1] + 1)
                    for u in range(CT):
                        for c in range(DC):
                            for x_part in (xt_h, xt_l):
                                last = pe.matmul(ps[:, u * 2 * E:(u + 1) * 2 * E],
                                                 x_part[s][:, c, u * P:(u + 1) * P], wr_hl[:, c, :],
                                                 start=(c == 0 and x_part is xt_h),
                                                 stop=(c == DC - 1 and x_part is xt_l))
                if pos == "HT":
                    pairs = ((a_h, xt_h), (a_h, xt_l), (a_l, xt_h))
                    for c in range(DC):
                        for k, (w, x_part) in enumerate(pairs):
                            last = pe.matmul(ps[:, 0:CH], w[:, c, :], x_part[s][:, c, :],
                                             start=(c == 0 and k == 0), stop=(c == DC - 1 and k == 2))
                if pos == "WR":
                    pe.wait_ge(w_rep_ready[s], ch.ffn + 1)
                    for u in range(CT):
                        last = pe.transpose(ps[:, u * P:(u + 1) * P], w_rep[s][:, u, :], ident[:, :])
                if pos in ("FFa", "FFb"):
                    for c in range(DC):
                        for k, (x_part, w) in enumerate(((xt_h, wb_h), (xt_h, wb_l), (xt_l, wb_h))):
                            pe.matmul(ps[:, :], x_part[s][:, c, tok], w[:, c, :], start=(c == 0 and k == 0), stop=False)
                    pe.wait_ge(hT_l_ready[s], ch.ffn + 1)
                    for k, (h_part, w) in enumerate(((hT_h, b_h), (hT_h, b_l), (hT_l, b_h))):
                        last = pe.matmul(ps[:, :], h_part[s][:, tok], w[:, :], start=False, stop=(k == 2))
                if pos == "VK":
                    for m, w in enumerate((sv, sk)):
                        for c in range(DC):
                            for x_part in (xt_h, xt_l):
                                last = pe.matmul(ps[:, m * CH:(m + 1) * CH], w[:, c, :], x_part[s][:, c, :],
                                                 start=(c == 0 and x_part is xt_h),
                                                 stop=(c == DC - 1 and x_part is xt_l))
                if pos in ("Q0", "Q1"):
                    m0 = 0 if pos == "Q0" else 2
                    for m in range(2):
                        for c in range(DC):
                            for x_part in (xt_h, xt_l):
                                last = pe.matmul(ps[:, m * CH:(m + 1) * CH], sq[:, c, (m0 + m) * P:(m0 + m + 1) * P],
                                                 x_part[s][:, c, :], start=(c == 0 and x_part is xt_h),
                                                 stop=(c == DC - 1 and x_part is xt_l))
                if pos == "VT":
                    pe.wait_ge(guard_step[s], ch.guard0 + 3)
                    for u in range(CT):
                        last = pe.transpose(ps[:, u * P:(u + 1) * P], zd[s][:, u * P:(u + 1) * P], ident[:, :])
                if pos in ("Oa", "Ob"):
                    for c in range(DC):
                        for x_part in (xt_h, xt_l):
                            last = pe.matmul(ps[:, :], x_part[s][:, c, tok], so[:, c, :],
                                             start=(c == 0 and x_part is xt_h), stop=(c == DC - 1 and x_part is xt_l))
                last.then_inc(filler_ready[s], 1)

            def max_matmul(use, bnk, r, t):
                j, q, half = t // (2 * QT), t // 2 % QT, t % 2
                if not isinstance(use, int) or use >= 2:
                    pe.wait_ge(max_read, use - 1)
                pe.matmul(ps_max[bnk][:, :], qst[0:SR, r, j, q * P:(q + 1) * P], kst[0:SR, r, half * 512:half * 512 + 512],
                          start=True, stop=True).then_inc(max_scores, 1)

            def shift_transpose(i, uu, use, bnk):
                pe.wait_ge(shift_parts, i * (4 * UB) + 4 * (uu + 1))
                pe.wait_ge(max_read, use - 1)
                pe.transpose(ps_max[bnk][:, 0:P // 2].bitcast(BF16), shift[:, uu % 2, :], identb[:, :]
                             ).then_inc(max_scores, 1)

            def score(i, uu, kt, j):
                if not isinstance(i, int) or 32 * (UB * i + uu) + 4 * kt + j >= 2:
                    pe.wait_ge(probs_ready, i * (32 * UB) + (32 * uu + 4 * kt + j - 1))
                pe.matmul(ps_score[j % 2][:, :], kst[0:SR + PARTS, uu, kt * P:(kt + 1) * P],
                          qst[0:SR + PARTS, uu, j, :], start=True, stop=True).then_inc(scores_ready, 1)

            def times_v(i, uu, kt):
                k = uu % 2
                pe.wait_ge(probs_ready, i * (32 * UB) + (32 * uu + 4 * kt + 4))
                if kt == 0:
                    pe.wait_ge(v_ready, i * UB + (uu + 1))
                    if not isinstance(i, int) or UB * i + uu >= 2:
                        pe.wait_ge(att_ready, i * UB + (uu - 1))
                for j in range(REP):
                    last = pe.matmul(ps_out[k][32 * j:32 * j + 32, :], v_ring[:, k, kt, :], probs[:, kt % 2, j, :],
                                     start=(kt == 0), stop=(kt == KT - 1))
                last.then_inc(probs_used, 1)

            def turn_out(i, uu):
                pe.wait_ge(o_copied, i * UB + (uu + 1))
                for q in range(QT):
                    last = pe.transpose(ps_out[uu % 2][:, q * P:(q + 1) * P], o_sb[:, uu % 2, q * P:(q + 1) * P],
                                        ident[:, :])
                last.then_inc(o_turned, 1)

            def body(i, plan, first=False, last=False):
                for slot in range(8 * UB):
                    uu, kt = slot // 8, slot % 8
                    has_max = not (last and uu >= 2)
                    if kt == 0 and has_max:
                        pe.wait_ge(qk_loaded[(uu + 2) % UB], i * 192 + 192 * ((uu + 2) // UB + 1))
                    if kt == 0:
                        pe.wait_ge(rows_loaded[uu], i * 48 + 48)
                    if kt == 1 and not (last and uu == 3):
                        shift_transpose(i, uu + 1, shift_use(i, uu, last), (1 + uu + (SHIFT_POS if has_max else 0)) % 2)
                    tiles = [(max_use(i, uu, pos), (1 + uu + pos) % 2, t) for pos, t in max_tiles(kt)] if has_max else []
                    for j in range(2):
                        if tiles:
                            max_matmul(tiles[j][0], tiles[j][1], (uu + 2) % UB, tiles[j][2])
                        score(i, uu, kt, j)
                    if not (first and slot == 0):
                        times_v(i, uu - (kt == 0), (kt - 1) % KT)
                    if kt == 2 and not (first and uu == 0):
                        turn_out(i, uu - 1)
                    for j in range(2, 4):
                        if tiles:
                            max_matmul(tiles[j][0], tiles[j][1], (uu + 2) % UB, tiles[j][2])
                        score(i, uu, kt, j)
                    if slot in plan:
                        fill(plan[slot])

            for n in range(2):
                for item in front_body([Chunk("front", s, n) for s in range(2)]):
                    fill(item)
            for slot, item in enumerate(front_body([Chunk("front", s, 2) for s in range(2)])):
                if slot in (0, 12):
                    pe.wait_ge(qk_loaded[slot // 12], 192)
                for use, v, t in start_uses(slot):
                    if t is None:
                        shift_transpose(0, 0, use, use % 2)
                    else:
                        max_matmul(use, use % 2, v, t)
                fill(item)
            body(0, pair_plan([Chunk("front", s, 3) for s in range(2)]), first=True)
            body(1, {})
            with pe.Fori(2, 7) as i:
                body(i, back_plan(Chunk("back", 0, i - 2)))
            body(7, back_plan(Chunk("back", 0, 5)), last=True)
            times_v(8, -1, KT - 1)
            turn_out(8, -1)
            for item in both(BACK, [Chunk("back", 0, 6, tail=True), Chunk("back", 1, 0, tail=True)]):
                fill(item)


def kernel(**inputs):
    import numpy as np
    from concourse import bacc
    from concourse.bass_utils import run_bass_kernel_spmd

    a = {k.replace("L0_attn_", "").replace("L0_ffn_", ""): np.asarray(v) for k, v in inputs.items()}
    cols = lambda v: np.ascontiguousarray(v.reshape(-1, P).T)
    laid = {
        "x": a["hidden_states"].reshape(T, D),
        "wbT": a["W_base"].T, "b": a["b_base"], "wrT": a["W_router"].T,
        "aT": a["lora_A"].reshape(E * R, D).T,
        "bT": a["lora_B"].transpose(0, 2, 1).reshape(E * R, D),
        "qN": a["q_weight"], "kN": a["k_weight"], "vN": a["v_weight"],
        "qT": a["q_weight"].T, "kT": a["k_weight"].T, "vT": a["v_weight"].T, "oT": a["o_weight"].T,
        "qs": cols(a["q_scale"]), "ks": cols(a["k_scale"]), "vs": cols(a["v_scale"]), "osc": a["o_scale"],
    }
    nc = bacc.Bacc("TRN2", target_bir_lowering=False, num_devices=1)
    arrays, args = {}, []
    for name, v in laid.items():
        arrays[name] = np.ascontiguousarray(v)
        args.append(nc.dram_tensor(name, v.shape, mybir.dt.from_np(v.dtype), kind="ExternalInput").ap())
    args.append(nc.dram_tensor("out", (T, D), F32, kind="ExternalOutput").ap())
    macaron(nc, *args)
    r = run_bass_kernel_spmd(nc, [arrays], core_ids=[0])
    return r.results[0]["out"].reshape(B, S, D)
```

```python
from contextlib import ExitStack

import concourse.bass as bass
from concourse import mybir

F32 = mybir.dt.float32
F32R = mybir.dt.float32r
BF16 = mybir.dt.bfloat16
I32 = mybir.dt.int32
U32 = mybir.dt.uint32
ALU = mybir.AluOpType
ACT = mybir.ActivationFunctionType
AX = mybir.AxisListType.X

P = 128
B, S, D = 2, 1024, 512
T = B * S
H, KV, HD = 32, 8, 16
REP = H // KV
E, R = 8, 16
DC = D // P
CH = 256
CT = CH // P
NCH = T // CH
BLK = 512
QT = BLK // P
KT = S // P
NU = (T // BLK) * KV
UB = 4
PARTS = 3
PAIRS = 6
SR = PAIRS * HD
Q_PARTS = (0, 0, 0, 1, 1, 2)
K_PARTS = (0, 1, 2, 0, 1, 0)
EPS = 1e-5
BIG = 1e6
INF_BITS = 0x7F800000
KQ = CH + DC * CH
ZW = 3 * 512

FRONT = [s.split() for s in (
    "LN1a", "LN1b", "", "LN1c", "", "T1a", "T1al", "T1b", "T1bl", "", "RT", "HT0", "HT1", "RU",
    "R0", "R1", "R2", "R3", "R4", "R5", "", "WR", "WH", "WL", "",
    "FFa0", "FFa1", "FFa2", "FFa3", "FFb0", "FFb1", "FFb2", "FFb3", "",
    "LN2a", "LN2b", "", "LN2c", "", "T2a", "T2al", "T2b", "T2bl", "",
    "VK0", "VK1", "Q00 C0", "Q01", "Q10 G0 C1", "Q11 P0", "G1", "VT P1 C2", "", "G2", "P2",
    "S0", "S1", "", "S2", "S3", "", "ST", "", "")]
BACK = [s.split() for s in (
    12 * [""] + ["T0a", "T0al", "T0b", "T0bl", "", "Oa0", "Oa1", "Ob0", "Ob1 C0", "", "C1", "G0", "P0", "G1", "P1",
    "ADD", "", "LN1a", "LN1b", "", "LN1c", "", "T1a", "T1al", "T1b", "T1bl", "RT", "HT0", "HT1", "RU",
    "R0", "R1", "R2", "R3", "R4", "R5", "", "WR", "WH", "WL",
    "FFa0", "FFa1", "FFa2", "FFa3", "FFb0", "FFb1", "FFb2", "FFb3"])]
F_USES = ["T1a", "T1b", "RT", "HT", "RU", "WR", "FFa", "FFb", "T2a", "T2b", "VK", "Q0", "Q1", "VT"]
B_USES = ["T0a", "T0b", "Oa", "Ob", "T1a", "T1b", "RT", "HT", "RU", "WR", "FFa", "FFb"]
PIECES = {"HT": 2, "FFa": DC, "FFb": DC, "VK": 2, "Q0": 2, "Q1": 2, "Oa": 2, "Ob": 2}
NF, NB = len(F_USES), len(B_USES)
FRONT_PAIRS = NCH // 2
ALONE_PAIRS = FRONT_PAIRS - 1
PAIR_PERIOD = 47
LOOP_BACKS = NCH - 2
WAIT_PADS = 256
R_STEPS = 14


def stage_of(step):
    for stage, pieces in PIECES.items():
        if step[:-1] == stage:
            return stage, int(step[-1]), int(step[-1]) == pieces - 1
    return step, 0, True


class Chunk:

    def __init__(self, kind, slot, n, tail=False):
        self.kind, self.slot, self.n, self.tail = kind, slot, n, tail
        self.front = kind == "front"
        self.alone = tail or (self.front and isinstance(n, int) and n < ALONE_PAIRS)
        self.uses = F_USES if self.front else B_USES
        self.ffn = n if self.front else FRONT_PAIRS + n
        self.t0 = n * 4 if self.front else 4 * FRONT_PAIRS + n * 4
        self.guard0 = n * 9 if self.front else 9 * FRONT_PAIRS + n * 6
        self.clamp0 = n * 6 if self.front else 6 * FRONT_PAIRS + n * 4
        self.load = (n + 1) * 16 if self.front else 16 * FRONT_PAIRS + (n + 1) * 48
        self.mb0 = n * NF if self.front else NF * FRONT_PAIRS + n * NB

    def ln(self, which):
        return self.n * 2 + which if self.front else 2 * FRONT_PAIRS + self.n

    def written(self, stage):
        return self.mb0 + (self.uses.index(stage) + 1)

    def bank(self, stage):
        s = self.uses.index(stage)
        if self.front and self.alone:
            return self.slot, self.n * NF + s
        if self.front:
            return s % 2, ALONE_PAIRS * NF + self.slot * (NF // 2) + s // 2
        if not self.tail:
            return s % 2, NF * FRONT_PAIRS + self.n * (NB // 2) + s // 2
        return self.slot, NF * FRONT_PAIRS + (NB // 2) * LOOP_BACKS + s

    def tn(self, stage):
        return ["T1a", "T1b", "T2a", "T2b"].index(stage) if self.front else ["T0a", "T0b", "T1a", "T1b"].index(stage)


def positive(value):
    return not isinstance(value, int) or value > 0


def macaron(nc, x, wbT, b, wrT, aT, bT, qN, kN, vN, qT, kT, vT, oT, qs, ks, vs, osc, out):
    ctx = ExitStack()
    with ctx:
        def sb(name, shape, dt):
            return ctx.enter_context(nc.sbuf_tensor(name, shape, dt))

        def sem(name):
            return ctx.enter_context(nc.semaphore(name))

        x1_dram = nc.dram_tensor("x1_dram", [T, D], F32, kind="Internal").ap()
        q_dram = nc.dram_tensor("q_dram", [PARTS, D, T], BF16, kind="Internal").ap()
        k_dram = nc.dram_tensor("k_dram", [PARTS, P, T], BF16, kind="Internal").ap()
        att_dram = nc.dram_tensor("att_dram", [T // P, KV, P, REP * HD], F32, kind="Internal").ap()

        ident = sb("ident", [P, P], F32)
        identb = sb("identb", [P, P], BF16)
        ones = sb("ones", [P, P], F32)
        hi_plus_lo = sb("hi_plus_lo", [2 * E, E], F32)
        expert_of = sb("expert_of", [P, P], F32)
        expert_i = sb("expert_i", [P, P], I32)
        mhalf = sb("mhalf", [P, CT], F32)
        wb_h, wb_l = sb("wb_h", [P, DC, D], F32R), sb("wb_l", [P, DC, D], F32R)
        wr_hl = sb("wr_hl", [P, DC, 2 * E], F32R)
        a_h, a_l = sb("a_h", [P, DC, P], F32R), sb("a_l", [P, DC, P], F32R)
        b_h, b_l = sb("b_h", [P, D], F32R), sb("b_l", [P, D], F32R)
        sq, sk = sb("sq", [P, DC, D], F32R), sb("sk", [P, DC, P], F32R)
        sv, so = sb("sv", [P, DC, P], F32R), sb("so", [P, DC, D], F32R)
        bias_half = sb("bias_half", [P, D], F32)
        o_scale = sb("o_scale", [P, D], F32)
        osc_row = sb("osc_row", [P, D], F32)
        raw_scale = sb("raw_scale", [P, 2 + DC], F32)
        col_scale = sb("col_scale", [P, 2 + DC], F32)
        wr_raw = sb("wr_raw", [P, DC, E], F32)

        probs = sb("probs", [P, 2, REP, BLK], F32)
        qst = sb("qst", [P, UB, REP, BLK], BF16)
        kst = sb("kst", [P, UB, S], BF16)
        v_all = sb("v_all", [P, T // P, KV * HD], F32)
        v_ring = sb("v_ring", [P, 2, KT, 2 * HD], F32)
        neg_max_parts = sb("neg_max_parts", [P, 2, REP * QT, 2], F32)
        neg_max = sb("neg_max", [P, 2, REP * QT], F32)
        neg_max_rest = sb("neg_max_rest", [P, 2, REP * QT], F32)
        shift = sb("shift", [P, 2, P], BF16)
        wait_pad = sb("wait_pad", [1, WAIT_PADS], BF16)
        shift_rows = sb("shift_rows", [P, 2, P], BF16)
        o_sb = sb("o_sb", [P, 2, BLK], F32)
        recip = sb("recip", [P, 2, QT, REP], F32)
        att = sb("att", [P, 2, QT, REP * HD], F32)

        xc = [sb(f"xc{s}", [P, CT, D], F32) for s in range(2)]
        xn = [sb(f"xn{s}", [P, CT, D], F32) for s in range(2)]
        xt_h = [sb(f"xt_h{s}", [P, DC, CH], F32R) for s in range(2)]
        xt_l = [sb(f"xt_l{s}", [P, DC, CH], F32R) for s in range(2)]
        hT = [sb(f"hT{s}", [P, CH], F32) for s in range(2)]
        hT_h = [sb(f"hT_h{s}", [P, CH], F32R) for s in range(2)]
        hT_l = [sb(f"hT_l{s}", [P, CH], F32R) for s in range(2)]
        w_rep = [sb(f"w_rep{s}", [P, CT, P], F32) for s in range(2)]
        w_tmp = [sb(f"w_tmp{s}", [P, 2 * CT, P], F32) for s in range(2)]
        zm = [sb(f"zm{s}", [P, 2 * ZW], F32) for s in range(2)]
        zd = [sb(f"zd{s}", [P, ZW], F32) for s in range(2)]
        stats = [sb(f"stats{s}", [P, CT, 6], F32) for s in range(2)]
        meanvar = [sb(f"meanvar{s}", [P, CT, 2], F32) for s in range(2)]
        var_eps = [sb(f"var_eps{s}", [P, CT], F32) for s in range(2)]
        rstd = [sb(f"rstd{s}", [P, CT], F32) for s in range(2)]
        logits_t = [sb(f"logits_t{s}", [2 * E, CH], F32) for s in range(2)]
        logit = [sb(f"logit{s}", [P, CT, E], F32) for s in range(2)]
        top = [sb(f"top{s}", [P, CT, 8], F32) for s in range(2)]
        top_i = [sb(f"top_i{s}", [P, CT, 8], U32) for s in range(2)]
        top_e = [sb(f"top_e{s}", [P, CT, 2], F32) for s in range(2)]
        gap = [sb(f"gap{s}", [P, CT], F32) for s in range(2)]
        e2 = [sb(f"e2{s}", [P, CT], F32) for s in range(2)]
        den = [sb(f"den{s}", [P, CT], F32) for s in range(2)]
        rden = [sb(f"rden{s}", [P, CT], F32) for s in range(2)]
        w12 = [sb(f"w12{s}", [P, CT, 2], F32) for s in range(2)]

        z = [t[:, 0:ZW] for t in zm]
        zneg = [t[:, ZW:2 * ZW] for t in zm]
        parts = [t[:, 0:PARTS * KQ // 2].bitcast(BF16).rearrange("p (c n) -> p c n", c=PARTS) for t in zm]

        raw_wb, raw_q = probs[:, 0, :, :], probs[:, 1, :, :]
        raw_qn = zm[0][:, 0:DC * D].rearrange("p (c n) -> p c n", c=DC)
        raw_o = zm[1][:, 0:DC * D].rearrange("p (c n) -> p c n", c=DC)
        stage = [qst[:, r, :, :].rearrange("p a b -> p (a b)").bitcast(F32) for r in range(UB)]
        raw_k, raw_v = [stage[0][:, i * D:(i + 1) * D].rearrange("p (c n) -> p c n", c=DC) for i in range(2)]
        raw_a, raw_b = stage[1][:, 0:D].rearrange("p (c n) -> p c n", c=DC), stage[1][:, D:2 * D]
        raw_vn, raw_kn = stage[2][:, 0:D], stage[2][:, D:2 * D]

        def bank(name):
            return ctx.enter_context(nc.psum_tensor(name, [P, 512], F32))

        ps_max = [bank(f"ps_max{i}") for i in range(2)]
        ps_score = [bank(f"ps_score{i}") for i in range(2)]
        ps_out = [bank(f"ps_out{i}") for i in range(2)]
        ps_fill = [bank(f"ps_fill{i}") for i in range(2)]

        ffn_in = sem("ffn_in")
        attn_in = sem("attn_in")
        const_ready = sem("const_ready")
        ffn_hi = sem("ffn_hi")
        ffn_lo = sem("ffn_lo")
        signs_ready = sem("signs_ready")
        abs_ready = sem("abs_ready")
        osum_ready = sem("osum_ready")
        scale_step = sem("scale_step")
        qk_loaded = [sem(f"qk_loaded{r}") for r in range(UB)]
        rows_loaded = [sem(f"rows_loaded{r}") for r in range(UB)]
        max_scores = sem("max_scores")
        max_read = sem("max_read")
        neg_max_ready = sem("neg_max_ready")
        shift_parts = sem("shift_parts")
        scores_ready = sem("scores_ready")
        probs_ready = sem("probs_ready")
        probs_used = sem("probs_used")
        v_ready = sem("v_ready")
        o_copied = sem("o_copied")
        o_turned = sem("o_turned")
        recip_ready = sem("recip_ready")
        att_ready = sem("att_ready")
        att_stored = [sem(f"att_stored{i}") for i in range(2)]
        filler_ready = [sem(f"filler_ready{s}") for s in range(2)]
        filler_read = [sem(f"filler_read{i}") for i in range(2)]
        chunk_loaded = [sem(f"chunk_loaded{s}") for s in range(2)]
        stats_ready = [sem(f"stats_ready{s}") for s in range(2)]
        rstd_ready = [sem(f"rstd_ready{s}") for s in range(2)]
        xn_ready = [sem(f"xn_ready{s}") for s in range(2)]
        bias_added = [sem(f"bias_added{s}") for s in range(2)]
        xt_h_ready = [sem(f"xt_h_ready{s}") for s in range(2)]
        router_step = [sem(f"router_step{s}") for s in range(2)]
        e2_ready = [sem(f"e2_ready{s}") for s in range(2)]
        w_rep_ready = [sem(f"w_rep_ready{s}") for s in range(2)]
        hT_h_ready = [sem(f"hT_h_ready{s}") for s in range(2)]
        hT_l_ready = [sem(f"hT_l_ready{s}") for s in range(2)]
        clamped = [sem(f"clamped{s}") for s in range(2)]
        guard_step = [sem(f"guard_step{s}") for s in range(2)]
        part_cast = [sem(f"part_cast{s}") for s in range(2)]
        part_rest = [sem(f"part_rest{s}") for s in range(2)]
        parts_stored = [sem(f"parts_stored{s}") for s in range(2)]
        xc_stored = [sem(f"xc_stored{s}") for s in range(2)]
        residual = [sem(f"residual{s}") for s in range(2)]

        pad_columns = iter(range(1, WAIT_PADS))

        def pad():
            c = next(pad_columns)
            return wait_pad[0:1, c:c + 1]

        def dve_wait(dve, semaphore, value):
            if isinstance(value, int):
                dve.wait_ge(semaphore, value)
            else:
                dve.wait_ge(semaphore, value)
                dve.tensor_copy(pad(), wait_pad[0:1, 0:1])

        def gp_wait(gp, semaphore, value):
            if isinstance(value, int):
                gp.wait_ge(semaphore, value)
            else:
                gp.wait_ge(semaphore, value)
                gp.tensor_tensor(pad(), wait_pad[0:1, 0:1], wait_pad[0:1, 0:1], ALU.add)

        def max_use(i, uu, pos):
            return i * (33 * UB) + (65 + 33 * uu + pos)

        SHIFT_POS = 4

        def max_tiles(kt):
            return [(t + (t >= SHIFT_POS), t) for t in range(4 * kt, 4 * kt + 4)]

        def shift_use(i, uu, last):
            return max_use(i, uu, 0 if last and uu >= 2 else SHIFT_POS)

        def start_uses(step):
            uses = [(t, 0, t) for t in range(32)]
            uses += [(max_use(0, -1, pos), 1, t) for pos, t in enumerate(range(SHIFT_POS))]
            uses += [(max_use(0, -1, SHIFT_POS), 0, None)]
            uses += [(max_use(0, -1, t + 1), 1, t) for t in range(SHIFT_POS, 32)]
            return [u for n, u in enumerate(uses) if START + n * START_PACE[0] // START_PACE[1] == step]

        def in_turns(steps, chunks, period):
            keyed = [(ch.n * period + k, ch.slot, j, ch, step) for ch in chunks for k, line in enumerate(steps)
                     for j, step in enumerate(line)]
            return [(key, ch, step) for key, _, _, ch, step in sorted(keyed, key=lambda t: t[:3])]

        keyed = in_turns(FRONT, [Chunk("front", s, n) for n in range(ALONE_PAIRS) for s in range(2)], PAIR_PERIOD)
        ALONE = [(ch, step) for _, ch, step in keyed]
        BATCH0_STORED = max(k for k, (ch, step) in enumerate(ALONE) if ch.n == 1 and step == "ST") + 1
        START = BATCH0_STORED + 2
        START_PACE = (len(ALONE) - START, 65)

        def front_plan(slot):
            return {k: [(Chunk("front", slot, FRONT_PAIRS - 1), step) for step in line]
                    for k, line in enumerate(FRONT)}

        def back_plan(chunk):
            return {k: [(chunk, step) for step in line] for k, line in enumerate(BACK)}

        def tail_steps():
            chunks = [Chunk("back", 0, 6, tail=True), Chunk("back", 1, 0, tail=True)]
            return [(ch, step) for line in BACK for step in line for ch in chunks]

        block = ctx.enter_context(nc.Block())

        @block.sync
        def _(sp):
            def chunk_rows(dram, c):
                return dram[bass.ds(c * CH, CH), :].rearrange("(t p) d -> p t d", p=P)

            def load_front(ch):
                s, n = ch.slot, ch.n
                if n > 0:
                    sp.wait_ge(xc_stored[s], n * 16)
                    sp.wait_ge(xn_ready[s], n * (2 * 2))
                sp.dma_start(xc[s][:, :, :], chunk_rows(x, n * 2 + s)).then_inc(chunk_loaded[s], 16)

            def fill(item):
                ch, pos = item
                s, n = ch.slot, ch.n
                if ch.front and pos == "VK1" and n < FRONT_PAIRS - 1:
                    load_front(Chunk("front", s, n + 1))
                if ch.front and pos == "FFb3":
                    sp.wait_ge(filler_read[ch.bank("FFb")[0]], ch.bank("FFb")[1] + 1)
                    sp.dma_start(chunk_rows(x1_dram, n * 2 + s), xc[s][:, :, :]).then_inc(xc_stored[s], 16)
                if ch.front and pos == "ST":
                    c = n * 2 + s
                    sp.wait_ge(part_rest[s], n * 2 + 2)
                    for part in range(PARTS):
                        sp.dma_start(k_dram[part, :, bass.ds(c * CH, CH)],
                                     parts[s][:, part, 0:CH]).then_inc(parts_stored[s], 16)
                        sp.dma_start(q_dram[part, :, bass.ds(c * CH, CH)].rearrange("(m p) t -> p m t", p=P),
                                     parts[s][:, part, CH:KQ].rearrange("p (m t) -> p m t", t=CH)
                                     ).then_inc(parts_stored[s], 16)
                if not ch.front and pos == "FFb3":
                    a = n if not ch.tail else NCH - 2 + s
                    for st in ("FFa", "FFb"):
                        sp.wait_ge(filler_read[ch.bank(st)[0]], ch.bank(st)[1] + 1)
                    sp.dma_start(chunk_rows(out, a), xc[s][:, :, :]).then_inc(xc_stored[s], 16)

            def load_back(ch):
                s, n = ch.slot, ch.n
                a = n if not ch.tail else NCH - 2 + s
                sp.wait_ge(xc_stored[s], n * 16 + 16 * FRONT_PAIRS)
                for i in range(2):
                    sp.wait_ge(att_stored[i], (a // 2) * 64 + 64)
                sp.dma_start(xc[s][:, :, :], chunk_rows(x1_dram, a)).then_inc(chunk_loaded[s], 16)
                for t in range(CT):
                    sp.dma_start(xn[s][:, t, :].rearrange("p (k d) -> p k d", k=KV),
                                 att_dram[bass.ds(a * 2 + t, 1), :, :, :].rearrange("o k p d -> p (o k) d")
                                 ).then_inc(chunk_loaded[s], 16)

            def load_qk(i, uu):
                r = uu % UB
                if not isinstance(i, int) or UB * i + uu >= UB:
                    sp.wait_ge(scores_ready, i * (32 * UB) + 32 * (uu - 3))
                j = i + uu // UB
                t0, o0, k0 = (j // 2) * BLK, (j % 2) * (UB * REP * HD) + r * REP * HD, (j // 4) * S
                for slot in range(PAIRS):
                    rows = slice(slot * HD, (slot + 1) * HD)
                    sp.dma_start(qst[rows, r, :, :],
                                 q_dram[Q_PARTS[slot], bass.ds(o0, REP * HD), bass.ds(t0, BLK)]
                                 .rearrange("(j d) t -> d j t", j=REP)).then_inc(qk_loaded[r], 16)
                    sp.dma_start(kst[rows, r, :],
                                 k_dram[K_PARTS[slot], bass.ds((j % 2) * (UB * HD) + r * HD, HD), bass.ds(k0, S)]
                                 ).then_inc(qk_loaded[r], 16)

            def load_rows(i, uu, use):
                r = uu % UB
                sp.wait_ge(max_read, use + 1)
                for part in range(PARTS):
                    sp.dma_start(qst[SR + part:SR + part + 1, r, :, :].rearrange("c j (q p) -> c (j q) p", p=P),
                                 shift_rows[REP * QT * part:REP * QT * (part + 1), uu % 2, :]
                                 ).then_inc(rows_loaded[r], 16)

            def store_att(i, uu):
                j = i + uu // UB
                sp.wait_ge(att_ready, i * UB + (uu + 1))
                sp.dma_start(att_dram[bass.ds((j // 2) * QT, QT), bass.ds((j % 2) * UB + uu % UB, 1), :, :]
                             .rearrange("q o p d -> p q (o d)"), att[:, uu % 2, :, :]).then_inc(att_stored[uu % 2], 16)

            def body(i, plan, load_next, first=False, last=False):
                for slot in range(8 * UB):
                    uu, kt = slot // 8, slot % 8
                    if kt == 0 and not (last and uu >= 1):
                        load_qk(i, uu + 3)
                    if kt == 2 and not (last and uu == 3):
                        load_rows(i, uu + 1, shift_use(i, uu, last))
                    if kt == 4 and not (first and uu == 0):
                        store_att(i, uu - 1)
                    if slot == 5 and load_next is not None:
                        load_back(load_next)
                    for half in (2 * slot - 2, 2 * slot - 1):
                        for item in plan.get(half, []):
                            fill(item)

            for s in range(2):
                load_front(Chunk("front", s, 0))
            for dst, src in (
                (bias_half[:, :], b.partition_broadcast(P)),
                (wr_raw[:, :, :], wrT.rearrange("(c p) n -> p c n", p=P)),
                (raw_a, aT.rearrange("(c p) n -> p c n", p=P)),
                (raw_wb, wbT.rearrange("(c p) n -> p c n", p=P)), (raw_b, bT),
            ):
                sp.dma_start(dst, src).then_inc(ffn_in, 16)
            for dst, src in (
                (osc_row[:, :], osc.partition_broadcast(P)),
                (raw_scale[:, 0:1], vs), (raw_scale[:, 1:2], ks), (raw_scale[:, 2:2 + DC], qs),
                (raw_k, kT.rearrange("(c p) n -> p c n", p=P)), (raw_v, vT.rearrange("(c p) n -> p c n", p=P)),
                (raw_kn, kN), (raw_vn, vN), (raw_q, qT.rearrange("(c p) n -> p c n", p=P)),
                (raw_qn, qN.rearrange("(c p) n -> p c n", p=P)), (raw_o, oT.rearrange("(c p) n -> p c n", p=P)),
            ):
                sp.dma_start(dst, src).then_inc(attn_in, 16)
            for k, item in enumerate(ALONE):
                if k == BATCH0_STORED:
                    for s in range(2):
                        sp.wait_ge(parts_stored[s], 16 * 2 * PARTS * 2)
                    sp.wait_ge(scale_step, 7)
                    sp.wait_ge(signs_ready, 4)
                    for v in range(3):
                        load_qk(0, v)
                fill(item)
                if [u for u in start_uses(k) if u[2] is None]:
                    load_rows(0, 0, max_use(0, -1, SHIFT_POS))
            body(0, front_plan(0), None, first=True)
            body(1, front_plan(1), None)
            for s in range(2):
                sp.wait_ge(parts_stored[s], 16 * 2 * PARTS * 4)
                sp.wait_ge(xc_stored[s], 16 * FRONT_PAIRS)
                sp.wait_ge(xn_ready[s], 4 * FRONT_PAIRS)
                sp.wait_ge(filler_ready[s], Chunk("front", s, FRONT_PAIRS - 1).written("T2b"))
            with sp.Fori(2, 7) as i:
                ch = Chunk("back", 0, i - 2)
                body(i, back_plan(ch), ch)
            ch = Chunk("back", 0, 5)
            body(7, back_plan(ch), ch, last=True)
            store_att(8, -1)
            for ch in (Chunk("back", 0, 6, tail=True), Chunk("back", 1, 0, tail=True)):
                load_back(ch)
            for item in tail_steps():
                fill(item)
            sp.wait_ge(xc_stored[0], 16 * (FRONT_PAIRS + 7))
            sp.wait_ge(xc_stored[1], 16 * (FRONT_PAIRS + 1))
            for s in range(2):
                sp.wait_ge(att_stored[s], 16 * NU // 2)

        @block.gpsimd
        def _(gp):
            for n, (dst, value) in enumerate(((ident[:, :], 0.0), (ones[:, :], 1.0), (mhalf[:, :], -0.5),
                                              (v_ring[:, :, :, HD:2 * HD], 1.0), (kst[SR:P, :, :], 1.0),
                                              (shift[:, :, :], 0.0), (wait_pad[:, :], 0.0))):
                if n:
                    gp.wait_ge(const_ready, n)
                gp.memset(dst, value).then_inc(const_ready, 1)
            gp.wait_ge(const_ready, 7)
            gp.iota(expert_i[:, :], pattern=[[1, E], [0, R]], base=0, channel_multiplier=0).then_inc(const_ready, 1)
            gp.wait_ge(const_ready, 8)
            gp.affine_select(out=ident[:, :], in_=ident[:, :], compare_op=ALU.not_equal, fill=1.0, base=0,
                             pattern=[[-1, P]], channel_multiplier=1).then_inc(const_ready, 1)
            gp.tensor_copy(expert_of[:, :], expert_i[:, :]).then_inc(const_ready, 1)
            gp.wait_ge(const_ready, 10)
            gp.tensor_copy(identb[:, :], ident[:, :]).then_inc(const_ready, 1)
            gp.tensor_tensor(hi_plus_lo[:, :], ident[0:2 * E, 0:E], ident[0:2 * E, E:2 * E],
                             ALU.add).then_inc(const_ready, 1)

            def norm(ch, which):
                s, L = ch.slot, ch.ln(which)
                gp_wait(gp, stats_ready[s], L * 4 + 4)
                gp.tensor_scalar(var_eps[s][:, :], meanvar[s][:, :, 1], EPS, None, ALU.add).then_inc(rstd_ready[s], 1)
                gp.wait_ge(rstd_ready[s], L * 2 + 1)
                gp.tensor_tensor(rstd[s][:, :], var_eps[s][:, :], mhalf[:, :], ALU.pow).then_inc(rstd_ready[s], 1)

            def add_bias(ch, which):
                s = ch.slot
                gp.wait_ge(xn_ready[s], ch.ln(which) * 2 + 2)
                for t in range(CT):
                    gp.tensor_tensor(xc[s][:, t, :], xc[s][:, t, :], bias_half[:, :], ALU.add).then_inc(bias_added[s], 1)

            def clamp(ch, stg, piece):
                s = ch.slot
                cols = slice(512 * piece, 512 * piece + 512)
                bnk, reads = ch.bank(stg)
                gp_wait(gp, filler_read[bnk], reads + 1)
                gp.tensor_scalar(zd[s][:, cols], z[s][:, cols], 0.0, BIG, ALU.max, ALU.min).then_inc(clamped[s], 1)
                gp.tensor_scalar(zneg[s][:, cols], z[s][:, cols], 0.0, -BIG, ALU.min, ALU.max).then_inc(clamped[s], 1)

            def fill(item):
                ch, pos = item
                s, n = ch.slot, ch.n
                if pos in ("LN1b", "LN2b"):
                    norm(ch, 0 if pos == "LN1b" else 1)
                if ch.alone:
                    return
                if pos == "LN1c":
                    add_bias(ch, 0)
                if pos in ("C0", "C1", "C2"):
                    k = int(pos[1])
                    clamp(ch, (("VK", "Q0", "Q1") if ch.front else ("Oa", "Ob"))[k], k)
                if pos in ("S1", "S3"):
                    kq = zd[s][:, CH:CH + KQ]
                    k = 1 if pos == "S1" else 2
                    gp.wait_ge(part_cast[s], n * 2 + k)
                    if k == 1:
                        gp.tensor_tensor(kq, kq, parts[s][:, 0, :], ALU.subtract).then_inc(part_rest[s], 1)
                    else:
                        gp.wait_ge(part_rest[s], n * 2 + 1)
                        gp.tensor_tensor(parts[s][:, 2, :], kq, parts[s][:, 1, :], ALU.subtract).then_inc(part_rest[s], 1)
                if pos == "ADD":
                    gp.wait_ge(guard_step[s], ch.guard0 + 6)
                    for t in range(CT):
                        gp.tensor_tensor(xc[s][:, t, :], xc[s][:, t, :], zd[s][:, 512 * t:512 * t + 512],
                                         ALU.add).then_inc(residual[s], 1)

            def split_shift(i, uu):
                k = uu % 2
                n = REP * QT
                v4 = i * (4 * UB) + 4 * uu
                gp_wait(gp, neg_max_ready, i * UB + (uu + 1))
                gp.tensor_copy(shift[:, k, 0:n], neg_max[:, k, :]).then_inc(shift_parts, 1)
                gp.wait_ge(shift_parts, v4 + 1)
                gp.tensor_tensor(neg_max_rest[:, k, :], neg_max[:, k, :], shift[:, k, 0:n],
                                 ALU.subtract).then_inc(shift_parts, 1)
                gp_wait(gp, shift_parts, v4 + 2)
                gp.tensor_copy(shift[:, k, n:2 * n], neg_max_rest[:, k, :]).then_inc(shift_parts, 1)
                gp.wait_ge(shift_parts, v4 + 3)
                gp.tensor_tensor(shift[:, k, 2 * n:3 * n], neg_max_rest[:, k, :], shift[:, k, n:2 * n],
                                 ALU.subtract).then_inc(shift_parts, 1)

            def load_v(i, uu):
                j = i + uu // UB
                if not isinstance(i, int) or UB * i + uu >= 2:
                    gp.wait_ge(probs_used, i * (8 * UB) + 8 * (uu - 1))
                gp.tensor_copy(v_ring[:, uu % 2, :, 0:HD],
                               v_all[:, bass.ds((j // 4) * KT, KT), bass.ds((j % 2) * (UB * HD) + (uu % UB) * HD, HD)]
                               ).then_inc(v_ready, 1)

            def body(i, plan, last=False):
                for slot in range(8 * UB):
                    uu, kt = slot // 8, slot % 8
                    if kt == 2 and not (last and uu == 3):
                        load_v(i, uu + 1)
                    for half in (2 * slot - 1, 2 * slot):
                        for item in plan.get(half, []):
                            fill(item)
                    if kt == 7 and not (last and uu >= 2):
                        split_shift(i, uu + 2)

            for k, item in enumerate(ALONE):
                if k == START:
                    for s in range(2):
                        gp.wait_ge(filler_read[s], 2 * NF)
                    load_v(0, 0)
                if start_uses(k) and start_uses(k)[0][0] == 33:
                    split_shift(0, 0)
                fill(item)
            split_shift(0, 1)
            gp.wait_ge(ffn_lo, 5)
            body(0, front_plan(0))
            body(1, front_plan(1))
            for s in range(2):
                gp.wait_ge(filler_read[s], FRONT_PAIRS * NF)
            with gp.Fori(2, 7) as i:
                body(i, back_plan(Chunk("back", 0, i - 2)))
            body(7, back_plan(Chunk("back", 0, 5)), last=True)
            for item in tail_steps():
                fill(item)

        @block.scalar
        def _(act):
            act.wait_ge(ffn_in, 5 * 16)
            act.activation(wr_hl[:, :, 0:E], wr_raw[:, :, :], ACT.Copy).then_inc(ffn_hi, 1)
            for dst, src in ((a_h, raw_a), (wb_h, raw_wb), (b_h, raw_b)):
                act.activation(dst[:], src, ACT.Copy).then_inc(ffn_hi, 1)

            def attn_weights():
                act.wait_ge(attn_in, 11 * 16)
                for dst, src in ((so, raw_o), (sk, raw_k), (sv, raw_v), (sq, raw_q)):
                    act.activation(dst[:, :, :], src, ACT.Sign).then_inc(signs_ready, 1)

            def fill(item):
                ch, pos = item
                s, n = ch.slot, ch.n
                pos, _, final = stage_of(pos)
                if not final:
                    return
                if pos in ch.uses:
                    bnk, reads = ch.bank(pos)
                    ps = ps_fill[bnk]
                if pos in ("T0a", "T0b", "T1a", "T1b", "T2a", "T2b"):
                    t = 0 if pos.endswith("a") else 1
                    act.wait_ge(filler_ready[s], ch.written(pos))
                    act.activation(xt_h[s][:, :, t * P:(t + 1) * P], ps[:, :].rearrange("p (c n) -> p c n", c=DC),
                                   ACT.Copy).then_inc(xt_h_ready[s], 1)
                if pos == "RT":
                    act.wait_ge(filler_ready[s], ch.written(pos))
                    act.activation(logits_t[s][:, :], ps[0:2 * E, 0:CH], ACT.Copy).then_inc(filler_read[bnk], 1)
                if pos == "R2":
                    act.wait_ge(router_step[s], ch.ffn * R_STEPS + 6)
                    act.activation(e2[s][:, :], gap[s][:, :], ACT.Exp).then_inc(e2_ready[s], 1)
                if pos == "HT":
                    act.wait_ge(filler_ready[s], ch.written(pos))
                    act.activation(hT[s][:, :], ps[:, 0:CH], ACT.Copy).then_inc(filler_read[bnk], 1)
                if pos == "WH":
                    act.wait_ge(filler_read[ch.bank("WR")[0]], ch.bank("WR")[1] + 1)
                    act.activation(hT_h[s][:, :], hT[s][:, :], ACT.Copy).then_inc(hT_h_ready[s], 1)
                if pos == "VK":
                    act.wait_ge(filler_ready[s], ch.written(pos))
                    act.wait_ge(scale_step, 7)
                    if positive(n):
                        act.wait_ge(parts_stored[s], n * (16 * 2 * PARTS))
                    act.activation(z[s][:, 0:CH], ps[:, 0:CH], ACT.Copy, scale=col_scale[:, 0:1])
                    act.activation(z[s][:, CH:2 * CH], ps[:, CH:2 * CH], ACT.Copy,
                                   scale=col_scale[:, 1:2]).then_inc(filler_read[bnk], 1)
                if pos in ("Q0", "Q1"):
                    m0 = 0 if pos == "Q0" else 2
                    act.wait_ge(filler_ready[s], ch.written(pos))
                    for m in range(2):
                        a0 = 512 + (m0 + m) * CH
                        last = act.activation(z[s][:, a0:a0 + CH], ps[:, m * CH:(m + 1) * CH], ACT.Copy,
                                              scale=col_scale[:, 2 + m0 + m:3 + m0 + m])
                    last.then_inc(filler_read[bnk], 1)
                if pos == "VT":
                    act.wait_ge(filler_ready[s], ch.written(pos))
                    act.activation(v_all[:, bass.ds((n * 2 + s) * CT, CT), :],
                                   ps[:, 0:CH].rearrange("p (t n) -> p t n", t=CT), ACT.Copy
                                   ).then_inc(filler_read[bnk], 1)
                if pos == "S0":
                    act.wait_ge(guard_step[s], ch.guard0 + 9)
                    act.activation(parts[s][:, 0, :], zd[s][:, CH:CH + KQ], ACT.Copy).then_inc(part_cast[s], 1)
                if pos == "S2":
                    act.wait_ge(part_rest[s], n * 2 + 1)
                    act.activation(parts[s][:, 1, :], zd[s][:, CH:CH + KQ], ACT.Copy).then_inc(part_cast[s], 1)

            def exp_tile(i, uu, kt, j):
                act.wait_ge(scores_ready, i * (32 * UB) + (32 * uu + 4 * kt + j + 1))
                if j == 0 and (not isinstance(i, int) or 8 * (UB * i + uu) + kt >= 2):
                    act.wait_ge(probs_used, i * (8 * UB) + (8 * uu + kt - 1))
                act.activation(probs[:, kt % 2, j, :], ps_score[j % 2][:, :], ACT.Exp,
                               scale=1.0 / HD ** 0.5).then_inc(probs_ready, 1)

            def copy_out(i, uu):
                act.wait_ge(probs_used, i * (8 * UB) + 8 * (uu + 1))
                if not isinstance(i, int) or UB * i + uu >= 2:
                    act.wait_ge(o_turned, i * UB + (uu - 1))
                act.activation(o_sb[:, uu % 2, :], ps_out[uu % 2][:, :], ACT.Copy).then_inc(o_copied, 1)

            def body(i, plan, first=False):
                for slot in range(8 * UB):
                    uu, kt = slot // 8, slot % 8
                    exp_tile(i, uu, kt, 0)
                    exp_tile(i, uu, kt, 1)
                    if kt == 1 and not (first and uu == 0):
                        copy_out(i, uu - 1)
                    for item in plan.get(2 * slot - 1, []):
                        fill(item)
                    exp_tile(i, uu, kt, 2)
                    exp_tile(i, uu, kt, 3)
                    for item in plan.get(2 * slot, []):
                        fill(item)

            for k, item in enumerate(ALONE):
                fill(item)
                if item[0].n == 0 and item[1] == "FFa0" and item[0].slot == 0:
                    attn_weights()
            body(0, front_plan(0), first=True)
            body(1, front_plan(1))
            with act.Fori(2, 7) as i:
                body(i, back_plan(Chunk("back", 0, i - 2)))
            body(7, back_plan(Chunk("back", 0, 5)))
            copy_out(8, -1)
            for item in tail_steps():
                fill(item)

        @block.vector
        def _(dve):
            def ffn_weights():
                dve.wait_ge(ffn_hi, 4)
                dve.wait_ge(ffn_in, 5 * 16)
                dve.tensor_tensor(wr_hl[:, :, E:2 * E], wr_raw[:, :, :], wr_hl[:, :, 0:E].bitcast(F32),
                                  ALU.subtract).then_inc(ffn_lo, 1)
                dve.tensor_tensor(a_l[:, :, :], raw_a, a_h[:, :, :].bitcast(F32), ALU.subtract).then_inc(ffn_lo, 1)
                dve.tensor_scalar(bias_half[:, :], bias_half[:, :], 0.5, None, ALU.mult).then_inc(ffn_lo, 1)
                dve.tensor_tensor(wb_l[:, :, :], raw_wb, wb_h[:, :, :].bitcast(F32), ALU.subtract).then_inc(ffn_lo, 1)
                dve.tensor_tensor(b_l[:, :], raw_b, b_h[:, :].bitcast(F32), ALU.subtract).then_inc(ffn_lo, 1)

            def attn_scales():
                dve.wait_ge(attn_in, 11 * 16)
                dve.wait_ge(signs_ready, 1)
                dve.scalar_tensor_tensor(out=raw_o, in0=raw_o, scalar=-1.0, in1=raw_o, op0=ALU.mult,
                                         op1=ALU.max).then_inc(abs_ready, 1)
                dve.tensor_reduce(col_scale[:, 0:1], raw_vn, AX, ALU.add,
                                  apply_absolute_value=True).then_inc(scale_step, 1)
                dve.tensor_reduce(col_scale[:, 1:2], raw_kn, AX, ALU.add,
                                  apply_absolute_value=True).then_inc(scale_step, 1)
                dve.tensor_reduce(col_scale[:, 2:2 + DC], raw_qn, AX, ALU.add,
                                  apply_absolute_value=True).then_inc(scale_step, 1)
                dve.wait_ge(scale_step, 3)
                dve.tensor_scalar(col_scale[:, :], col_scale[:, :], 1.0 / D, 1e-8, ALU.mult,
                                  ALU.max).then_inc(scale_step, 1)
                dve.wait_ge(osum_ready, 1)
                dve.tensor_scalar(o_scale[:, :], ps_out[0][:, :], 1.0 / D, 1e-8, ALU.mult,
                                  ALU.max).then_inc(scale_step, 1)
                dve.wait_ge(scale_step, 4)
                dve.tensor_tensor(col_scale[:, :], col_scale[:, :], raw_scale[:, :], ALU.mult).then_inc(scale_step, 1)
                dve.wait_ge(scale_step, 5)
                dve.tensor_tensor(o_scale[:, :], o_scale[:, :], osc_row[:, :], ALU.mult).then_inc(scale_step, 1)

            def router(ch, step):
                s = ch.slot
                base = ch.ffn * R_STEPS
                st = router_step[s]
                if step == "R0":
                    bnk, reads = ch.bank("RU")
                    dve.wait_ge(filler_ready[s], ch.written("RU"))
                    dve.tensor_copy(logit[s][:, :, :], ps_fill[bnk][:, 0:CT * E].rearrange("p (t e) -> p t e", t=CT)
                                    ).then_inc(filler_read[bnk], 1)
                    dve_wait(dve, filler_read[bnk], reads + 1)
                    for t in range(CT):
                        dve.max(top[s][:, t, :], logit[s][:, t, :]).then_inc(st, 1)
                if step == "R1":
                    dve_wait(dve, st, base + 2)
                    for t in range(CT):
                        dve.max_index(top_i[s][:, t, :], top[s][:, t, :], logit[s][:, t, :]).then_inc(st, 1)
                    dve.wait_ge(st, base + 4)
                    dve.tensor_copy(top_e[s][:, :, :], top_i[s][:, :, 0:2]).then_inc(st, 1)
                    dve.tensor_tensor(gap[s][:, :], top[s][:, :, 1], top[s][:, :, 0], ALU.subtract).then_inc(st, 1)
                if step == "R3":
                    dve.wait_ge(e2_ready[s], ch.ffn + 1)
                    dve.tensor_scalar(den[s][:, :], e2[s][:, :], 1.0, None, ALU.add).then_inc(st, 1)
                    dve.wait_ge(st, base + 7)
                    dve.reciprocal(rden[s][:, :], den[s][:, :]).then_inc(st, 1)
                if step == "R4":
                    dve.wait_ge(st, base + 8)
                    dve.tensor_scalar(w12[s][:, :, 0], rden[s][:, :], 2.0, None, ALU.mult).then_inc(st, 1)
                    dve.wait_ge(st, base + 9)
                    dve.tensor_tensor(w12[s][:, :, 1], w12[s][:, :, 0], e2[s][:, :], ALU.mult).then_inc(st, 1)
                if step == "R5":
                    dve.wait_ge(st, base + 10)
                    for t in range(CT):
                        for k in range(2):
                            dve.tensor_scalar(w_tmp[s][:, 2 * t + k, :], expert_of[:, :], top_e[s][:, t, k:k + 1],
                                              w12[s][:, t, k:k + 1], ALU.is_equal, ALU.mult).then_inc(st, 1)
                    dve.wait_ge(st, base + 14)
                    tmp = w_tmp[s][:, :, :].rearrange("p (t k) n -> p t k n", k=2)
                    dve.tensor_tensor(w_rep[s][:, :, :], tmp[:, :, 0, :], tmp[:, :, 1, :],
                                      ALU.add).then_inc(w_rep_ready[s], 1)

            def guard(ch, step):
                s, k = ch.slot, int(step[1])
                cols = slice(512 * k, 512 * k + 512)
                g = ch.guard0 + 3 * k
                mask = zneg[s][:, cols].bitcast(I32)
                if step[0] == "C" and ch.alone:
                    bnk, reads = ch.bank((("VK", "Q0", "Q1") if ch.front else ("Oa", "Ob"))[k])
                    dve.wait_ge(filler_read[bnk], reads + 1)
                    dve.tensor_scalar(zd[s][:, cols], z[s][:, cols], 0.0, BIG, ALU.max, ALU.min).then_inc(clamped[s], 1)
                    dve.tensor_scalar(zneg[s][:, cols], z[s][:, cols], 0.0, -BIG, ALU.min,
                                      ALU.max).then_inc(clamped[s], 1)
                if step[0] == "G":
                    dve.wait_ge(clamped[s], ch.clamp0 + 2 * (k + 1))
                    dve.tensor_tensor(zd[s][:, cols], zd[s][:, cols], zneg[s][:, cols],
                                      ALU.add).then_inc(guard_step[s], 1)
                    dve.wait_ge(guard_step[s], g + 1)
                    dve.tensor_scalar(mask, z[s][:, cols].bitcast(I32), INF_BITS, INF_BITS, ALU.bitwise_and,
                                      ALU.bitwise_xor).then_inc(guard_step[s], 1)
                if step[0] == "P":
                    dve_wait(dve, guard_step[s], g + 2)
                    dve.copy_predicated(zd[s][:, cols], mask, z[s][:, cols]).then_inc(guard_step[s], 1)

            def fill(item):
                ch, pos = item
                s, n = ch.slot, ch.n
                stage, piece, final = stage_of(pos)
                if not final:
                    return
                if stage in ch.uses:
                    bnk, reads = ch.bank(stage)
                    ps = ps_fill[bnk]
                if pos == "LN1a":
                    if ch.front:
                        dve.wait_ge(chunk_loaded[s], ch.load)
                    else:
                        dve.wait_ge(residual[s], n * 2 + 2)
                if pos == "LN2a":
                    dve.wait_ge(filler_read[ch.bank("FFb")[0]], ch.bank("FFb")[1] + 1)
                L = ch.ln(1 if pos.startswith("LN2") else 0)
                if pos in ("LN1a", "LN2a"):
                    dve.bn_stats(stats[s][:, 0, :], xc[s][:, 0, :]).then_inc(stats_ready[s], 1)
                if pos in ("LN1b", "LN2b"):
                    dve.bn_stats(stats[s][:, 1, :], xc[s][:, 1, :]).then_inc(stats_ready[s], 1)
                    dve_wait(dve, stats_ready[s], L * 4 + 2)
                    for t in range(CT):
                        dve.bn_aggr(meanvar[s][:, t, :], stats[s][:, t, :]).then_inc(stats_ready[s], 1)
                if pos in ("LN1c", "LN2c"):
                    dve.wait_ge(stats_ready[s], L * 4 + 4)
                    dve.wait_ge(rstd_ready[s], L * 2 + 2)
                    for t in range(CT):
                        dve.tensor_scalar(xn[s][:, t, :], xc[s][:, t, :], meanvar[s][:, t, 0:1], rstd[s][:, t:t + 1],
                                          ALU.subtract, ALU.mult).then_inc(xn_ready[s], 1)
                if pos == "WR" and ch.alone:
                    dve.wait_ge(xn_ready[s], L * 2 + 2)
                    if n == 0:
                        dve.wait_ge(ffn_lo, 3)
                    for t in range(CT):
                        dve.tensor_tensor(xc[s][:, t, :], xc[s][:, t, :], bias_half[:, :],
                                          ALU.add).then_inc(bias_added[s], 1)
                if pos in ("T0al", "T0bl", "T1al", "T1bl", "T2al", "T2bl"):
                    stage = pos[:3]
                    bnk = ch.bank(stage)[0]
                    t = 0 if stage.endswith("a") else 1
                    dve.wait_ge(xt_h_ready[s], ch.t0 + ch.tn(stage) + 1)
                    dve.tensor_tensor(xt_l[s][:, :, t * P:(t + 1) * P],
                                      ps_fill[bnk][:, :].rearrange("p (c n) -> p c n", c=DC),
                                      xt_h[s][:, :, t * P:(t + 1) * P].bitcast(F32),
                                      ALU.subtract).then_inc(filler_read[bnk], 1)
                if pos[0] == "R" and pos[1] in "0123456789":
                    router(ch, pos)
                if pos[0] in "CGP":
                    guard(ch, pos)
                kq = zd[s][:, CH:CH + KQ]
                if pos == "S1" and ch.alone:
                    dve.wait_ge(part_cast[s], n * 2 + 1)
                    dve.tensor_tensor(kq, kq, parts[s][:, 0, :], ALU.subtract).then_inc(part_rest[s], 1)
                if pos == "S3" and ch.alone:
                    dve.wait_ge(part_cast[s], n * 2 + 2)
                    dve.wait_ge(part_rest[s], n * 2 + 1)
                    dve.tensor_tensor(parts[s][:, 2, :], kq, parts[s][:, 1, :], ALU.subtract).then_inc(part_rest[s], 1)
                if pos == "ADD" and ch.alone:
                    dve.wait_ge(guard_step[s], ch.guard0 + 6)
                    for t in range(CT):
                        dve.tensor_tensor(xc[s][:, t, :], xc[s][:, t, :], zd[s][:, 512 * t:512 * t + 512],
                                          ALU.add).then_inc(residual[s], 1)
                if pos == "WR":
                    dve.wait_ge(filler_ready[s], ch.written(pos))
                    dve.wait_ge(filler_read[ch.bank("HT")[0]], ch.bank("HT")[1] + 1)
                    dve.tensor_tensor(hT[s][:, :], ps[:, 0:CH], hT[s][:, :], ALU.mult).then_inc(filler_read[bnk], 1)
                if pos == "WL":
                    dve.wait_ge(hT_h_ready[s], ch.ffn + 1)
                    dve.tensor_tensor(hT_l[s][:, :], hT[s][:, :], hT_h[s][:, :].bitcast(F32),
                                      ALU.subtract).then_inc(hT_l_ready[s], 1)
                if stage in ("FFa", "FFb"):
                    t = 0 if stage == "FFa" else 1
                    dve.wait_ge(filler_ready[s], ch.written(stage))
                    dve.wait_ge(bias_added[s], ch.ffn * 2 + (t + 1))
                    dve.scalar_tensor_tensor(out=xc[s][:, t, :], in0=ps[:, :], scalar=0.5, in1=xc[s][:, t, :],
                                             op0=ALU.mult, op1=ALU.add).then_inc(filler_read[bnk], 1)
                if stage in ("Oa", "Ob"):
                    t = 0 if stage == "Oa" else 1
                    dve.wait_ge(filler_ready[s], ch.written(stage))
                    dve.tensor_tensor(z[s][:, 512 * t:512 * t + 512], ps[:, :], o_scale[:, :],
                                      ALU.mult).then_inc(filler_read[bnk], 1)

            def reduce_tile(i, uu, pos, t):
                use = max_use(i, uu, pos)
                b = (1 + uu + pos) % 2
                dve.wait_ge(max_scores, use + 1)
                if t == 0 and (not isinstance(i, int) or UB * i + uu >= 0):
                    dve.wait_ge(neg_max_ready, i * UB + (uu + 1))
                dve.tensor_reduce(neg_max_parts[:, uu % 2, t // 2, t % 2:t % 2 + 1], ps_max[b][:, :], AX, ALU.max,
                                  negate=True).then_inc(max_read, 1)

            def combine(i, uu, use):
                dve.wait_ge(max_read, use + 1)
                if not isinstance(i, int) or UB * i + uu >= 2:
                    dve.wait_ge(shift_parts, i * (4 * UB) + 4 * (uu - 1))
                dve.tensor_tensor(neg_max[:, uu % 2, :], neg_max_parts[:, uu % 2, :, 0], neg_max_parts[:, uu % 2, :, 1],
                                  ALU.min).then_inc(neg_max_ready, 1)

            def copy_rows(i, uu, use, b):
                dve.wait_ge(max_scores, use + 1)
                if not isinstance(i, int) or UB * i + uu >= 2:
                    dve.wait_ge(rows_loaded[(uu - 2) % UB], i * 48 + 48 * ((uu - 2) // UB + 1))
                n = PARTS * REP * QT
                dve.tensor_copy(shift_rows[0:n, uu % 2, :], ps_max[b][0:n, 0:P // 2].bitcast(BF16)
                                ).then_inc(max_read, 1)

            def normalise(i, uu):
                k = uu % 2
                o = ps_out[k][:, :].rearrange("p (q j n) -> p q j n", q=QT, j=REP)
                dve.wait_ge(o_turned, i * UB + (uu + 1))
                dve.reciprocal(recip[:, k, :, :], o[:, :, :, HD]).then_inc(recip_ready, 1)
                dve.wait_ge(recip_ready, i * UB + (uu + 1))
                if not isinstance(i, int) or UB * i + uu >= 2:
                    dve.wait_ge(att_stored[k], i * 32 + 16 * (uu // 2))
                dve.tensor_tensor(att[:, k, :, :].rearrange("p q (j d) -> p q j d", j=REP), o[:, :, :, 0:HD],
                                  recip[:, k, :, :].unsqueeze(3).broadcast_to([P, QT, REP, HD]),
                                  ALU.mult).then_inc(att_ready, 1)

            def body(i, plan, first=False, last=False):
                for slot in range(8 * UB):
                    uu, kt = slot // 8, slot % 8
                    has_max = not (last and uu >= 2)
                    tiles = max_tiles(kt) if has_max else []
                    if kt == 1 and not (last and uu == 3):
                        copy_rows(i, uu + 1, shift_use(i, uu, last), (1 + uu + (SHIFT_POS if has_max else 0)) % 2)
                    for pos, t in tiles[:2]:
                        reduce_tile(i, uu, pos, t)
                    for item in plan.get(2 * slot - 1, []):
                        fill(item)
                    if kt == 3 and not (first and uu == 0):
                        normalise(i, uu - 1)
                    for pos, t in tiles[2:]:
                        reduce_tile(i, uu, pos, t)
                    for item in plan.get(2 * slot, []):
                        fill(item)
                    if kt == 7 and has_max:
                        combine(i, uu + 2, max_use(i, uu, 32))

            for k, item in enumerate(ALONE):
                for use, v, t in start_uses(k):
                    if t is None:
                        copy_rows(0, 0, use, use % 2)
                    else:
                        dve.wait_ge(max_scores, use + 1)
                        dve.tensor_reduce(neg_max_parts[:, v, t // 2, t % 2:t % 2 + 1], ps_max[use % 2][:, :], AX,
                                          ALU.max, negate=True).then_inc(max_read, 1)
                    if use == 31:
                        combine(0, 0, 31)
                fill(item)
                if item[0].n == 0 and item[0].slot == 1 and item[1] == "LN1c":
                    ffn_weights()
                if item[0].n == 0 and item[0].slot == 1 and item[1] == "FFa3":
                    attn_scales()
            combine(0, 1, 64)
            body(0, front_plan(0), first=True)
            body(1, front_plan(1))
            with dve.Fori(2, 7) as i:
                body(i, back_plan(Chunk("back", 0, i - 2)))
            body(7, back_plan(Chunk("back", 0, 5)), last=True)
            normalise(8, -1)
            for item in tail_steps():
                fill(item)

        @block.tensor
        def _(pe):
            pe.wait_ge(const_ready, 12)

            def sum_o():
                pe.wait_ge(abs_ready, 1)
                for c in range(DC):
                    last = pe.matmul(ps_out[0][:, :], ones[:, :], raw_o[:, c, :], start=(c == 0), stop=(c == DC - 1))
                last.then_inc(osum_ready, 1)

            def fill(item):
                ch, pos = item
                s = ch.slot
                step, (pos, piece, final) = pos, stage_of(pos)
                if pos not in ch.uses:
                    return
                bnk, reads = ch.bank(pos)
                ps = ps_fill[bnk]
                if piece == 0 and positive(reads):
                    pe.wait_ge(filler_read[bnk], reads)

                def in_sbuf(stage):
                    other, before = ch.bank(stage)
                    if other != bnk:
                        pe.wait_ge(filler_read[other], before + 1)

                t = 1 if pos.endswith("b") else 0
                tok = slice(t * P, (t + 1) * P)
                if pos in ("T0a", "T0b", "T1a", "T1b", "T2a", "T2b"):
                    if pos.startswith("T0"):
                        pe.wait_ge(chunk_loaded[s], ch.load)
                    else:
                        which = 1 if pos.startswith("T2") else 0
                        pe.wait_ge(xn_ready[s], ch.ln(which) * 2 + (t + 1))
                    for c in range(DC):
                        last = pe.transpose(ps[:, c * P:(c + 1) * P], xn[s][:, t, c * P:(c + 1) * P], ident[:, :])
                if pos == "RT":
                    in_sbuf("T1b")
                    if ch.alone and ch.front and ch.n == 0:
                        pe.wait_ge(ffn_lo, 2)
                    for c in range(DC):
                        for x_part in (xt_h, xt_l):
                            last = pe.matmul(ps[0:2 * E, 0:CH], wr_hl[:, c, :], x_part[s][:, c, :],
                                             start=(c == 0 and x_part is xt_h), stop=(c == DC - 1 and x_part is xt_l))
                if pos == "HT":
                    pairs = ((a_h, xt_h), (a_h, xt_l), (a_l, xt_h))
                    for c in (2 * piece, 2 * piece + 1):
                        for k, (w, x_part) in enumerate(pairs):
                            last = pe.matmul(ps[:, 0:CH], w[:, c, :], x_part[s][:, c, :],
                                             start=(c == 0 and k == 0), stop=(c == DC - 1 and k == 2))
                if pos == "RU":
                    in_sbuf("RT")
                    for u in range(CT):
                        last = pe.matmul(ps[:, u * E:(u + 1) * E], logits_t[s][:, u * P:(u + 1) * P],
                                         hi_plus_lo[:, :], start=True, stop=True)
                if pos == "WR":
                    pe.wait_ge(w_rep_ready[s], ch.ffn + 1)
                    for u in range(CT):
                        last = pe.transpose(ps[:, u * P:(u + 1) * P], w_rep[s][:, u, :], ident[:, :])
                if pos in ("FFa", "FFb"):
                    if ch.alone and ch.front and ch.n == 0 and piece == 0:
                        pe.wait_ge(ffn_lo, 5)
                    c = piece
                    for k, (x_part, w) in enumerate(((xt_h, wb_h), (xt_h, wb_l), (xt_l, wb_h))):
                        pe.matmul(ps[:, :], x_part[s][:, c, tok], w[:, c, :], start=(c == 0 and k == 0), stop=False)
                    if final:
                        pe.wait_ge(hT_l_ready[s], ch.ffn + 1)
                        for k, (h_part, w) in enumerate(((hT_h, b_h), (hT_h, b_l), (hT_l, b_h))):
                            last = pe.matmul(ps[:, :], h_part[s][:, tok], w[:, :], start=False, stop=(k == 2))
                if pos == "VK":
                    if piece == 0:
                        in_sbuf("T2b")
                        if ch.alone and ch.n == 0:
                            pe.wait_ge(signs_ready, 4)
                    w = (sv, sk)[piece]
                    for c in range(DC):
                        for x_part in (xt_h, xt_l):
                            last = pe.matmul(ps[:, piece * CH:(piece + 1) * CH], w[:, c, :], x_part[s][:, c, :],
                                             start=(c == 0 and x_part is xt_h), stop=(c == DC - 1 and x_part is xt_l))
                if pos in ("Q0", "Q1"):
                    m = int(pos[1]) * 2 + piece
                    for c in range(DC):
                        for x_part in (xt_h, xt_l):
                            last = pe.matmul(ps[:, piece * CH:(piece + 1) * CH], sq[:, c, m * P:(m + 1) * P],
                                             x_part[s][:, c, :], start=(c == 0 and x_part is xt_h),
                                             stop=(c == DC - 1 and x_part is xt_l))
                if pos == "VT":
                    pe.wait_ge(guard_step[s], ch.guard0 + 3)
                    for u in range(CT):
                        last = pe.transpose(ps[:, u * P:(u + 1) * P], zd[s][:, u * P:(u + 1) * P], ident[:, :])
                if pos in ("Oa", "Ob"):
                    if piece == 0:
                        in_sbuf("T0" + pos[-1])
                    for c in (2 * piece, 2 * piece + 1):
                        for x_part in (xt_h, xt_l):
                            last = pe.matmul(ps[:, :], x_part[s][:, c, tok], so[:, c, :],
                                             start=(c == 0 and x_part is xt_h), stop=(c == DC - 1 and x_part is xt_l))
                if final:
                    last.then_inc(filler_ready[s], 1)

            def max_matmul(use, bnk, r, t):
                j, q, half = t // (2 * QT), t // 2 % QT, t % 2
                if not isinstance(use, int) or use >= 2:
                    pe.wait_ge(max_read, use - 1)
                pe.matmul(ps_max[bnk][:, :], qst[0:SR, r, j, q * P:(q + 1) * P], kst[0:SR, r, half * 512:half * 512 + 512],
                          start=True, stop=True).then_inc(max_scores, 1)

            def shift_transpose(i, uu, use, bnk):
                pe.wait_ge(shift_parts, i * (4 * UB) + 4 * (uu + 1))
                pe.wait_ge(max_read, use - 1)
                pe.transpose(ps_max[bnk][:, 0:P // 2].bitcast(BF16), shift[:, uu % 2, :], identb[:, :]
                             ).then_inc(max_scores, 1)

            def score(i, uu, kt, j):
                if not isinstance(i, int) or 32 * (UB * i + uu) + 4 * kt + j >= 2:
                    pe.wait_ge(probs_ready, i * (32 * UB) + (32 * uu + 4 * kt + j - 1))
                pe.matmul(ps_score[j % 2][:, :], kst[0:SR + PARTS, uu, kt * P:(kt + 1) * P],
                          qst[0:SR + PARTS, uu, j, :], start=True, stop=True).then_inc(scores_ready, 1)

            def times_v(i, uu, kt):
                k = uu % 2
                pe.wait_ge(probs_ready, i * (32 * UB) + (32 * uu + 4 * kt + 4))
                if kt == 0:
                    pe.wait_ge(v_ready, i * UB + (uu + 1))
                    if not isinstance(i, int) or UB * i + uu >= 2:
                        pe.wait_ge(att_ready, i * UB + (uu - 1))
                for j in range(REP):
                    last = pe.matmul(ps_out[k][32 * j:32 * j + 32, :], v_ring[:, k, kt, :], probs[:, kt % 2, j, :],
                                     start=(kt == 0), stop=(kt == KT - 1))
                last.then_inc(probs_used, 1)

            def turn_out(i, uu):
                pe.wait_ge(o_copied, i * UB + (uu + 1))
                for q in range(QT):
                    last = pe.transpose(ps_out[uu % 2][:, q * P:(q + 1) * P], o_sb[:, uu % 2, q * P:(q + 1) * P],
                                        ident[:, :])
                last.then_inc(o_turned, 1)

            def body(i, plan, first=False, last=False):
                for slot in range(8 * UB):
                    uu, kt = slot // 8, slot % 8
                    has_max = not (last and uu >= 2)
                    if kt == 0 and has_max:
                        pe.wait_ge(qk_loaded[(uu + 2) % UB], i * 192 + 192 * ((uu + 2) // UB + 1))
                    if kt == 0:
                        pe.wait_ge(rows_loaded[uu], i * 48 + 48)
                    if kt == 1 and not (last and uu == 3):
                        shift_transpose(i, uu + 1, shift_use(i, uu, last), (1 + uu + (SHIFT_POS if has_max else 0)) % 2)
                    tiles = [(max_use(i, uu, pos), (1 + uu + pos) % 2, (uu + 2) % UB, t) for pos, t in max_tiles(kt)] if has_max else []
                    if tiles:
                        max_matmul(*tiles[0])
                    score(i, uu, kt, 0)
                    score(i, uu, kt, 1)
                    if tiles:
                        max_matmul(*tiles[1])
                    if not (first and slot == 0):
                        times_v(i, uu - (kt == 0), (kt - 1) % KT)
                    if kt == 2 and not (first and uu == 0):
                        turn_out(i, uu - 1)
                    if tiles:
                        max_matmul(*tiles[2])
                    score(i, uu, kt, 2)
                    for item in plan.get(2 * slot, []):
                        fill(item)
                    score(i, uu, kt, 3)
                    if tiles:
                        max_matmul(*tiles[3])
                    for item in plan.get(2 * slot + 1, []):
                        fill(item)

            for k, item in enumerate(ALONE):
                for use, v, t in start_uses(k):
                    if t is None:
                        shift_transpose(0, 0, use, use % 2)
                    else:
                        if t == 0:
                            pe.wait_ge(qk_loaded[v], 192)
                        max_matmul(use, use % 2, v, t)
                fill(item)
                if item[0].n == 0 and item[0].slot == 1 and item[1] == "FFa3":
                    sum_o()
            body(0, front_plan(0), first=True)
            body(1, front_plan(1))
            with pe.Fori(2, 7) as i:
                body(i, back_plan(Chunk("back", 0, i - 2)))
            body(7, back_plan(Chunk("back", 0, 5)), last=True)
            times_v(8, -1, KT - 1)
            turn_out(8, -1)
            for item in tail_steps():
                fill(item)


def kernel(**inputs):
    import numpy as np
    from concourse import bacc
    from concourse.bass_utils import run_bass_kernel_spmd

    a = {k.replace("L0_attn_", "").replace("L0_ffn_", ""): np.asarray(v) for k, v in inputs.items()}
    cols = lambda v: np.ascontiguousarray(v.reshape(-1, P).T)
    laid = {
        "x": a["hidden_states"].reshape(T, D),
        "wbT": a["W_base"].T, "b": a["b_base"], "wrT": a["W_router"].T,
        "aT": a["lora_A"].reshape(E * R, D).T,
        "bT": a["lora_B"].transpose(0, 2, 1).reshape(E * R, D),
        "qN": a["q_weight"], "kN": a["k_weight"], "vN": a["v_weight"],
        "qT": a["q_weight"].T, "kT": a["k_weight"].T, "vT": a["v_weight"].T, "oT": a["o_weight"].T,
        "qs": cols(a["q_scale"]), "ks": cols(a["k_scale"]), "vs": cols(a["v_scale"]), "osc": a["o_scale"],
    }
    nc = bacc.Bacc("TRN2", target_bir_lowering=False, num_devices=1)
    arrays, args = {}, []
    for name, v in laid.items():
        arrays[name] = np.ascontiguousarray(v)
        args.append(nc.dram_tensor(name, v.shape, mybir.dt.from_np(v.dtype), kind="ExternalInput").ap())
    args.append(nc.dram_tensor("out", (T, D), F32, kind="ExternalOutput").ap())
    macaron(nc, *args)
    r = run_bass_kernel_spmd(nc, [arrays], core_ids=[0])
    return r.results[0]["out"].reshape(B, S, D)
```

```python
from contextlib import ExitStack

import concourse.bass as bass
from concourse import mybir

F32 = mybir.dt.float32
F32R = mybir.dt.float32r
BF16 = mybir.dt.bfloat16
I32 = mybir.dt.int32
U32 = mybir.dt.uint32
ALU = mybir.AluOpType
ACT = mybir.ActivationFunctionType
AX = mybir.AxisListType.X

P = 128
B, S, D = 2, 1024, 512
T = B * S
H, KV, HD = 32, 8, 16
REP = H // KV
E, R = 8, 16
DC = D // P
CH = 256
CT = CH // P
NCH = T // CH
BLK = 512
QT = BLK // P
KT = S // P
NU = (T // BLK) * KV
UB = 4
PARTS = 3
PAIRS = 6
SR = PAIRS * HD
Q_PARTS = (0, 0, 0, 1, 1, 2)
K_PARTS = (0, 1, 2, 0, 1, 0)
EPS = 1e-5
BIG = 1e6
INF_BITS = 0x7F800000
KQ = CH + DC * CH
ZW = 3 * 512

FRONT = [s.split() for s in (
    "LN1a", "LN1b", "", "LN1c", "LN1d", "T1a", "T1al", "T1b", "T1bl", "", "RT", "", "RU",
    "R0", "R1", "R2 HT0", "R3 R4 HT1", "R5", "", "WR", "", "WH FFa0", "WL FFa1", "FFa2", "FFa3", "",
    "FFb0", "FFb1", "FFb2", "FFb3", "",
    "LN2a", "LN2b", "", "LN2c", "LN2d", "T2a", "T2al", "", "T2b", "T2bl", "",
    "VK0", "VK1", "C0", "Q00", "Q01", "G0 C1", "Q10 P0", "Q11", "G1 C2", "VT P1", "", "G2", "P2",
    "S0", "S1", "", "S2", "S3", "", "ST", "", "")]
BACK = [s.split() for s in (
    12 * [""] + ["T0a", "T0al", "", "T0b", "T0bl", "", "Oa0", "Oa1", "C0", "Ob0", "Ob1", "", "G0 C1", "P0", "", "G1", "P1",
    "ADD", "", "LN1a", "LN1b", "", "LN1c", "LN1d", "T1a", "T1al", "", "T1b", "T1bl", "", "RT", "", "RU",
    "R0", "R1", "R2 HT0", "R3 R4 HT1", "R5", "", "", "WR", "", "WH FFa0", "WL FFa1", "FFa2", "FFa3", "",
    "FFb0", "FFb1", "FFb2", "FFb3"])]
F_USES = ["T1a", "T1b", "RT", "RU", "HT", "WR", "FFa", "FFb", "T2a", "T2b", "VK", "Q0", "Q1", "VT"]
B_USES = ["T0a", "T0b", "Oa", "Ob", "T1a", "T1b", "RT", "RU", "HT", "WR", "FFa", "FFb"]
PIECES = {"HT": 2, "FFa": DC, "FFb": DC, "VK": 2, "Q0": 2, "Q1": 2, "Oa": 2, "Ob": 2}
NF, NB = len(F_USES), len(B_USES)
FRONT_PAIRS = NCH // 2
ALONE_PAIRS = FRONT_PAIRS - 1
PAIR_PERIOD = 47
SLOT_LAG = 9
TAIL_LAG = 7
START_DELAY = 32
FRONT_ON_DVE = ("clamp", "sum")
START_ON_DVE = ()
TAIL_ON_DVE = ("clamp", "sum", "bias", "add")
LOOP_BACKS = NCH - 2
WAIT_PADS = 256
R_STEPS = 14


def stage_of(step):
    for stage, pieces in PIECES.items():
        if step[:-1] == stage:
            return stage, int(step[-1]), int(step[-1]) == pieces - 1
    return step, 0, True


class Chunk:

    def __init__(self, kind, slot, n, tail=False):
        self.kind, self.slot, self.n, self.tail = kind, slot, n, tail
        self.front = kind == "front"
        self.alone = tail or (self.front and isinstance(n, int) and n < ALONE_PAIRS)
        self.uses = F_USES if self.front else B_USES
        self.ffn = n if self.front else FRONT_PAIRS + n
        self.t0 = n * 4 if self.front else 4 * FRONT_PAIRS + n * 4
        self.guard0 = n * 6 if self.front else 6 * FRONT_PAIRS + n * 4
        self.clamp0 = n * 6 if self.front else 6 * FRONT_PAIRS + n * 4
        self.sum0 = n * 3 if self.front else 3 * FRONT_PAIRS + n * 2
        self.load = (n + 1) * 16 if self.front else 16 * FRONT_PAIRS + n * 48 + (32 if tail else 48)
        self.mb0 = n * NF if self.front else NF * FRONT_PAIRS + n * NB

    def on_dve(self, work):
        if not self.alone:
            return False
        return work in (TAIL_ON_DVE if self.tail else START_ON_DVE if self.n == ALONE_PAIRS - 1 else FRONT_ON_DVE)

    def ln(self, which):
        return self.n * 2 + which if self.front else 2 * FRONT_PAIRS + self.n

    def written(self, stage):
        return self.mb0 + (self.uses.index(stage) + 1)

    def bank(self, stage):
        s = self.uses.index(stage)
        if self.front and self.alone:
            return self.slot, self.n * NF + s
        before = ALONE_PAIRS * NF
        if self.front:
            return 0, before + self.slot * NF + s
        if not self.tail:
            return 0, before + 2 * NF + self.n * NB + s
        return self.slot, before + (1 - self.slot) * (2 * NF + LOOP_BACKS * NB) + s

    def tn(self, stage):
        return ["T1a", "T1b", "T2a", "T2b"].index(stage) if self.front else ["T0a", "T0b", "T1a", "T1b"].index(stage)


def positive(value):
    return not isinstance(value, int) or value > 0


def macaron(nc, x, wbT, b, wrT, aT, bT, qN, kN, vN, qT, kT, vT, oT, qs, ks, vs, osc, out):
    ctx = ExitStack()
    with ctx:
        def sb(name, shape, dt):
            return ctx.enter_context(nc.sbuf_tensor(name, shape, dt))

        def sem(name):
            return ctx.enter_context(nc.semaphore(name))

        x1_dram = nc.dram_tensor("x1_dram", [T, D], F32, kind="Internal").ap()
        q_dram = nc.dram_tensor("q_dram", [PARTS, D, T], BF16, kind="Internal").ap()
        k_dram = nc.dram_tensor("k_dram", [PARTS, P, T], BF16, kind="Internal").ap()
        att_dram = nc.dram_tensor("att_dram", [T // P, KV, P, REP * HD], F32, kind="Internal").ap()

        ident = sb("ident", [P, P], F32)
        identb = sb("identb", [P, P], BF16)
        ones = sb("ones", [P, P], F32)
        hi_plus_lo = sb("hi_plus_lo", [2 * E, E], F32)
        expert_of = sb("expert_of", [P, E], F32)
        expert_i = sb("expert_i", [P, E], I32)
        mhalf = sb("mhalf", [P, CT], F32)
        wb_h, wb_l = sb("wb_h", [P, DC, D], F32R), sb("wb_l", [P, DC, D], F32R)
        wr_hl = sb("wr_hl", [P, DC, 2 * E], F32R)
        a_h, a_l = sb("a_h", [P, DC, P], F32R), sb("a_l", [P, DC, P], F32R)
        b_h, b_l = sb("b_h", [P, D], F32R), sb("b_l", [P, D], F32R)
        sq, sk = sb("sq", [P, DC, D], F32R), sb("sk", [P, DC, P], F32R)
        sv, so = sb("sv", [P, DC, P], F32R), sb("so", [P, DC, D], F32R)
        bias_half = sb("bias_half", [P, D], F32)
        o_scale = sb("o_scale", [P, D], F32)
        osc_row = sb("osc_row", [P, D], F32)
        raw_scale = sb("raw_scale", [P, 2 + DC], F32)
        col_scale = sb("col_scale", [P, 2 + DC], F32)
        wr_raw = sb("wr_raw", [P, DC, E], F32)

        probs = sb("probs", [P, 2, REP, BLK], F32)
        qst = sb("qst", [P, UB, REP, BLK], BF16)
        kst = sb("kst", [P, UB, S], BF16)
        v_all = sb("v_all", [P, T // P, KV * HD], F32)
        v_ring = sb("v_ring", [P, 2, KT, 2 * HD], F32)
        neg_max_parts = sb("neg_max_parts", [P, 2, REP * QT, 2], F32)
        neg_max = sb("neg_max", [P, 2, REP * QT], F32)
        neg_max_rest = sb("neg_max_rest", [P, 2, REP * QT], F32)
        shift = sb("shift", [P, 2, P], BF16)
        wait_pad = sb("wait_pad", [1, WAIT_PADS], BF16)
        shift_rows = sb("shift_rows", [P, 2, P], BF16)
        o_sb = sb("o_sb", [P, 2, BLK], F32)
        recip = sb("recip", [P, 2, QT, REP], F32)
        att = sb("att", [P, 2, QT, REP * HD], F32)

        xc = [sb(f"xc{s}", [P, CT, D], F32) for s in range(2)]
        xn = [sb(f"xn{s}", [P, CT, D], F32) for s in range(2)]
        xt_h = [sb(f"xt_h{s}", [P, DC, CH], F32R) for s in range(2)]
        xt_l = [sb(f"xt_l{s}", [P, DC, CH], F32R) for s in range(2)]
        hT = [sb(f"hT{s}", [P, CH], F32) for s in range(2)]
        hT_h = [sb(f"hT_h{s}", [P, CH], F32R) for s in range(2)]
        hT_l = [sb(f"hT_l{s}", [P, CH], F32R) for s in range(2)]
        w_rep = [sb(f"w_rep{s}", [P, CT, P], F32) for s in range(2)]
        w_tmp = [sb(f"w_tmp{s}", [P, 2 * CT, E], F32) for s in range(2)]
        zm = [sb(f"zm{s}", [P, 2 * ZW], F32) for s in range(2)]
        zd = [sb(f"zd{s}", [P, ZW], F32) for s in range(2)]
        stats = [sb(f"stats{s}", [P, CT, 6], F32) for s in range(2)]
        meanvar = [sb(f"meanvar{s}", [P, CT, 2], F32) for s in range(2)]
        var_eps = [sb(f"var_eps{s}", [P, CT], F32) for s in range(2)]
        rstd = [sb(f"rstd{s}", [P, CT], F32) for s in range(2)]
        neg_mean = [sb(f"neg_mean{s}", [P, CT], F32) for s in range(2)]
        ln_shift = [sb(f"ln_shift{s}", [P, CT], F32) for s in range(2)]
        logits_t = [sb(f"logits_t{s}", [2 * E, CH], F32) for s in range(2)]
        logit = [sb(f"logit{s}", [P, CT, E], F32) for s in range(2)]
        top = [sb(f"top{s}", [P, CT, 8], F32) for s in range(2)]
        top_i = [sb(f"top_i{s}", [P, CT, 8], U32) for s in range(2)]
        top_e = [sb(f"top_e{s}", [P, CT, 2], F32) for s in range(2)]
        gap = [sb(f"gap{s}", [P, CT], F32) for s in range(2)]
        e2 = [sb(f"e2{s}", [P, CT], F32) for s in range(2)]
        den = [sb(f"den{s}", [P, CT], F32) for s in range(2)]
        rden = [sb(f"rden{s}", [P, CT], F32) for s in range(2)]
        w12 = [sb(f"w12{s}", [P, CT, 2], F32) for s in range(2)]

        z = [t[:, 0:ZW] for t in zm]
        zneg = [t[:, ZW:2 * ZW] for t in zm]
        parts = [t[:, 0:PARTS * KQ // 2].bitcast(BF16).rearrange("p (c n) -> p c n", c=PARTS) for t in zm]

        raw_wb, raw_q = probs[:, 0, :, :], probs[:, 1, :, :]
        raw_qn = zm[0][:, 0:DC * D].rearrange("p (c n) -> p c n", c=DC)
        raw_o = zm[1][:, 0:DC * D].rearrange("p (c n) -> p c n", c=DC)
        stage = [qst[:, r, :, :].rearrange("p a b -> p (a b)").bitcast(F32) for r in range(UB)]
        raw_k, raw_v = [stage[0][:, i * D:(i + 1) * D].rearrange("p (c n) -> p c n", c=DC) for i in range(2)]
        raw_a, raw_b = stage[1][:, 0:D].rearrange("p (c n) -> p c n", c=DC), stage[1][:, D:2 * D]
        raw_vn, raw_kn = stage[2][:, 0:D], stage[2][:, D:2 * D]

        def bank(name):
            return ctx.enter_context(nc.psum_tensor(name, [P, 512], F32))

        ps_max2 = [bank(f"ps_max{i}") for i in range(2)]
        ps_score = [bank(f"ps_score{i}") for i in range(2)]
        ps_out = [bank(f"ps_out{i}") for i in range(2)]
        ps_fill = [bank(f"ps_fill{i}") for i in range(2)]
        ps_max = ps_max2 + [ps_fill[1]]

        ffn_in = sem("ffn_in")
        attn_in = sem("attn_in")
        const_ready = sem("const_ready")
        ffn_hi = sem("ffn_hi")
        ffn_lo = sem("ffn_lo")
        signs_ready = sem("signs_ready")
        abs_ready = sem("abs_ready")
        osum_ready = sem("osum_ready")
        scale_step = sem("scale_step")
        qk_loaded = [sem(f"qk_loaded{r}") for r in range(UB)]
        rows_loaded = [sem(f"rows_loaded{r}") for r in range(UB)]
        max_scores = sem("max_scores")
        max_read = sem("max_read")
        neg_max_ready = sem("neg_max_ready")
        shift_parts = sem("shift_parts")
        scores_ready = sem("scores_ready")
        probs_ready = sem("probs_ready")
        probs_used = sem("probs_used")
        v_ready = sem("v_ready")
        o_copied = sem("o_copied")
        o_turned = sem("o_turned")
        recip_ready = sem("recip_ready")
        att_ready = sem("att_ready")
        att_stored = [sem(f"att_stored{i}") for i in range(2)]
        filler_ready = [sem(f"filler_ready{s}") for s in range(2)]
        filler_read = [sem(f"filler_read{i}") for i in range(2)]
        chunk_loaded = [sem(f"chunk_loaded{s}") for s in range(2)]
        x1_loaded = [sem(f"x1_loaded{s}") for s in range(2)]
        stats_ready = [sem(f"stats_ready{s}") for s in range(2)]
        rstd_ready = [sem(f"rstd_ready{s}") for s in range(2)]
        xn_ready = [sem(f"xn_ready{s}") for s in range(2)]
        bias_added = [sem(f"bias_added{s}") for s in range(2)]
        xt_h_ready = [sem(f"xt_h_ready{s}") for s in range(2)]
        router_step = [sem(f"router_step{s}") for s in range(2)]
        e2_ready = [sem(f"e2_ready{s}") for s in range(2)]
        w_rep_ready = [sem(f"w_rep_ready{s}") for s in range(2)]
        hT_h_ready = [sem(f"hT_h_ready{s}") for s in range(2)]
        hT_l_ready = [sem(f"hT_l_ready{s}") for s in range(2)]
        clamped = [sem(f"clamped{s}") for s in range(2)]
        clamp_sum = [sem(f"clamp_sum{s}") for s in range(2)]
        guard_step = [sem(f"guard_step{s}") for s in range(2)]
        part_cast = [sem(f"part_cast{s}") for s in range(2)]
        part_rest = [sem(f"part_rest{s}") for s in range(2)]
        parts_stored = [sem(f"parts_stored{s}") for s in range(2)]
        xc_stored = [sem(f"xc_stored{s}") for s in range(2)]
        residual = [sem(f"residual{s}") for s in range(2)]

        pad_columns = iter(range(1, WAIT_PADS))

        def pad():
            c = next(pad_columns)
            return wait_pad[0:1, c:c + 1]

        def dve_wait(dve, semaphore, value):
            if isinstance(value, int):
                dve.wait_ge(semaphore, value)
            else:
                dve.wait_ge(semaphore, value)
                dve.tensor_copy(pad(), wait_pad[0:1, 0:1])

        def gp_wait(gp, semaphore, value):
            if isinstance(value, int):
                gp.wait_ge(semaphore, value)
            else:
                gp.wait_ge(semaphore, value)
                gp.tensor_tensor(pad(), wait_pad[0:1, 0:1], wait_pad[0:1, 0:1], ALU.add)

        def max_use(i, uu, pos):
            return i * (33 * UB) + (65 + 33 * uu + pos)

        SHIFT_POS = 4
        START_USES = max_use(0, 0, 0)

        def body_bank(pos):
            return (START_USES + pos) % 3

        def max_tiles(kt):
            return [(t + (t >= SHIFT_POS), t) for t in range(4 * kt, 4 * kt + 4)]

        def shift_use(i, uu, last):
            return max_use(i, uu, 0 if last and uu >= 2 else SHIFT_POS)

        def start_uses(step):
            uses = [(t, 0, t) for t in range(32)]
            uses += [(max_use(0, -1, pos), 1, t) for pos, t in enumerate(range(SHIFT_POS))]
            uses += [(max_use(0, -1, SHIFT_POS), 0, None)]
            uses += [(max_use(0, -1, t + 1), 1, t) for t in range(SHIFT_POS, 32)]
            return [u for n, u in enumerate(uses) if START + n * START_PACE[0] // START_PACE[1] == step]

        def in_turns(steps, chunks, period):
            keyed = [(ch.n * period + k + SLOT_LAG * ch.slot, ch.slot, j, ch, step) for ch in chunks
                     for k, line in enumerate(steps) for j, step in enumerate(line)]
            return [(key, ch, step) for key, _, _, ch, step in sorted(keyed, key=lambda t: t[:3])]

        keyed = in_turns(FRONT, [Chunk("front", s, n) for n in range(ALONE_PAIRS) for s in range(2)], PAIR_PERIOD)
        ALONE = [(ch, step) for _, ch, step in keyed]
        BATCH0_STORED = max(k for k, (ch, step) in enumerate(ALONE) if ch.n == 1 and step == "ST") + 1
        START = BATCH0_STORED + START_DELAY
        START_PACE = (len(ALONE) - START, 65)

        def front_plan(slot):
            return {k: [(Chunk("front", slot, FRONT_PAIRS - 1), step) for step in line]
                    for k, line in enumerate(FRONT)}

        def back_plan(chunk):
            return {k: [(chunk, step) for step in line] for k, line in enumerate(BACK)}

        def tail_steps():
            chunks = [Chunk("back", 0, 6, tail=True), Chunk("back", 1, 0, tail=True)]
            keyed = [(k + TAIL_LAG * ch.slot, ch.slot, j, ch, step) for ch in chunks for k, line in enumerate(BACK)
                     for j, step in enumerate(line)]
            return [(ch, step) for _, _, _, ch, step in sorted(keyed, key=lambda t: t[:3])]

        block = ctx.enter_context(nc.Block())

        @block.sync
        def _(sp):
            def chunk_rows(dram, c):
                return dram[bass.ds(c * CH, CH), :].rearrange("(t p) d -> p t d", p=P)

            def load_front(ch):
                s, n = ch.slot, ch.n
                if n > 0:
                    sp.wait_ge(xc_stored[s], n * 16)
                    sp.wait_ge(xn_ready[s], n * (2 * 2))
                sp.dma_start(xc[s][:, :, :], chunk_rows(x, n * 2 + s)).then_inc(chunk_loaded[s], 16)

            def fill(item):
                ch, pos = item
                s, n = ch.slot, ch.n
                if ch.front and pos == "VK1" and n < FRONT_PAIRS - 1:
                    load_front(Chunk("front", s, n + 1))
                if ch.front and pos == "FFb3":
                    sp.wait_ge(filler_read[ch.bank("FFb")[0]], ch.bank("FFb")[1] + 1)
                    sp.dma_start(chunk_rows(x1_dram, n * 2 + s), xc[s][:, :, :]).then_inc(xc_stored[s], 16)
                if ch.front and pos == "ST":
                    c = n * 2 + s
                    sp.wait_ge(part_rest[s], n * 2 + 2)
                    for part in range(PARTS):
                        sp.dma_start(k_dram[part, :, bass.ds(c * CH, CH)],
                                     parts[s][:, part, 0:CH]).then_inc(parts_stored[s], 16)
                        sp.dma_start(q_dram[part, :, bass.ds(c * CH, CH)].rearrange("(m p) t -> p m t", p=P),
                                     parts[s][:, part, CH:KQ].rearrange("p (m t) -> p m t", t=CH)
                                     ).then_inc(parts_stored[s], 16)
                if not ch.front and pos == "FFb3":
                    a = n if not ch.tail else NCH - 2 + s
                    sp.wait_ge(filler_read[ch.bank("FFb")[0]], ch.bank("FFb")[1] + 1)
                    sp.dma_start(chunk_rows(out, a), xc[s][:, :, :]).then_inc(xc_stored[s], 16)

            def load_x1(ch, loaded):
                s, n = ch.slot, ch.n
                a = n if not ch.tail else NCH - 2 + s
                sp.wait_ge(xc_stored[s], n * 16 + 16 * FRONT_PAIRS)
                sp.dma_start(xc[s][:, :, :], chunk_rows(x1_dram, a)).then_inc(loaded, 16)

            def load_att(ch):
                s, n = ch.slot, ch.n
                a = n if not ch.tail else NCH - 2 + s
                for i in range(2):
                    sp.wait_ge(att_stored[i], (a // 2) * 64 + 64 - (16 if ch.tail and i == 1 else 0))
                heads = KV - 1 if ch.tail else KV
                for t in range(CT):
                    sp.dma_start(xn[s][:, t, 0:heads * REP * HD].rearrange("p (k d) -> p k d", k=heads),
                                 att_dram[bass.ds(a * 2 + t, 1), 0:heads, :, :].rearrange("o k p d -> p (o k) d")
                                 ).then_inc(chunk_loaded[s], 16)

            def load_qk(i, uu):
                r = uu % UB
                if not isinstance(i, int) or UB * i + uu >= UB:
                    sp.wait_ge(scores_ready, i * (32 * UB) + 32 * (uu - 3))
                j = i + uu // UB
                t0, o0, k0 = (j // 2) * BLK, (j % 2) * (UB * REP * HD) + r * REP * HD, (j // 4) * S
                for slot in range(PAIRS):
                    rows = slice(slot * HD, (slot + 1) * HD)
                    sp.dma_start(qst[rows, r, :, :],
                                 q_dram[Q_PARTS[slot], bass.ds(o0, REP * HD), bass.ds(t0, BLK)]
                                 .rearrange("(j d) t -> d j t", j=REP)).then_inc(qk_loaded[r], 16)
                    sp.dma_start(kst[rows, r, :],
                                 k_dram[K_PARTS[slot], bass.ds((j % 2) * (UB * HD) + r * HD, HD), bass.ds(k0, S)]
                                 ).then_inc(qk_loaded[r], 16)

            def load_rows(i, uu, use):
                r = uu % UB
                sp.wait_ge(max_read, use + 1)
                for part in range(PARTS):
                    sp.dma_start(qst[SR + part:SR + part + 1, r, :, :].rearrange("c j (q p) -> c (j q) p", p=P),
                                 shift_rows[REP * QT * part:REP * QT * (part + 1), uu % 2, :]
                                 ).then_inc(rows_loaded[r], 16)

            def store_att(i, uu):
                j = i + uu // UB
                sp.wait_ge(att_ready, i * UB + (uu + 1))
                sp.dma_start(att_dram[bass.ds((j // 2) * QT, QT), bass.ds((j % 2) * UB + uu % UB, 1), :, :]
                             .rearrange("q o p d -> p q (o d)"), att[:, uu % 2, :, :]).then_inc(att_stored[uu % 2], 16)

            def body(i, plan, load_next, first=False, last=False):
                for slot in range(8 * UB):
                    uu, kt = slot // 8, slot % 8
                    if kt == 0 and not (last and uu >= 1):
                        load_qk(i, uu + 3)
                    if kt == 2 and not (last and uu == 3):
                        load_rows(i, uu + 1, shift_use(i, uu, last))
                    if kt == 4 and not (first and uu == 0):
                        store_att(i, uu - 1)
                    if slot == 5 and load_next is not None:
                        load_x1(load_next, chunk_loaded[0])
                        load_att(load_next)
                    if last and slot == 8 * UB - 2:
                        sp.wait_ge(filler_ready[0], load_next.written("T1b"))
                        for ch in tail:
                            load_att(ch)
                        load_x1(tail[1], x1_loaded[1])
                    for half in (2 * slot - 2, 2 * slot - 1):
                        for item in plan.get(half, []):
                            fill(item)
                for item in plan.get(16 * UB - 2, []):
                    fill(item)

            tail = [Chunk("back", 0, 6, tail=True), Chunk("back", 1, 0, tail=True)]
            for s in range(2):
                load_front(Chunk("front", s, 0))
            for dst, src in (
                (bias_half[:, :], b.partition_broadcast(P)),
                (wr_raw[:, :, :], wrT.rearrange("(c p) n -> p c n", p=P)),
                (raw_a, aT.rearrange("(c p) n -> p c n", p=P)),
                (raw_wb, wbT.rearrange("(c p) n -> p c n", p=P)), (raw_b, bT),
            ):
                sp.dma_start(dst, src).then_inc(ffn_in, 16)
            for dst, src in (
                (osc_row[:, :], osc.partition_broadcast(P)),
                (raw_scale[:, 0:1], vs), (raw_scale[:, 1:2], ks), (raw_scale[:, 2:2 + DC], qs),
                (raw_k, kT.rearrange("(c p) n -> p c n", p=P)), (raw_v, vT.rearrange("(c p) n -> p c n", p=P)),
                (raw_kn, kN), (raw_vn, vN), (raw_q, qT.rearrange("(c p) n -> p c n", p=P)),
                (raw_qn, qN.rearrange("(c p) n -> p c n", p=P)), (raw_o, oT.rearrange("(c p) n -> p c n", p=P)),
            ):
                sp.dma_start(dst, src).then_inc(attn_in, 16)
            for k, item in enumerate(ALONE):
                if k == BATCH0_STORED:
                    for s in range(2):
                        sp.wait_ge(parts_stored[s], 16 * 2 * PARTS * 2)
                    sp.wait_ge(scale_step, 7)
                    sp.wait_ge(signs_ready, 4)
                    for v in range(3):
                        load_qk(0, v)
                fill(item)
                if [u for u in start_uses(k) if u[2] is None]:
                    load_rows(0, 0, max_use(0, -1, SHIFT_POS))
            body(0, front_plan(0), None, first=True)
            body(1, front_plan(1), None)
            for s in range(2):
                sp.wait_ge(parts_stored[s], 16 * 2 * PARTS * 4)
                sp.wait_ge(xc_stored[s], 16 * FRONT_PAIRS)
                sp.wait_ge(xn_ready[s], 4 * FRONT_PAIRS)
                sp.wait_ge(filler_ready[s], Chunk("front", s, FRONT_PAIRS - 1).written("T2b"))
            with sp.Fori(2, 7) as i:
                ch = Chunk("back", 0, i - 2)
                body(i, back_plan(ch), ch)
            ch = Chunk("back", 0, 5)
            body(7, back_plan(ch), ch, last=True)
            load_x1(tail[0], x1_loaded[0])
            for item in tail_steps():
                fill(item)
            sp.wait_ge(xc_stored[0], 16 * (FRONT_PAIRS + 7))
            sp.wait_ge(xc_stored[1], 16 * (FRONT_PAIRS + 1))
            for s in range(2):
                sp.wait_ge(att_stored[s], 16 * (NU // 2 - s))

        @block.gpsimd
        def _(gp):
            for n, (dst, value) in enumerate(((ident[:, :], 0.0), (ones[:, :], 1.0), (mhalf[:, :], -0.5),
                                              (v_ring[:, :, :, HD:2 * HD], 1.0), (kst[SR:P, :, :], 1.0),
                                              (shift[:, :, :], 0.0), (wait_pad[:, :], 0.0))):
                if n:
                    gp.wait_ge(const_ready, n)
                gp.memset(dst, value).then_inc(const_ready, 1)
            gp.wait_ge(const_ready, 7)
            gp.iota(expert_i[:, :], pattern=[[1, E]], base=0, channel_multiplier=0).then_inc(const_ready, 1)
            gp.wait_ge(const_ready, 8)
            gp.affine_select(out=ident[:, :], in_=ident[:, :], compare_op=ALU.not_equal, fill=1.0, base=0,
                             pattern=[[-1, P]], channel_multiplier=1).then_inc(const_ready, 1)
            gp.tensor_copy(expert_of[:, :], expert_i[:, :]).then_inc(const_ready, 1)
            gp.wait_ge(const_ready, 10)
            gp.tensor_copy(identb[:, :], ident[:, :]).then_inc(const_ready, 1)
            gp.tensor_tensor(hi_plus_lo[:, :], ident[0:2 * E, 0:E], ident[0:2 * E, E:2 * E],
                             ALU.add).then_inc(const_ready, 1)

            def norm(ch, which):
                s, L = ch.slot, ch.ln(which)
                gp_wait(gp, stats_ready[s], L * 4 + 4)
                gp.tensor_scalar(var_eps[s][:, :], meanvar[s][:, :, 1], EPS, None, ALU.add).then_inc(rstd_ready[s], 1)
                gp.tensor_scalar(neg_mean[s][:, :], meanvar[s][:, :, 0], -1.0, None, ALU.mult).then_inc(rstd_ready[s], 1)
                gp.wait_ge(rstd_ready[s], L * 4 + 1)
                gp.tensor_tensor(rstd[s][:, :], var_eps[s][:, :], mhalf[:, :], ALU.pow).then_inc(rstd_ready[s], 1)
                gp.wait_ge(rstd_ready[s], L * 4 + 3)
                gp.tensor_tensor(ln_shift[s][:, :], neg_mean[s][:, :], rstd[s][:, :], ALU.mult).then_inc(rstd_ready[s], 1)

            def add_bias(ch, which):
                s = ch.slot
                gp.wait_ge(xn_ready[s], ch.ln(which) * 2 + 2)
                if ch.alone and ch.front:
                    gp.wait_ge(ffn_lo, 3)
                for t in range(CT):
                    gp.tensor_tensor(xc[s][:, t, :], xc[s][:, t, :], bias_half[:, :], ALU.add).then_inc(bias_added[s], 1)

            def clamp(ch, stg, piece):
                s = ch.slot
                cols = slice(512 * piece, 512 * piece + 512)
                bnk, reads = ch.bank(stg)
                gp_wait(gp, filler_read[bnk], reads + 1)
                gp.tensor_scalar(zd[s][:, cols], z[s][:, cols], 0.0, BIG, ALU.max, ALU.min).then_inc(clamped[s], 1)
                gp.tensor_scalar(zneg[s][:, cols], z[s][:, cols], 0.0, -BIG, ALU.min, ALU.max).then_inc(clamped[s], 1)

            def clamped_sum(ch, piece):
                s = ch.slot
                cols = slice(512 * piece, 512 * piece + 512)
                gp.wait_ge(clamped[s], ch.clamp0 + (2 * piece + 2))
                gp.tensor_tensor(zd[s][:, cols], zd[s][:, cols], zneg[s][:, cols], ALU.add).then_inc(clamp_sum[s], 1)

            def fill(item):
                ch, pos = item
                s, n = ch.slot, ch.n
                if pos in ("LN1b", "LN2b"):
                    norm(ch, 0 if pos == "LN1b" else 1)
                if pos == "LN1d" and not ch.on_dve("bias"):
                    add_bias(ch, 0)
                if pos in ("C0", "C1", "C2") and not ch.on_dve("clamp"):
                    k = int(pos[1])
                    clamp(ch, (("VK", "Q0", "Q1") if ch.front else ("Oa", "Ob"))[k], k)
                    clamped_sum(ch, k)
                if pos in ("G0", "G1", "G2") and ch.on_dve("clamp") and not ch.on_dve("sum"):
                    clamped_sum(ch, int(pos[1]))
                if pos in ("S1", "S3") and not ch.on_dve("split"):
                    kq = zd[s][:, CH:CH + KQ]
                    k = 1 if pos == "S1" else 2
                    gp.wait_ge(part_cast[s], n * 2 + k)
                    if k == 1:
                        gp.tensor_tensor(kq, kq, parts[s][:, 0, :], ALU.subtract).then_inc(part_rest[s], 1)
                    else:
                        gp.wait_ge(part_rest[s], n * 2 + 1)
                        gp.tensor_tensor(parts[s][:, 2, :], kq, parts[s][:, 1, :], ALU.subtract).then_inc(part_rest[s], 1)
                if pos == "ADD" and not ch.on_dve("add"):
                    gp.wait_ge(guard_step[s], ch.guard0 + 4)
                    for t in range(CT):
                        gp.tensor_tensor(xc[s][:, t, :], xc[s][:, t, :], zd[s][:, 512 * t:512 * t + 512],
                                         ALU.add).then_inc(residual[s], 1)

            def split_shift(i, uu):
                k = uu % 2
                n = REP * QT
                v4 = i * (4 * UB) + 4 * uu
                gp_wait(gp, neg_max_ready, i * UB + (uu + 1))
                gp.tensor_copy(shift[:, k, 0:n], neg_max[:, k, :]).then_inc(shift_parts, 1)
                gp.wait_ge(shift_parts, v4 + 1)
                gp.tensor_tensor(neg_max_rest[:, k, :], neg_max[:, k, :], shift[:, k, 0:n],
                                 ALU.subtract).then_inc(shift_parts, 1)
                gp_wait(gp, shift_parts, v4 + 2)
                gp.tensor_copy(shift[:, k, n:2 * n], neg_max_rest[:, k, :]).then_inc(shift_parts, 1)
                gp.wait_ge(shift_parts, v4 + 3)
                gp.tensor_tensor(shift[:, k, 2 * n:3 * n], neg_max_rest[:, k, :], shift[:, k, n:2 * n],
                                 ALU.subtract).then_inc(shift_parts, 1)

            def load_v(i, uu):
                j = i + uu // UB
                if not isinstance(i, int) or UB * i + uu >= 2:
                    gp.wait_ge(probs_used, i * (8 * UB) + 8 * (uu - 1))
                gp.tensor_copy(v_ring[:, uu % 2, :, 0:HD],
                               v_all[:, bass.ds((j // 4) * KT, KT), bass.ds((j % 2) * (UB * HD) + (uu % UB) * HD, HD)]
                               ).then_inc(v_ready, 1)

            def body(i, plan, last=False):
                for slot in range(8 * UB):
                    uu, kt = slot // 8, slot % 8
                    if kt == 2 and not (last and uu == 3):
                        load_v(i, uu + 1)
                    for half in (2 * slot - 1, 2 * slot):
                        for item in plan.get(half, []):
                            fill(item)
                    if kt == 7 and not (last and uu >= 2):
                        split_shift(i, uu + 2)

            for k, item in enumerate(ALONE):
                if k == START:
                    for s in range(2):
                        gp.wait_ge(filler_read[s], 2 * NF)
                    load_v(0, 0)
                if any(use == 33 for use, _, _ in start_uses(k)):
                    split_shift(0, 0)
                fill(item)
            split_shift(0, 1)
            body(0, front_plan(0))
            body(1, front_plan(1))
            gp.wait_ge(filler_read[0], (ALONE_PAIRS + 2) * NF)
            with gp.Fori(2, 7) as i:
                body(i, back_plan(Chunk("back", 0, i - 2)))
            body(7, back_plan(Chunk("back", 0, 5)), last=True)
            for item in tail_steps():
                fill(item)

        @block.scalar
        def _(act):
            act.wait_ge(ffn_in, 5 * 16)
            act.activation(wr_hl[:, :, 0:E], wr_raw[:, :, :], ACT.Copy).then_inc(ffn_hi, 1)
            for dst, src in ((a_h, raw_a), (wb_h, raw_wb), (b_h, raw_b)):
                act.activation(dst[:], src, ACT.Copy).then_inc(ffn_hi, 1)

            def attn_weights():
                act.wait_ge(attn_in, 11 * 16)
                for dst, src in ((so, raw_o), (sk, raw_k), (sv, raw_v), (sq, raw_q)):
                    act.activation(dst[:, :, :], src, ACT.Sign).then_inc(signs_ready, 1)

            def fill(item):
                ch, pos = item
                s, n = ch.slot, ch.n
                pos, _, final = stage_of(pos)
                if not final:
                    return
                if pos in ch.uses:
                    bnk, reads = ch.bank(pos)
                    ps = ps_fill[bnk]
                if pos in ("LN1c", "LN1d", "LN2c", "LN2d"):
                    t = "cd".index(pos[3])
                    act.wait_ge(rstd_ready[s], ch.ln(int(pos[2]) - 1) * 4 + 4)
                    act.activation(xn[s][:, t, :], xc[s][:, t, :], ACT.Identity, bias=ln_shift[s][:, t:t + 1],
                                   scale=rstd[s][:, t:t + 1]).then_inc(xn_ready[s], 1)
                if pos in ("T0a", "T0b", "T1a", "T1b", "T2a", "T2b"):
                    t = 0 if pos.endswith("a") else 1
                    act.wait_ge(filler_ready[s], ch.written(pos))
                    act.activation(xt_h[s][:, :, t * P:(t + 1) * P], ps[:, :].rearrange("p (c n) -> p c n", c=DC),
                                   ACT.Copy).then_inc(xt_h_ready[s], 1)
                if pos == "RT":
                    act.wait_ge(filler_ready[s], ch.written(pos))
                    act.activation(logits_t[s][:, :], ps[0:2 * E, 0:CH], ACT.Copy).then_inc(filler_read[bnk], 1)
                if pos == "R2":
                    act.wait_ge(router_step[s], ch.ffn * R_STEPS + 6)
                    act.activation(e2[s][:, :], gap[s][:, :], ACT.Exp).then_inc(e2_ready[s], 1)
                if pos == "HT":
                    act.wait_ge(filler_ready[s], ch.written(pos))
                    act.activation(hT[s][:, :], ps[:, 0:CH], ACT.Copy).then_inc(filler_read[bnk], 1)
                if pos == "WH":
                    act.wait_ge(filler_read[ch.bank("WR")[0]], ch.bank("WR")[1] + 1)
                    act.activation(hT_h[s][:, :], hT[s][:, :], ACT.Copy).then_inc(hT_h_ready[s], 1)
                if pos == "VK":
                    act.wait_ge(filler_ready[s], ch.written(pos))
                    act.wait_ge(scale_step, 7)
                    if positive(n):
                        act.wait_ge(parts_stored[s], n * (16 * 2 * PARTS))
                    act.activation(z[s][:, 0:CH], ps[:, 0:CH], ACT.Copy, scale=col_scale[:, 0:1])
                    act.activation(z[s][:, CH:2 * CH], ps[:, CH:2 * CH], ACT.Copy,
                                   scale=col_scale[:, 1:2]).then_inc(filler_read[bnk], 1)
                if pos in ("Q0", "Q1"):
                    m0 = 0 if pos == "Q0" else 2
                    act.wait_ge(filler_ready[s], ch.written(pos))
                    for m in range(2):
                        a0 = 512 + (m0 + m) * CH
                        last = act.activation(z[s][:, a0:a0 + CH], ps[:, m * CH:(m + 1) * CH], ACT.Copy,
                                              scale=col_scale[:, 2 + m0 + m:3 + m0 + m])
                    last.then_inc(filler_read[bnk], 1)
                if pos == "VT":
                    act.wait_ge(filler_ready[s], ch.written(pos))
                    act.activation(v_all[:, bass.ds((n * 2 + s) * CT, CT), :],
                                   ps[:, 0:CH].rearrange("p (t n) -> p t n", t=CT), ACT.Copy
                                   ).then_inc(filler_read[bnk], 1)
                if pos == "S0":
                    act.wait_ge(guard_step[s], ch.guard0 + 6)
                    act.activation(parts[s][:, 0, :], zd[s][:, CH:CH + KQ], ACT.Copy).then_inc(part_cast[s], 1)
                if pos == "S2":
                    act.wait_ge(part_rest[s], n * 2 + 1)
                    act.activation(parts[s][:, 1, :], zd[s][:, CH:CH + KQ], ACT.Copy).then_inc(part_cast[s], 1)

            def exp_tile(i, uu, kt, j):
                act.wait_ge(scores_ready, i * (32 * UB) + (32 * uu + 4 * kt + j + 1))
                if j == 0 and (not isinstance(i, int) or 8 * (UB * i + uu) + kt >= 2):
                    act.wait_ge(probs_used, i * (8 * UB) + (8 * uu + kt - 1))
                act.activation(probs[:, kt % 2, j, :], ps_score[j % 2][:, :], ACT.Exp,
                               scale=1.0 / HD ** 0.5).then_inc(probs_ready, 1)

            def copy_out(i, uu):
                act.wait_ge(probs_used, i * (8 * UB) + 8 * (uu + 1))
                if not isinstance(i, int) or UB * i + uu >= 2:
                    act.wait_ge(o_turned, i * UB + (uu - 1))
                act.activation(o_sb[:, uu % 2, :], ps_out[uu % 2][:, :], ACT.Copy).then_inc(o_copied, 1)

            def body(i, plan, first=False):
                for slot in range(8 * UB):
                    uu, kt = slot // 8, slot % 8
                    exp_tile(i, uu, kt, 0)
                    exp_tile(i, uu, kt, 1)
                    if kt == 1 and not (first and uu == 0):
                        copy_out(i, uu - 1)
                    for item in plan.get(2 * slot - 1, []):
                        fill(item)
                    exp_tile(i, uu, kt, 2)
                    exp_tile(i, uu, kt, 3)
                    for item in plan.get(2 * slot, []):
                        fill(item)

            for k, item in enumerate(ALONE):
                fill(item)
                if item[0].n == 0 and item[1] == "FFa0" and item[0].slot == 0:
                    attn_weights()
            body(0, front_plan(0), first=True)
            body(1, front_plan(1))
            with act.Fori(2, 7) as i:
                body(i, back_plan(Chunk("back", 0, i - 2)))
            body(7, back_plan(Chunk("back", 0, 5)))
            copy_out(8, -1)
            for item in tail_steps():
                fill(item)

        @block.vector
        def _(dve):
            def ffn_weights():
                dve.wait_ge(ffn_hi, 4)
                dve.wait_ge(ffn_in, 5 * 16)
                dve.tensor_tensor(wr_hl[:, :, E:2 * E], wr_raw[:, :, :], wr_hl[:, :, 0:E].bitcast(F32),
                                  ALU.subtract).then_inc(ffn_lo, 1)
                dve.tensor_tensor(a_l[:, :, :], raw_a, a_h[:, :, :].bitcast(F32), ALU.subtract).then_inc(ffn_lo, 1)
                dve.tensor_scalar(bias_half[:, :], bias_half[:, :], 0.5, None, ALU.mult).then_inc(ffn_lo, 1)
                dve.tensor_tensor(wb_l[:, :, :], raw_wb, wb_h[:, :, :].bitcast(F32), ALU.subtract).then_inc(ffn_lo, 1)
                dve.tensor_tensor(b_l[:, :], raw_b, b_h[:, :].bitcast(F32), ALU.subtract).then_inc(ffn_lo, 1)

            def attn_scales():
                dve.wait_ge(attn_in, 11 * 16)
                dve.wait_ge(signs_ready, 1)
                dve.scalar_tensor_tensor(out=raw_o, in0=raw_o, scalar=-1.0, in1=raw_o, op0=ALU.mult,
                                         op1=ALU.max).then_inc(abs_ready, 1)
                dve.tensor_reduce(col_scale[:, 0:1], raw_vn, AX, ALU.add,
                                  apply_absolute_value=True).then_inc(scale_step, 1)
                dve.tensor_reduce(col_scale[:, 1:2], raw_kn, AX, ALU.add,
                                  apply_absolute_value=True).then_inc(scale_step, 1)
                dve.tensor_reduce(col_scale[:, 2:2 + DC], raw_qn, AX, ALU.add,
                                  apply_absolute_value=True).then_inc(scale_step, 1)
                dve.wait_ge(scale_step, 3)
                dve.tensor_scalar(col_scale[:, :], col_scale[:, :], 1.0 / D, 1e-8, ALU.mult,
                                  ALU.max).then_inc(scale_step, 1)
                dve.wait_ge(osum_ready, 1)
                dve.tensor_scalar(o_scale[:, :], ps_out[0][:, :], 1.0 / D, 1e-8, ALU.mult,
                                  ALU.max).then_inc(scale_step, 1)
                dve.wait_ge(scale_step, 4)
                dve.tensor_tensor(col_scale[:, :], col_scale[:, :], raw_scale[:, :], ALU.mult).then_inc(scale_step, 1)
                dve.wait_ge(scale_step, 5)
                dve.tensor_tensor(o_scale[:, :], o_scale[:, :], osc_row[:, :], ALU.mult).then_inc(scale_step, 1)

            def router(ch, step):
                s = ch.slot
                base = ch.ffn * R_STEPS
                st = router_step[s]
                if step == "R0":
                    bnk, reads = ch.bank("RU")
                    dve.wait_ge(filler_ready[s], ch.written("RU"))
                    dve.tensor_copy(logit[s][:, :, :], ps_fill[bnk][:, 0:CT * E].rearrange("p (t e) -> p t e", t=CT)
                                    ).then_inc(filler_read[bnk], 1)
                    dve_wait(dve, filler_read[bnk], reads + 1)
                    for t in range(CT):
                        dve.max(top[s][:, t, :], logit[s][:, t, :]).then_inc(st, 1)
                if step == "R1":
                    dve_wait(dve, st, base + 2)
                    for t in range(CT):
                        dve.max_index(top_i[s][:, t, :], top[s][:, t, :], logit[s][:, t, :]).then_inc(st, 1)
                    dve.wait_ge(st, base + 4)
                    dve.tensor_copy(top_e[s][:, :, :], top_i[s][:, :, 0:2]).then_inc(st, 1)
                    dve.tensor_tensor(gap[s][:, :], top[s][:, :, 1], top[s][:, :, 0], ALU.subtract).then_inc(st, 1)
                if step == "R3":
                    dve.wait_ge(e2_ready[s], ch.ffn + 1)
                    dve.tensor_scalar(den[s][:, :], e2[s][:, :], 1.0, None, ALU.add).then_inc(st, 1)
                    dve.wait_ge(st, base + 7)
                    dve.reciprocal(rden[s][:, :], den[s][:, :]).then_inc(st, 1)
                if step == "R4":
                    dve.wait_ge(st, base + 8)
                    dve.tensor_scalar(w12[s][:, :, 0], rden[s][:, :], 2.0, None, ALU.mult).then_inc(st, 1)
                    dve.wait_ge(st, base + 9)
                    dve.tensor_tensor(w12[s][:, :, 1], w12[s][:, :, 0], e2[s][:, :], ALU.mult).then_inc(st, 1)
                if step == "R5":
                    dve.wait_ge(st, base + 10)
                    for t in range(CT):
                        for k in range(2):
                            dve.tensor_scalar(w_tmp[s][:, 2 * t + k, :], expert_of[:, :], top_e[s][:, t, k:k + 1],
                                              w12[s][:, t, k:k + 1], ALU.is_equal, ALU.mult).then_inc(st, 1)
                    dve.wait_ge(st, base + 14)
                    tmp = w_tmp[s][:, :, :].rearrange("p (t k) n -> p t k n", k=2)
                    dve.tensor_tensor(w_rep[s][:, :, :].rearrange("p t (e r) -> p t e r", r=R),
                                      tmp[:, :, 0, :].unsqueeze(3).broadcast_to([P, CT, E, R]),
                                      tmp[:, :, 1, :].unsqueeze(3).broadcast_to([P, CT, E, R]),
                                      ALU.add).then_inc(w_rep_ready[s], 1)

            def guard(ch, step):
                s, k = ch.slot, int(step[1])
                cols = slice(512 * k, 512 * k + 512)
                mask = zneg[s][:, cols].bitcast(I32)
                if step[0] == "C" and ch.on_dve("clamp"):
                    bnk, reads = ch.bank((("VK", "Q0", "Q1") if ch.front else ("Oa", "Ob"))[k])
                    dve.wait_ge(filler_read[bnk], reads + 1)
                    dve.tensor_scalar(zd[s][:, cols], z[s][:, cols], 0.0, BIG, ALU.max, ALU.min).then_inc(clamped[s], 1)
                    dve.tensor_scalar(zneg[s][:, cols], z[s][:, cols], 0.0, -BIG, ALU.min,
                                      ALU.max).then_inc(clamped[s], 1)
                if step[0] == "G" and ch.on_dve("sum"):
                    dve.wait_ge(clamped[s], ch.clamp0 + (2 * k + 2))
                    dve.tensor_tensor(zd[s][:, cols], zd[s][:, cols], zneg[s][:, cols],
                                      ALU.add).then_inc(clamp_sum[s], 1)
                if step[0] == "G":
                    dve.wait_ge(clamp_sum[s], ch.sum0 + (k + 1))
                    dve.tensor_scalar(mask, z[s][:, cols].bitcast(I32), INF_BITS, INF_BITS, ALU.bitwise_and,
                                      ALU.bitwise_xor).then_inc(guard_step[s], 1)
                if step[0] == "P":
                    dve_wait(dve, guard_step[s], ch.guard0 + (2 * k + 1))
                    dve.copy_predicated(zd[s][:, cols], mask, z[s][:, cols]).then_inc(guard_step[s], 1)

            def fill(item):
                ch, pos = item
                s, n = ch.slot, ch.n
                stage, piece, final = stage_of(pos)
                if not final:
                    return
                if stage in ch.uses:
                    bnk, reads = ch.bank(stage)
                    ps = ps_fill[bnk]
                if pos == "LN1a":
                    if ch.front:
                        dve.wait_ge(chunk_loaded[s], ch.load)
                    else:
                        dve.wait_ge(residual[s], n * 2 + 2)
                if pos == "LN2a":
                    dve.wait_ge(filler_read[ch.bank("FFb")[0]], ch.bank("FFb")[1] + 1)
                L = ch.ln(1 if pos.startswith("LN2") else 0)
                if pos in ("LN1a", "LN2a"):
                    dve.bn_stats(stats[s][:, 0, :], xc[s][:, 0, :]).then_inc(stats_ready[s], 1)
                if pos in ("LN1b", "LN2b"):
                    dve.bn_stats(stats[s][:, 1, :], xc[s][:, 1, :]).then_inc(stats_ready[s], 1)
                    dve_wait(dve, stats_ready[s], L * 4 + 2)
                    for t in range(CT):
                        dve.bn_aggr(meanvar[s][:, t, :], stats[s][:, t, :]).then_inc(stats_ready[s], 1)
                if pos == "WR" and ch.on_dve("bias"):
                    dve.wait_ge(xn_ready[s], L * 2 + 2)
                    if n == 0:
                        dve.wait_ge(ffn_lo, 3)
                    for t in range(CT):
                        dve.tensor_tensor(xc[s][:, t, :], xc[s][:, t, :], bias_half[:, :],
                                          ALU.add).then_inc(bias_added[s], 1)
                if pos in ("T0al", "T0bl", "T1al", "T1bl", "T2al", "T2bl"):
                    stage = pos[:3]
                    bnk = ch.bank(stage)[0]
                    t = 0 if stage.endswith("a") else 1
                    dve.wait_ge(xt_h_ready[s], ch.t0 + ch.tn(stage) + 1)
                    dve.tensor_tensor(xt_l[s][:, :, t * P:(t + 1) * P],
                                      ps_fill[bnk][:, :].rearrange("p (c n) -> p c n", c=DC),
                                      xt_h[s][:, :, t * P:(t + 1) * P].bitcast(F32),
                                      ALU.subtract).then_inc(filler_read[bnk], 1)
                if pos[0] == "R" and pos[1] in "0123456789":
                    router(ch, pos)
                if pos[0] in "CGP":
                    guard(ch, pos)
                kq = zd[s][:, CH:CH + KQ]
                if pos == "S1" and ch.on_dve("split"):
                    dve.wait_ge(part_cast[s], n * 2 + 1)
                    dve.tensor_tensor(kq, kq, parts[s][:, 0, :], ALU.subtract).then_inc(part_rest[s], 1)
                if pos == "S3" and ch.on_dve("split"):
                    dve.wait_ge(part_cast[s], n * 2 + 2)
                    dve.wait_ge(part_rest[s], n * 2 + 1)
                    dve.tensor_tensor(parts[s][:, 2, :], kq, parts[s][:, 1, :], ALU.subtract).then_inc(part_rest[s], 1)
                if pos == "ADD" and ch.on_dve("add"):
                    dve.wait_ge(x1_loaded[s], 16)
                    dve.wait_ge(guard_step[s], ch.guard0 + 4)
                    for t in range(CT):
                        dve.tensor_tensor(xc[s][:, t, :], xc[s][:, t, :], zd[s][:, 512 * t:512 * t + 512],
                                          ALU.add).then_inc(residual[s], 1)
                if pos == "WR":
                    dve.wait_ge(filler_ready[s], ch.written(pos))
                    dve.wait_ge(filler_read[ch.bank("HT")[0]], ch.bank("HT")[1] + 1)
                    dve.tensor_tensor(hT[s][:, :], ps[:, 0:CH], hT[s][:, :], ALU.mult).then_inc(filler_read[bnk], 1)
                if pos == "WL":
                    dve.wait_ge(hT_h_ready[s], ch.ffn + 1)
                    dve.tensor_tensor(hT_l[s][:, :], hT[s][:, :], hT_h[s][:, :].bitcast(F32),
                                      ALU.subtract).then_inc(hT_l_ready[s], 1)
                if stage in ("FFa", "FFb"):
                    t = 0 if stage == "FFa" else 1
                    dve.wait_ge(filler_ready[s], ch.written(stage))
                    dve.wait_ge(bias_added[s], ch.ffn * 2 + (t + 1))
                    dve.scalar_tensor_tensor(out=xc[s][:, t, :], in0=ps[:, :], scalar=0.5, in1=xc[s][:, t, :],
                                             op0=ALU.mult, op1=ALU.add).then_inc(filler_read[bnk], 1)
                if stage in ("Oa", "Ob"):
                    t = 0 if stage == "Oa" else 1
                    dve.wait_ge(filler_ready[s], ch.written(stage))
                    dve.tensor_tensor(z[s][:, 512 * t:512 * t + 512], ps[:, :], o_scale[:, :],
                                      ALU.mult).then_inc(filler_read[bnk], 1)

            def reduce_tile(i, uu, pos, t):
                use = max_use(i, uu, pos)
                b = body_bank(pos)
                dve.wait_ge(max_scores, use + 1)
                if t == 0 and (not isinstance(i, int) or UB * i + uu >= 0):
                    dve.wait_ge(neg_max_ready, i * UB + (uu + 1))
                dve.tensor_reduce(neg_max_parts[:, uu % 2, t // 2, t % 2:t % 2 + 1], ps_max[b][:, :], AX, ALU.max,
                                  negate=True).then_inc(max_read, 1)

            def combine(i, uu, use):
                dve.wait_ge(max_read, use + 1)
                if not isinstance(i, int) or UB * i + uu >= 2:
                    dve.wait_ge(shift_parts, i * (4 * UB) + 4 * (uu - 1))
                dve.tensor_tensor(neg_max[:, uu % 2, :], neg_max_parts[:, uu % 2, :, 0], neg_max_parts[:, uu % 2, :, 1],
                                  ALU.min).then_inc(neg_max_ready, 1)

            def copy_rows(i, uu, use, b):
                dve.wait_ge(max_scores, use + 1)
                if not isinstance(i, int) or UB * i + uu >= 2:
                    dve.wait_ge(rows_loaded[(uu - 2) % UB], i * 48 + 48 * ((uu - 2) // UB + 1))
                n = PARTS * REP * QT
                dve.tensor_copy(shift_rows[0:n, uu % 2, :], ps_max[b][0:n, 0:P // 2].bitcast(BF16)
                                ).then_inc(max_read, 1)

            def normalise(i, uu):
                k = uu % 2
                o = ps_out[k][:, :].rearrange("p (q j n) -> p q j n", q=QT, j=REP)
                dve.wait_ge(o_turned, i * UB + (uu + 1))
                dve.reciprocal(recip[:, k, :, :], o[:, :, :, HD]).then_inc(recip_ready, 1)
                dve.wait_ge(recip_ready, i * UB + (uu + 1))
                if isinstance(i, int) and UB * i + uu == NU - 1:
                    for s in range(2):
                        dve.tensor_tensor(xn[s][:, :, (KV - 1) * REP * HD:].rearrange("p q (j d) -> p q j d", j=REP),
                                          o[:, s * CT:(s + 1) * CT, :, 0:HD],
                                          recip[:, k, s * CT:(s + 1) * CT, :].unsqueeze(3).broadcast_to([P, CT, REP, HD]),
                                          ALU.mult).then_inc(att_ready, 1)
                    return
                if not isinstance(i, int) or UB * i + uu >= 2:
                    dve.wait_ge(att_stored[k], i * 32 + 16 * (uu // 2))
                dve.tensor_tensor(att[:, k, :, :].rearrange("p q (j d) -> p q j d", j=REP), o[:, :, :, 0:HD],
                                  recip[:, k, :, :].unsqueeze(3).broadcast_to([P, QT, REP, HD]),
                                  ALU.mult).then_inc(att_ready, 1)

            def body(i, plan, first=False, last=False):
                for slot in range(8 * UB):
                    uu, kt = slot // 8, slot % 8
                    has_max = not (last and uu >= 2)
                    tiles = max_tiles(kt) if has_max else []
                    if kt == 1 and not (last and uu == 3):
                        copy_rows(i, uu + 1, shift_use(i, uu, last), body_bank(SHIFT_POS if has_max else 0))
                    for pos, t in tiles[:2]:
                        reduce_tile(i, uu, pos, t)
                    for item in plan.get(2 * slot - 1, []):
                        fill(item)
                    if kt == 3 and not (first and uu == 0):
                        normalise(i, uu - 1)
                    for pos, t in tiles[2:]:
                        reduce_tile(i, uu, pos, t)
                    for item in plan.get(2 * slot, []):
                        fill(item)
                    if kt == 7 and has_max:
                        combine(i, uu + 2, max_use(i, uu, 32))

            for k, item in enumerate(ALONE):
                for use, v, t in start_uses(k):
                    if t is None:
                        copy_rows(0, 0, use, use % 2)
                    else:
                        dve.wait_ge(max_scores, use + 1)
                        dve.tensor_reduce(neg_max_parts[:, v, t // 2, t % 2:t % 2 + 1], ps_max[use % 2][:, :], AX,
                                          ALU.max, negate=True).then_inc(max_read, 1)
                    if use == 31:
                        combine(0, 0, 31)
                fill(item)
                if item[0].n == 0 and item[0].slot == 1 and item[1] == "LN1c":
                    ffn_weights()
                if item[0].n == 0 and item[0].slot == 1 and item[1] == "FFa3":
                    attn_scales()
            combine(0, 1, 64)
            body(0, front_plan(0), first=True)
            body(1, front_plan(1))
            with dve.Fori(2, 7) as i:
                body(i, back_plan(Chunk("back", 0, i - 2)))
            body(7, back_plan(Chunk("back", 0, 5)), last=True)
            normalise(8, -1)
            for item in tail_steps():
                fill(item)

        @block.tensor
        def _(pe):
            pe.wait_ge(const_ready, 12)

            def sum_o():
                pe.wait_ge(abs_ready, 1)
                for c in range(DC):
                    last = pe.matmul(ps_out[0][:, :], ones[:, :], raw_o[:, c, :], start=(c == 0), stop=(c == DC - 1))
                last.then_inc(osum_ready, 1)

            def fill(item):
                ch, pos = item
                s = ch.slot
                step, (pos, piece, final) = pos, stage_of(pos)
                if pos not in ch.uses:
                    return
                bnk, reads = ch.bank(pos)
                ps = ps_fill[bnk]
                if piece == 0 and positive(reads):
                    pe.wait_ge(filler_read[bnk], reads)

                t = 1 if pos.endswith("b") else 0
                tok = slice(t * P, (t + 1) * P)
                if pos in ("T0a", "T0b", "T1a", "T1b", "T2a", "T2b"):
                    if pos.startswith("T0"):
                        pe.wait_ge(chunk_loaded[s], ch.load)
                        if ch.tail:
                            pe.wait_ge(att_ready, NU + s)
                    else:
                        which = 1 if pos.startswith("T2") else 0
                        pe.wait_ge(xn_ready[s], ch.ln(which) * 2 + (t + 1))
                    for c in range(DC):
                        last = pe.transpose(ps[:, c * P:(c + 1) * P], xn[s][:, t, c * P:(c + 1) * P], ident[:, :])
                if pos == "RT":
                    if ch.alone and ch.front and ch.n == 0:
                        pe.wait_ge(ffn_lo, 2)
                    for c in range(DC):
                        for x_part in (xt_h, xt_l):
                            last = pe.matmul(ps[0:2 * E, 0:CH], wr_hl[:, c, :], x_part[s][:, c, :],
                                             start=(c == 0 and x_part is xt_h), stop=(c == DC - 1 and x_part is xt_l))
                if pos == "HT":
                    pairs = ((a_h, xt_h), (a_h, xt_l), (a_l, xt_h))
                    for c in (2 * piece, 2 * piece + 1):
                        for k, (w, x_part) in enumerate(pairs):
                            last = pe.matmul(ps[:, 0:CH], w[:, c, :], x_part[s][:, c, :],
                                             start=(c == 0 and k == 0), stop=(c == DC - 1 and k == 2))
                if pos == "RU":
                    for u in range(CT):
                        last = pe.matmul(ps[:, u * E:(u + 1) * E], logits_t[s][:, u * P:(u + 1) * P],
                                         hi_plus_lo[:, :], start=True, stop=True)
                if pos == "WR":
                    pe.wait_ge(w_rep_ready[s], ch.ffn + 1)
                    for u in range(CT):
                        last = pe.transpose(ps[:, u * P:(u + 1) * P], w_rep[s][:, u, :], ident[:, :])
                if pos in ("FFa", "FFb"):
                    if ch.alone and ch.front and ch.n == 0 and piece == 0:
                        pe.wait_ge(ffn_lo, 5)
                    c = piece
                    for k, (x_part, w) in enumerate(((xt_h, wb_h), (xt_h, wb_l), (xt_l, wb_h))):
                        pe.matmul(ps[:, :], x_part[s][:, c, tok], w[:, c, :], start=(c == 0 and k == 0), stop=False)
                    if final:
                        pe.wait_ge(hT_l_ready[s], ch.ffn + 1)
                        for k, (h_part, w) in enumerate(((hT_h, b_h), (hT_h, b_l), (hT_l, b_h))):
                            last = pe.matmul(ps[:, :], h_part[s][:, tok], w[:, :], start=False, stop=(k == 2))
                if pos == "VK":
                    if piece == 0 and ch.alone and ch.n == 0:
                        pe.wait_ge(signs_ready, 4)
                    w = (sv, sk)[piece]
                    for c in range(DC):
                        for x_part in (xt_h, xt_l):
                            last = pe.matmul(ps[:, piece * CH:(piece + 1) * CH], w[:, c, :], x_part[s][:, c, :],
                                             start=(c == 0 and x_part is xt_h), stop=(c == DC - 1 and x_part is xt_l))
                if pos in ("Q0", "Q1"):
                    m = int(pos[1]) * 2 + piece
                    for c in range(DC):
                        for x_part in (xt_h, xt_l):
                            last = pe.matmul(ps[:, piece * CH:(piece + 1) * CH], sq[:, c, m * P:(m + 1) * P],
                                             x_part[s][:, c, :], start=(c == 0 and x_part is xt_h),
                                             stop=(c == DC - 1 and x_part is xt_l))
                if pos == "VT":
                    pe.wait_ge(guard_step[s], ch.guard0 + 2)
                    for u in range(CT):
                        last = pe.transpose(ps[:, u * P:(u + 1) * P], zd[s][:, u * P:(u + 1) * P], ident[:, :])
                if pos in ("Oa", "Ob"):
                    for c in (2 * piece, 2 * piece + 1):
                        for x_part in (xt_h, xt_l):
                            last = pe.matmul(ps[:, :], x_part[s][:, c, tok], so[:, c, :],
                                             start=(c == 0 and x_part is xt_h), stop=(c == DC - 1 and x_part is xt_l))
                if final:
                    last.then_inc(filler_ready[s], 1)

            def max_bank_free(use, ring):
                if isinstance(use, int) and START_USES <= use < START_USES + 3:
                    pe.wait_ge(max_read, START_USES)
                elif not isinstance(use, int) or use >= ring:
                    pe.wait_ge(max_read, use - ring + 1)

            def max_matmul(use, bnk, r, t, ring=3):
                j, q, half = t // (2 * QT), t // 2 % QT, t % 2
                max_bank_free(use, ring)
                pe.matmul(ps_max[bnk][:, :], qst[0:SR, r, j, q * P:(q + 1) * P], kst[0:SR, r, half * 512:half * 512 + 512],
                          start=True, stop=True).then_inc(max_scores, 1)

            def shift_transpose(i, uu, use, bnk, ring=3):
                pe.wait_ge(shift_parts, i * (4 * UB) + 4 * (uu + 1))
                max_bank_free(use, ring)
                pe.transpose(ps_max[bnk][:, 0:P // 2].bitcast(BF16), shift[:, uu % 2, :], identb[:, :]
                             ).then_inc(max_scores, 1)

            def score(i, uu, kt, j):
                if not isinstance(i, int) or 32 * (UB * i + uu) + 4 * kt + j >= 2:
                    pe.wait_ge(probs_ready, i * (32 * UB) + (32 * uu + 4 * kt + j - 1))
                pe.matmul(ps_score[j % 2][:, :], kst[0:SR + PARTS, uu, kt * P:(kt + 1) * P],
                          qst[0:SR + PARTS, uu, j, :], start=True, stop=True).then_inc(scores_ready, 1)

            def times_v(i, uu, kt):
                k = uu % 2
                pe.wait_ge(probs_ready, i * (32 * UB) + (32 * uu + 4 * kt + 4))
                if kt == 0:
                    pe.wait_ge(v_ready, i * UB + (uu + 1))
                    if not isinstance(i, int) or UB * i + uu >= 2:
                        pe.wait_ge(att_ready, i * UB + (uu - 1))
                for j in range(REP):
                    last = pe.matmul(ps_out[k][32 * j:32 * j + 32, :], v_ring[:, k, kt, :], probs[:, kt % 2, j, :],
                                     start=(kt == 0), stop=(kt == KT - 1))
                last.then_inc(probs_used, 1)

            def turn_out(i, uu):
                pe.wait_ge(o_copied, i * UB + (uu + 1))
                for q in range(QT):
                    last = pe.transpose(ps_out[uu % 2][:, q * P:(q + 1) * P], o_sb[:, uu % 2, q * P:(q + 1) * P],
                                        ident[:, :])
                last.then_inc(o_turned, 1)

            def body(i, plan, first=False, last=False):
                for slot in range(8 * UB):
                    uu, kt = slot // 8, slot % 8
                    has_max = not (last and uu >= 2)
                    if kt == 0 and has_max:
                        pe.wait_ge(qk_loaded[(uu + 2) % UB], i * 192 + 192 * ((uu + 2) // UB + 1))
                    if kt == 0:
                        pe.wait_ge(rows_loaded[uu], i * 48 + 48)
                    if kt == 1 and not (last and uu == 3):
                        shift_transpose(i, uu + 1, shift_use(i, uu, last), body_bank(SHIFT_POS if has_max else 0))
                    tiles = [(max_use(i, uu, pos), body_bank(pos), (uu + 2) % UB, t) for pos, t in max_tiles(kt)] if has_max else []
                    for j in range(2):
                        score(i, uu, kt, j)
                        if tiles:
                            max_matmul(*tiles[j])
                    if not (first and slot == 0):
                        times_v(i, uu - (kt == 0), (kt - 1) % KT)
                    if kt == 2 and not (first and uu == 0):
                        turn_out(i, uu - 1)
                    score(i, uu, kt, 2)
                    if tiles:
                        max_matmul(*tiles[2])
                    for item in plan.get(2 * slot, []):
                        fill(item)
                    score(i, uu, kt, 3)
                    if tiles:
                        max_matmul(*tiles[3])
                    for item in plan.get(2 * slot + 1, []):
                        fill(item)

            for k, item in enumerate(ALONE):
                for use, v, t in start_uses(k):
                    if t is None:
                        shift_transpose(0, 0, use, use % 2, ring=2)
                    else:
                        if t == 0:
                            pe.wait_ge(qk_loaded[v], 192)
                        max_matmul(use, use % 2, v, t, ring=2)
                fill(item)
                if item[0].n == 0 and item[0].slot == 1 and item[1] == "FFa3":
                    sum_o()
            pe.wait_ge(filler_read[1], ALONE_PAIRS * NF)
            body(0, front_plan(0), first=True)
            body(1, front_plan(1))
            with pe.Fori(2, 7) as i:
                body(i, back_plan(Chunk("back", 0, i - 2)))
            body(7, back_plan(Chunk("back", 0, 5)), last=True)
            times_v(8, -1, KT - 1)
            turn_out(8, -1)
            pe.wait_ge(max_read, max_use(7, 2, 1))
            for item in tail_steps():
                fill(item)


def kernel(**inputs):
    import numpy as np
    from concourse import bacc
    from concourse.bass_utils import run_bass_kernel_spmd

    a = {k.replace("L0_attn_", "").replace("L0_ffn_", ""): np.asarray(v) for k, v in inputs.items()}
    cols = lambda v: np.ascontiguousarray(v.reshape(-1, P).T)
    laid = {
        "x": a["hidden_states"].reshape(T, D),
        "wbT": a["W_base"].T, "b": a["b_base"], "wrT": a["W_router"].T,
        "aT": a["lora_A"].reshape(E * R, D).T,
        "bT": a["lora_B"].transpose(0, 2, 1).reshape(E * R, D),
        "qN": a["q_weight"], "kN": a["k_weight"], "vN": a["v_weight"],
        "qT": a["q_weight"].T, "kT": a["k_weight"].T, "vT": a["v_weight"].T, "oT": a["o_weight"].T,
        "qs": cols(a["q_scale"]), "ks": cols(a["k_scale"]), "vs": cols(a["v_scale"]), "osc": a["o_scale"],
    }
    nc = bacc.Bacc("TRN2", target_bir_lowering=False, num_devices=1)
    arrays, args = {}, []
    for name, v in laid.items():
        arrays[name] = np.ascontiguousarray(v)
        args.append(nc.dram_tensor(name, v.shape, mybir.dt.from_np(v.dtype), kind="ExternalInput").ap())
    args.append(nc.dram_tensor("out", (T, D), F32, kind="ExternalOutput").ap())
    macaron(nc, *args)
    r = run_bass_kernel_spmd(nc, [arrays], core_ids=[0])
    return r.results[0]["out"].reshape(B, S, D)
```
